# Optimizing a Trainium2 kernel written in Bass

```python
import numpy as np
import jax
import jax.numpy as jnp

def _softmax(x, axis=-1):
    return jax.nn.softmax(x, axis=axis)

def _gelu(x):
    return jax.nn.gelu(x, approximate=True)

def _silu(x):
    return jax.nn.silu(x)

def _sigmoid(x):
    return jax.nn.sigmoid(x)

def _layernorm(x, axis=-1, eps=1e-05):
    m = jnp.mean(x, axis=axis, keepdims=True)
    v = jnp.var(x, axis=axis, keepdims=True)
    return (x - m) / jnp.sqrt(v + eps)

def _scatter_add(tgt, idx, src, axis=0):
    return tgt.at[idx].add(src)

def _segment_sum(src, seg, n):
    return jax.ops.segment_sum(src, seg, n)
kernel_name = 'mk_xattn_ffn_d2_seqx_r4_2d2a1c'

def setup_inputs(seed: int=0):
    np.random.seed(seed)
    _w = jnp.asarray

    def _rec_inputs():
        import jax
        import jax.numpy as jnp
        _rk = jax.random.key(seed)
        x = -0.0005207 + 1.001 * jax.random.normal(jax.random.fold_in(_rk, 1), (8, 256, 256), jnp.float32)
        _lenS = 256 - jax.random.randint(jax.random.fold_in(_rk, 7), (8,), 0, max(1, 256 // 4) + 1, jnp.int32)
        _lenS2 = 256 - jax.random.randint(jax.random.fold_in(_rk, 8), (8,), 0, max(1, 256 // 4) + 1, jnp.int32)
        _ctx_1024P = jax.random.normal(jax.random.fold_in(_rk, 11), (8, 16, 256), jnp.float32)
        _ctx_1024c = jax.random.dirichlet(jax.random.fold_in(_rk, 511), 0.3 * jnp.ones((16,), jnp.float32), (8, 256))
        _ctx_1024t = jnp.einsum('bsk,bkd->bsd', _ctx_1024c, _ctx_1024P)
        _ctx_1024t = _ctx_1024t * jax.lax.rsqrt(jnp.mean(jnp.square(_ctx_1024t)) + 1e-12) * 0.953939
        ctx_1024 = -0.000514642 + 1.00011 * (_ctx_1024t + 0.3 * jax.random.normal(jax.random.fold_in(_rk, 611), (8, 256, 256), jnp.float32))
        return (x, ctx_1024)
    x, ctx_1024 = _rec_inputs()

    def _L0_xattn_setup():
        import jax, jax.numpy as jnp
        import numpy as np
        B, S, E, NH = (1, 512, 256, 8)
        DH = E // NH
        EPS_BACKEND = 1e-06
        EPS_NORM = 1e-05
        key = jax.random.key(seed)
        ks = jax.random.split(key, 8)
        q = jax.random.normal(ks[0], (B, S, E), jnp.float32)
        k = jax.random.normal(ks[1], (B, S, E), jnp.float32)
        v = jax.random.normal(ks[2], (B, S, E), jnp.float32)
        igate_w = jax.random.normal(ks[3], (NH, 3 * E), jnp.float32) * 0.02
        igate_b = jax.random.normal(ks[4], (NH,), jnp.float32) * 0.1
        fgate_w = jax.random.normal(ks[5], (NH, 3 * E), jnp.float32) * 0.02
        fgate_b = jnp.linspace(3.0, 6.0, NH).astype(jnp.float32)
        norm_w = 1.0 + 0.1 * jax.random.normal(ks[6], (E,), jnp.float32)
        return dict(q=q, k=k, v=v, igate_w=igate_w, igate_b=igate_b, fgate_w=fgate_w, fgate_b=fgate_b, norm_w=norm_w)
    _L0_xattn_all = _L0_xattn_setup()
    _L0_xattn_in = {k: v for k, v in _L0_xattn_all.items() if k in ('igate_w', 'igate_b', 'fgate_w', 'fgate_b', 'norm_w')}
    del _L0_xattn_all

    def _L0_ffn_setup():
        import jax, jax.numpy as jnp
        import numpy as np
        TOP_K = 4
        CAP_FACTOR = 4

        def swiglu(x, w1, w2, w3):
            return jax.nn.silu(x @ w1) * (x @ w3) @ w2
        key = jax.random.key(seed)
        ks = jax.random.split(key, 8)
        B, S, D, H, E = (2, 512, 256, 128, 32)
        Hs = 2 * H
        sd = lambda *sh: 1.0 / np.sqrt(sh[-2])
        x = jax.random.normal(ks[0], (B, S, D), dtype=jnp.float32)
        Wg = jax.random.normal(ks[1], (D, E), dtype=jnp.float32) * (1.0 / np.sqrt(D))
        W1 = jax.random.normal(ks[2], (E, D, H), dtype=jnp.float32) * (1.0 / np.sqrt(D))
        W3 = jax.random.normal(ks[3], (E, D, H), dtype=jnp.float32) * (1.0 / np.sqrt(D))
        W2 = jax.random.normal(ks[4], (E, H, D), dtype=jnp.float32) * (1.0 / np.sqrt(H))
        Ws1 = jax.random.normal(ks[5], (D, Hs), dtype=jnp.float32) * (1.0 / np.sqrt(D))
        Ws3 = jax.random.normal(ks[6], (D, Hs), dtype=jnp.float32) * (1.0 / np.sqrt(D))
        Ws2 = jax.random.normal(ks[7], (Hs, D), dtype=jnp.float32) * (1.0 / np.sqrt(Hs))
        return {'x': x, 'Wg': Wg, 'W1': W1, 'W2': W2, 'W3': W3, 'Ws1': Ws1, 'Ws2': Ws2, 'Ws3': Ws3}
    _L0_ffn_all = _L0_ffn_setup()
    _L0_ffn_in = {k: v for k, v in _L0_ffn_all.items() if k in ('Wg', 'W1', 'W2', 'W3', 'Ws1', 'Ws2', 'Ws3')}
    del _L0_ffn_all

    def _L1_xattn_setup():
        import jax, jax.numpy as jnp
        import numpy as np
        L_IN, L_OUT = (512, 256)
        D_IN, D_OUT, D_POS = (256, 256, 64)
        B = 4
        EPS = 1e-05

        def _layernorm(x, g, b):
            m = jnp.mean(x, axis=-1, keepdims=True)
            v = jnp.mean(jnp.square(x - m), axis=-1, keepdims=True)
            return (x - m) * jax.lax.rsqrt(v + EPS) * g + b

        def _ffn(x, g, be, W1, b1, W2, b2):
            y = _layernorm(x, g, be)
            y = jax.nn.silu(y @ W1 + b1)
            y = y @ W2 + b2
            return y + x
        key = jax.random.key(seed)
        ks = jax.random.split(key, 24)
        s = lambda k, shp, sc=0.02: jax.random.normal(k, shp, dtype=jnp.float32) * sc
        d = {'z': jax.random.normal(ks[0], (B, L_IN, D_IN), dtype=jnp.float32), 'x': jax.random.normal(ks[1], (B, L_OUT, D_OUT), dtype=jnp.float32), 'pe': jax.random.normal(ks[2], (L_IN, D_POS), dtype=jnp.float32), 'W_in': s(ks[3], (D_IN, D_OUT)), 'b_in': jnp.zeros((D_OUT,), jnp.float32), 'g_ln': jnp.ones((D_OUT,), jnp.float32), 'beta_ln': jnp.zeros((D_OUT,), jnp.float32), 'Wp1': s(ks[4], (D_POS, D_POS + D_OUT)), 'bp1': jnp.zeros((D_POS + D_OUT,), jnp.float32), 'Wp2': s(ks[5], (D_POS + D_OUT, D_OUT)), 'bp2': jnp.zeros((D_OUT,), jnp.float32), 'a': jax.random.normal(ks[6], (1,), dtype=jnp.float32), 'g1': jnp.ones((D_OUT,), jnp.float32), 'be1': jnp.zeros((D_OUT,), jnp.float32), 'W1a': s(ks[7], (D_OUT, 2 * D_OUT)), 'b1a': jnp.zeros((2 * D_OUT,), jnp.float32), 'W1b': s(ks[8], (2 * D_OUT, D_OUT)), 'b1b': jnp.zeros((D_OUT,), jnp.float32), 'g2': jnp.ones((D_OUT,), jnp.float32), 'be2': jnp.zeros((D_OUT,), jnp.float32), 'W2a': s(ks[9], (D_OUT, 2 * D_OUT)), 'b2a': jnp.zeros((2 * D_OUT,), jnp.float32), 'W2b': s(ks[10], (2 * D_OUT, D_OUT)), 'b2b': jnp.zeros((D_OUT,), jnp.float32)}
        return d
    _L1_xattn_all = _L1_xattn_setup()
    _L1_xattn_in = {k: v for k, v in _L1_xattn_all.items() if k in ('pe', 'W_in', 'b_in', 'g_ln', 'beta_ln', 'Wp1', 'bp1', 'Wp2', 'bp2', 'a', 'g1', 'be1', 'W1a', 'b1a', 'W1b', 'b1b', 'g2', 'be2', 'W2a', 'b2a', 'W2b', 'b2b')}
    del _L1_xattn_all

    def _L1_ffn_setup():
        import jax, jax.numpy as jnp
        import numpy as np
        B, S, H = (2, 256, 256)
        E, F = (8, 1024)
        GATE_TEMP = 0.1
        key = jax.random.key(seed)
        ks = jax.random.split(key, 6)
        s_h = 1.0 / np.sqrt(H)
        s_f = 1.0 / np.sqrt(F)
        return {'hidden_states': jax.random.normal(ks[0], (B, S, H), dtype=jnp.float32), 'w_router': jax.random.normal(ks[1], (H, E), dtype=jnp.float32) * s_h, 'w_gating': jax.random.normal(ks[2], (H, E), dtype=jnp.float32) * s_h, 'w_gate': jax.random.normal(ks[3], (E, H, F), dtype=jnp.float32) * s_h, 'w_up': jax.random.normal(ks[4], (E, H, F), dtype=jnp.float32) * s_h, 'w_down': jax.random.normal(ks[5], (E, F, H), dtype=jnp.float32) * s_f}
    _L1_ffn_all = _L1_ffn_setup()
    _L1_ffn_in = {k: v for k, v in _L1_ffn_all.items() if k in ('w_router', 'w_gating', 'w_gate', 'w_up', 'w_down')}
    del _L1_ffn_all
    return {'x': x, 'ctx_1024': ctx_1024, 'L0_xattn_igate_w': _L0_xattn_in['igate_w'], 'L0_xattn_igate_b': _L0_xattn_in['igate_b'], 'L0_xattn_fgate_w': _L0_xattn_in['fgate_w'], 'L0_xattn_fgate_b': _L0_xattn_in['fgate_b'], 'L0_xattn_norm_w': _L0_xattn_in['norm_w'], 'L0_ffn_Wg': _L0_ffn_in['Wg'], 'L0_ffn_W1': _L0_ffn_in['W1'], 'L0_ffn_W2': _L0_ffn_in['W2'], 'L0_ffn_W3': _L0_ffn_in['W3'], 'L0_ffn_Ws1': _L0_ffn_in['Ws1'], 'L0_ffn_Ws2': _L0_ffn_in['Ws2'], 'L0_ffn_Ws3': _L0_ffn_in['Ws3'], 'L1_xattn_pe': _L1_xattn_in['pe'], 'L1_xattn_W_in': _L1_xattn_in['W_in'], 'L1_xattn_b_in': _L1_xattn_in['b_in'], 'L1_xattn_g_ln': _L1_xattn_in['g_ln'], 'L1_xattn_beta_ln': _L1_xattn_in['beta_ln'], 'L1_xattn_Wp1': _L1_xattn_in['Wp1'], 'L1_xattn_bp1': _L1_xattn_in['bp1'], 'L1_xattn_Wp2': _L1_xattn_in['Wp2'], 'L1_xattn_bp2': _L1_xattn_in['bp2'], 'L1_xattn_a': _L1_xattn_in['a'], 'L1_xattn_g1': _L1_xattn_in['g1'], 'L1_xattn_be1': _L1_xattn_in['be1'], 'L1_xattn_W1a': _L1_xattn_in['W1a'], 'L1_xattn_b1a': _L1_xattn_in['b1a'], 'L1_xattn_W1b': _L1_xattn_in['W1b'], 'L1_xattn_b1b': _L1_xattn_in['b1b'], 'L1_xattn_g2': _L1_xattn_in['g2'], 'L1_xattn_be2': _L1_xattn_in['be2'], 'L1_xattn_W2a': _L1_xattn_in['W2a'], 'L1_xattn_b2a': _L1_xattn_in['b2a'], 'L1_xattn_W2b': _L1_xattn_in['W2b'], 'L1_xattn_b2b': _L1_xattn_in['b2b'], 'L1_ffn_w_router': _L1_ffn_in['w_router'], 'L1_ffn_w_gating': _L1_ffn_in['w_gating'], 'L1_ffn_w_gate': _L1_ffn_in['w_gate'], 'L1_ffn_w_up': _L1_ffn_in['w_up'], 'L1_ffn_w_down': _L1_ffn_in['w_down']}

def reference(x, ctx_1024, L0_xattn_igate_w, L0_xattn_igate_b, L0_xattn_fgate_w, L0_xattn_fgate_b, L0_xattn_norm_w, L0_ffn_Wg, L0_ffn_W1, L0_ffn_W2, L0_ffn_W3, L0_ffn_Ws1, L0_ffn_Ws2, L0_ffn_Ws3, L1_xattn_pe, L1_xattn_W_in, L1_xattn_b_in, L1_xattn_g_ln, L1_xattn_beta_ln, L1_xattn_Wp1, L1_xattn_bp1, L1_xattn_Wp2, L1_xattn_bp2, L1_xattn_a, L1_xattn_g1, L1_xattn_be1, L1_xattn_W1a, L1_xattn_b1a, L1_xattn_W1b, L1_xattn_b1b, L1_xattn_g2, L1_xattn_be2, L1_xattn_W2a, L1_xattn_b2a, L1_xattn_W2b, L1_xattn_b2b, L1_ffn_w_router, L1_ffn_w_gating, L1_ffn_w_gate, L1_ffn_w_up, L1_ffn_w_down):
    import jax
    import jax.numpy as jnp

    def _L0_xattn_ref(q, k, v, igate_w, igate_b, fgate_w, fgate_b, norm_w):
        import jax, jax.numpy as jnp
        import numpy as np
        B, S, E, NH = (1, 512, 256, 8)
        DH = E // NH
        EPS_BACKEND = 1e-06
        EPS_NORM = 1e-05
        Bq, Sq, Eq = q.shape
        nh = igate_w.shape[0]
        dh = Eq // nh
        gate_in = jnp.concatenate([q, k, v], axis=-1)
        ig = jnp.transpose(gate_in @ igate_w.T + igate_b, (0, 2, 1))
        fg = jnp.transpose(gate_in @ fgate_w.T + fgate_b, (0, 2, 1))
        qh = q.reshape(Bq, Sq, nh, dh).transpose(0, 2, 1, 3)
        kh = k.reshape(Bq, Sq, nh, dh).transpose(0, 2, 1, 3)
        vh = v.reshape(Bq, Sq, nh, dh).transpose(0, 2, 1, 3)
        log_f_cum = jnp.cumsum(jax.nn.log_sigmoid(fg), axis=-1)
        log_fg_mat = log_f_cum[:, :, :, None] - log_f_cum[:, :, None, :]
        ltr = jnp.tril(jnp.ones((Sq, Sq), dtype=bool))
        log_D = jnp.where(ltr, log_fg_mat + ig[:, :, None, :], -jnp.inf)
        max_log_D = jnp.max(log_D, axis=-1, keepdims=True)
        D = jnp.exp(log_D - max_log_D)
        qk = jnp.einsum('bhsd,bhtd->bhst', qh, kh) / jnp.sqrt(jnp.float32(dh))
        C = qk * D
        normalizer = jnp.maximum(jnp.abs(jnp.sum(C, axis=-1, keepdims=True)), jnp.exp(-max_log_D))
        h = jnp.einsum('bhst,bhtd->bhsd', C / (normalizer + EPS_BACKEND), vh)
        mean = jnp.mean(h, axis=-1, keepdims=True)
        var = jnp.var(h, axis=-1, keepdims=True)
        h_norm = (h - mean) / jnp.sqrt(var + EPS_NORM)
        h_norm = h_norm * norm_w.reshape(nh, dh)[None, :, None, :]
        return h_norm.transpose(0, 2, 1, 3).reshape(Bq, Sq, Eq)

    def _L0_ffn_ref(x, Wg, W1, W2, W3, Ws1, Ws2, Ws3):
        import jax, jax.numpy as jnp
        import numpy as np
        TOP_K = 4
        CAP_FACTOR = 4

        def swiglu(x, w1, w2, w3):
            return jax.nn.silu(x @ w1) * (x @ w3) @ w2
        B, S, D = x.shape
        E = Wg.shape[1]
        T = B * S
        xf = x.reshape(T, D)
        scores = jax.nn.softmax(xf @ Wg, axis=-1)
        weights, indices = jax.lax.top_k(scores, TOP_K)
        P = T * TOP_K
        pair_expert = indices.reshape(-1)
        pair_token = jnp.repeat(jnp.arange(T), TOP_K)
        pair_weight = weights.reshape(-1).astype(xf.dtype)
        C = CAP_FACTOR * P // E
        y = jnp.zeros_like(xf)
        for e in range(E):
            pos = jnp.nonzero(pair_expert == e, size=C, fill_value=P)[0]
            valid = pos < P
            safe = jnp.minimum(pos, P - 1)
            tok = jnp.where(valid, pair_token[safe], 0)
            w = jnp.where(valid, pair_weight[safe], 0.0)
            xg = xf[tok]
            out = swiglu(xg, W1[e], W2[e], W3[e]) * w[:, None]
            y = y.at[tok].add(out)
        z = swiglu(xf, Ws1, Ws2, Ws3)
        return (y + z).reshape(B, S, D)

    def _L1_xattn_ref(z, x, pe, W_in, b_in, g_ln, beta_ln, Wp1, bp1, Wp2, bp2, a, g1, be1, W1a, b1a, W1b, b1b, g2, be2, W2a, b2a, W2b, b2b):
        import jax, jax.numpy as jnp
        import numpy as np
        L_IN, L_OUT = (512, 256)
        D_IN, D_OUT, D_POS = (256, 256, 64)
        B = 4
        EPS = 1e-05

        def _layernorm(x, g, b):
            m = jnp.mean(x, axis=-1, keepdims=True)
            v = jnp.mean(jnp.square(x - m), axis=-1, keepdims=True)
            return (x - m) * jax.lax.rsqrt(v + EPS) * g + b

        def _ffn(x, g, be, W1, b1, W2, b2):
            y = _layernorm(x, g, be)
            y = jax.nn.silu(y @ W1 + b1)
            y = y @ W2 + b2
            return y + x
        L = L_IN
        z = z @ W_in + b_in
        zn = _layernorm(z, g_ln, beta_ln)
        fz = jnp.fft.rfft(zn, n=2 * L, axis=1)
        h = jax.nn.silu(pe @ Wp1 + bp1) @ Wp2 + bp2
        window = jnp.exp(-jnp.arange(L, dtype=jnp.float32) * jnp.exp(a[0]))
        wfh = jnp.fft.rfft(window[:, None] * h, n=2 * L, axis=0)
        cwhz = jnp.fft.irfft(wfh[None] * fz, n=2 * L, axis=1)[:, :L]
        idx = jnp.arange(L_OUT) * L // L_OUT
        dcwhz = cwhz[:, idx]
        xr = _ffn(x, g1, be1, W1a, b1a, W1b, b1b)
        y = xr * dcwhz
        y = _ffn(y, g2, be2, W2a, b2a, W2b, b2b)
        return y

    def _L1_ffn_ref(hidden_states, w_router, w_gating, w_gate, w_up, w_down):
        import jax, jax.numpy as jnp
        import numpy as np
        B, S, H = (2, 256, 256)
        E, F = (8, 1024)
        GATE_TEMP = 0.1
        x = hidden_states
        router_probs = jax.nn.softmax(jnp.einsum('bsh,he->bse', x, w_router), axis=-1)
        gate_weights = jax.nn.softmax(jnp.einsum('bsh,he->bse', x, w_gating) / GATE_TEMP, axis=-1)
        g = jnp.einsum('bsh,ehf->ebsf', x, w_gate)
        u = jnp.einsum('bsh,ehf->ebsf', x, w_up)
        h = jax.nn.silu(g) * u
        expert_out = jnp.einsum('ebsf,efh->ebsh', h, w_down)
        cw = router_probs * gate_weights
        cw = cw / (jnp.sum(cw, axis=-1, keepdims=True) + 1e-09)
        out = jnp.einsum('ebsh,bse->bsh', expert_out, cw)
        return out
    x = x + _L0_xattn_ref(_layernorm(x, axis=-1), ctx_1024, ctx_1024, L0_xattn_igate_w, L0_xattn_igate_b, L0_xattn_fgate_w, L0_xattn_fgate_b, L0_xattn_norm_w)
    x = x + _L0_ffn_ref(_layernorm(x, axis=-1), L0_ffn_Wg, L0_ffn_W1, L0_ffn_W2, L0_ffn_W3, L0_ffn_Ws1, L0_ffn_Ws2, L0_ffn_Ws3)
    x = x + _L1_xattn_ref(ctx_1024, _layernorm(x, axis=-1), L1_xattn_pe, L1_xattn_W_in, L1_xattn_b_in, L1_xattn_g_ln, L1_xattn_beta_ln, L1_xattn_Wp1, L1_xattn_bp1, L1_xattn_Wp2, L1_xattn_bp2, L1_xattn_a, L1_xattn_g1, L1_xattn_be1, L1_xattn_W1a, L1_xattn_b1a, L1_xattn_W1b, L1_xattn_b1b, L1_xattn_g2, L1_xattn_be2, L1_xattn_W2a, L1_xattn_b2a, L1_xattn_W2b, L1_xattn_b2b)
    x = x + _L1_ffn_ref(_layernorm(x, axis=-1), L1_ffn_w_router, L1_ffn_w_gating, L1_ffn_w_gate, L1_ffn_w_up, L1_ffn_w_down)
    return x

_drawn_inputs = setup_inputs


def setup_inputs(seed=0):
    import zlib

    import numpy as np

    out = dict(_drawn_inputs(seed))
    spreads = {'L1_xattn_b_in': (0.0, 0.444),
     'L1_xattn_g_ln': (1.0, 0.6),
     'L1_xattn_beta_ln': (0.0, 0.8),
     'L1_xattn_bp1': (0.0, 0.669),
     'L1_xattn_bp2': (0.0, 0.1),
     'L1_xattn_g1': (1.0, 0.6),
     'L1_xattn_be1': (0.0, 0.8),
     'L1_xattn_b1a': (0.0, 0.8),
     'L1_xattn_b1b': (0.0, 0.8),
     'L1_xattn_g2': (1.0, 0.6),
     'L1_xattn_be2': (0.0, 2.0),
     'L1_xattn_b2a': (0.0, 2.0),
     'L1_xattn_b2b': (0.0, 0.8)}
    factors = {'L0_xattn_igate_b': 64.0,
     'L1_xattn_pe': 3.294,
     'L1_xattn_Wp1': 3.449,
     'L1_xattn_Wp2': 3.124,
     'L1_xattn_W1a': 8.0,
     'L1_xattn_W1b': 8.0,
     'L0_xattn_fgate_w': 2.764,
     'L1_xattn_W2a': 7.72,
     'L1_xattn_W2b': 5.532,
     'L1_ffn_w_router': 8.0}
    for name, (base, spread) in spreads.items():
        noise = np.random.default_rng([zlib.crc32(name.encode()), seed]).standard_normal(out[name].shape)
        drawn = base * np.exp(spread * noise) if base else spread * noise
        out[name] = jnp.asarray(drawn.astype(out[name].dtype))
    for name, factor in factors.items():
        out[name] = (out[name] * factor).astype(out[name].dtype)
    return out
```

```python
import concourse.bass as bass
from concourse import mybir
from contextlib import ExitStack

F32 = mybir.dt.float32
F32R = mybir.dt.float32r
BF16 = mybir.dt.bfloat16
U32 = mybir.dt.uint32
ALU = mybir.AluOpType
ACT = mybir.ActivationFunctionType
AXX = mybir.AxisListType.X

P = 128
B, SEQ, D = 8, 256, 256
NT = B * SEQ // P
NH, DH = 8, 32
E0, TOPK = 32, 4
CAP = 4 * (B * SEQ * TOPK) // E0
E1 = 8
FT = 96
BLK = 512
UW = 3 * BLK
EPS = 1e-5
ARENA = 210000 // 64 * 64

U_SHARED, U_L0, U_FA, U_FB, U_L1 = 0, 1, 17, 19, 21
N_L0, N_L1 = 16, 32
PLAIN = 32
M_L0 = 4
M_FA = M_L0 + 8 * N_L0
M_FB = M_FA + 8
M_L1 = M_FB + 8


def build(nc, dram, out_d):
    ctx = ExitStack()
    with ctx:
        base = (nc.sbuf_base + 63) // 64 * 64
        ctx.enter_context(nc.sbuf_tensor("arena", [P, ARENA], mybir.dt.uint8))
        top = [base]
        start, end = {}, {}

        def at(name, shape, dt=F32, off=None):
            n = 2 if dt == BF16 else 4
            for s in shape[1:]:
                n *= s
            n = (n + 63) // 64 * 64
            if off is None:
                off = top[0]
                top[0] += n
            start[name], end[name] = off, off + n
            return nc.alloc_sbuf_tensor_at(name, shape, dt, offset=off)

        x = at("x", [P, NT, D])
        dcw = at("dcw", [P, NT, D])
        ya = at("ya", [P, NT, D])
        xn = at("xn", [P, NT, D])
        xTH = at("xTH", [P, 2, NT * P], F32R)
        xTL = at("xTL", [P, 2, NT * P], F32R)
        wS = at("wS", [P, 2, UW])
        wH = at("wH", [P, 2, UW], F32R)
        wL = at("wL", [P, 2, UW], F32R)
        sg = at("sg", [P, 2, 512])
        hF = at("hF", [P, 2, 512])
        hH = at("hH", [P, 2, 512], F32R)
        hL = at("hL", [P, 2, 512], F32R)
        tF = at("tF", [P, 2, 512])
        ident = at("ident", [P, P])
        bcv = at("bcv", [P, 7, D])
        cols = at("cols", [P, 19])
        sc0 = at("sc0", [P, NT, E0])
        sc1 = at("sc1", [P, NT, E0])
        sc2 = at("sc2", [P, NT, E0])
        cw0 = at("cw0", [P, NT, E0])
        selm = at("selm", [P, NT, E0], BF16)
        cw2 = at("cw2", [P, NT, 16])
        st = at("st", [P, NT, 6])
        mv = at("mv", [P, NT, 2])
        ve = at("ve", [P, NT])
        sd = at("sd", [P, NT])
        rs = at("rs", [P, NT])
        nt1 = at("nt1", [P, NT])
        sm = at("sm", [P, NT, 2])
        sm2 = at("sm2", [P, NT])
        mx8 = at("mx8", [P, NT, 8])
        ix8 = at("ix8", [P, NT, 8], U32)
        ixf = at("ixf", [P, NT, 8])
        iot = at("iot", [P, E0])
        tri = at("tri", [P, 2, P], BF16)
        wg0 = at("wg0", [P, 2, E0])
        wg0H = at("wg0H", [P, 2, E0], F32R)
        wg0L = at("wg0L", [P, 2, E0], F32R)
        wg1 = at("wg1", [P, 2, 16])
        wg1H = at("wg1H", [P, 2, 16], F32R)
        wg1L = at("wg1L", [P, 2, 16], F32R)
        vext = at("vext", [P, NT, NH, DH + 1])
        maskT = at("maskT", [P, 384], BF16)
        idb = at("idb", [P, P], BF16)
        gwt = at("gwt", [P, 6, 16])
        gbias = at("gbias", [P, 1])
        aT = at("aT", [P, 2, 64])
        eE = at("eE", [P, 2, 64])
        den = at("den", [P, 2, NH])
        mean = at("mean", [P, 2, 2, NH])
        var = at("var", [P, 2, NH])
        rstd = at("rstd", [P, 2, 2, NH])
        alog = at("alog", [P, 1])
        ea = at("ea", [P, 1])
        nl = at("nl", [P, 4])
        wnd = at("wnd", [P, 4])
        assert top[0] - base <= ARENA, top[0] - base
        sel = at("sel", [P, 64, P], F32R, start["dcw"])
        qT = at("qT", [P, 2, NT * P], F32, start["xTH"])
        kT = at("kT", [P, 2, NT * P], F32, start["xTL"])
        gateW = at("gateW", [P, 4, B, P], F32, start["wH"])
        cx = at("cx", [P, NT, D], F32, end["gateW"])
        Dm = at("Dm", [P, 2, 384], F32, end["cx"])
        Cm = at("Cm", [P, 2, 384], F32, end["Dm"])
        rg = at("rg", [P, 256], F32, start["sc0"])
        r1 = at("r1", [P, 256], F32, end["rg"])
        r2 = at("r2", [P, 256], F32, end["r1"])
        r3 = at("r3", [P, 256], F32, end["r2"])
        rF = at("rF", [P, 256], F32, end["r3"])
        rM = at("rM", [P, 256], F32, end["rF"])
        AE = at("AE", [P, 256], F32, end["rM"])
        ones = at("ones", [P, 256], F32, end["AE"])
        MHL = at("MHL", [P, 256], F32R, end["ones"])
        id2 = at("id2", [P, 64], F32, end["MHL"])
        hN = at("hN", [P, 2, 512], F32, start["xn"])
        hC = at("hC", [P, 2, 512], F32, end["hN"])
        hQ = at("hQ", [P, 2, 512], F32, end["hC"])
        hR = at("hR", [P, 2, 512], F32, end["hQ"])
        zn = at("zn", [P, B, 2, D], F32, start["xTH"])
        Zs = at("Zs", [P, 2, 4, 512], F32, start["xn"])
        FZ = at("FZ", [P, 4, FT], F32, start["wH"])
        FW = at("FW", [P, 4, 4, FT], F32, end["FZ"])
        GI = at("GI", [P, 4, D], F32, end["FW"])
        Win = at("Win", [P, 2, D], F32, end["GI"])
        peT = at("peT", [64, 512], F32, end["Win"])
        Wp1 = at("Wp1", [64, 320], F32, end["peT"])
        Wp2 = at("Wp2", [P, 3, D], F32, end["Wp1"])
        h1T = at("h1T", [P, 3, 512], F32, end["Wp2"])
        wf = at("wf", [P, 4, D], F32, end["h1T"])
        WF = at("WF", [P, 2, 4, D], F32, start["sc0"])
        PR = at("PR", [P, 2, 512], F32, start["vext"])
        PI = at("PI", [P, 2, 512], F32, end["PR"])
        tv = at("tv", [P, 2, 512], F32, end["PI"])
        tp = at("tp", [P, 2, 512], F32, end["tv"])
        assert end["Cm"] <= end["tF"] and end["wf"] <= start["Dm"] and end["id2"] <= end["cw2"]
        assert end["hR"] <= end["xn"] and end["WF"] <= end["cw2"] and end["tp"] <= end["vext"]

        ps = ctx.enter_context(nc.psum_tensor("ps", [P, 8, 512], F32))

        def sem(name):
            return ctx.enter_context(nc.semaphore(name))

        x_loaded = sem("x_loaded")
        ctx_loaded = sem("ctx_loaded")
        const_loaded = sem("const_loaded")
        conv_loaded = sem("conv_loaded")
        stage_loaded = [sem("stage0_loaded"), sem("stage1_loaded")]
        out_stored = sem("out_stored")
        var_done = sem("var_done")
        std_done = sem("std_done")
        norm_done = sem("norm_done")
        dve_step = sem("dve_step")
        pool_step = sem("pool_step")
        act_step = sem("act_step")
        gatew_done = sem("gatew_done")
        sel_done = sem("sel_done")
        vext_done = sem("vext_done")
        mixT_done = sem("mixT_done")
        mixT_copied = sem("mixT_copied")
        gates_done = sem("gates_done")
        gates_copied = sem("gates_copied")
        negabs_done = sem("negabs_done")
        softplus_done = sem("softplus_done")
        logf_done = sem("logf_done")
        logf_moved = sem("logf_moved")
        rows_done = sem("rows_done")
        rowsT_done = sem("rowsT_done")
        rowsT_copied = sem("rowsT_copied")
        qk_done = sem("qk_done")
        arg_done = sem("arg_done")
        decay_done = sem("decay_done")
        mixed_done = sem("mixed_done")
        pv_done = sem("pv_done")
        head_scaled = sem("head_scaled")
        head_centred = sem("head_centred")
        head_squared = sem("head_squared")
        head_var = sem("head_var")
        head_rstd = sem("head_rstd")
        head_added = sem("head_added")
        pos1_done = sem("pos1_done")
        pos1_silu = sem("pos1_silu")
        window_done = sem("window_done")
        pos2_done = sem("pos2_done")
        filt_done = sem("filt_done")
        filtF_done = sem("filtF_done")
        filtF_copied = sem("filtF_copied")
        zlin_done = sem("zlin_done")
        zlin_copied = sem("zlin_copied")
        zaff_dve = sem("zaff_dve")
        zF_done = sem("zF_done")
        zF_copied = sem("zF_copied")
        prod_re = sem("prod_re")
        prod_im = sem("prod_im")
        inv_done = sem("inv_done")
        inv_copied = sem("inv_copied")
        xT_done = sem("xT_done")
        xT_copied = sem("xT_copied")
        xT_high = sem("xT_high")
        xT_low = sem("xT_low")
        gate_split = sem("gate_split")
        logits_done = sem("logits_done")
        shifted_done = sem("shifted_done")
        exp_done = sem("exp_done")
        chosen_done = sem("chosen_done")
        counts_done = sem("counts_done")
        cw_done = sem("cw_done")
        w_high = sem("w_high")
        w_low = sem("w_low")
        up_done = sem("up_done")
        silu_done = sem("silu_done")
        mul_done = sem("mul_done")
        h_high = sem("h_high")
        h_low = sem("h_low")
        down_done = sem("down_done")
        evac_done = sem("evac_done")

        block = ctx.enter_context(nc.Block())

        def wait(eng, s, value):
            if not (isinstance(value, int) and value <= 0):
                eng.wait_ge(s, value)

        def f32(ap):
            return ap.bitcast(F32)

        def blocks(t, slot, plain):
            v = t[:, slot, :].rearrange("p (a c) -> p a c", c=BLK)
            return v[:, 0:3:2, :] if plain else v

        @block.sync
        def _(sp):
            xv = dram["x"].rearrange("b (h p) d -> p (b h) d", p=P)
            cv = dram["ctx"].rearrange("b (h p) d -> p (b h) d", p=P)
            sp.dma_start(ident[:, :], dram["ident"]).then_inc(const_loaded, 16)
            sp.dma_start(x[:, :, :], xv).then_inc(x_loaded, 16)
            sp.dma_start(cx[:, :, :], cv).then_inc(ctx_loaded, 16)
            for t, n in ((gwt, "gw"), (gbias, "gbias"), (maskT, "maskT"), (bcv, "bcv"), (cols, "cols"), (iot, "iot"),
                         (tri, "tri"), (wg0, "wg0"), (wg1, "wg1"), (alog, "alog"), (nl, "nl")):
                sp.dma_start(t[tuple(slice(None) for _ in t.shape)], dram[n]).then_inc(const_loaded, 16)

            def load(u, slot, src, plain=False):
                wait(sp, w_low, u - 1)
                sp.dma_start(blocks(wS, slot, plain), src.rearrange("p (a c) -> p a c", c=BLK)).then_inc(stage_loaded[slot], 16)

            load(0, 0, dram["w0"][0])
            load(1, 1, dram["w0"][1])
            sp.wait_ge(gates_done, 1)
            sp.wait_ge(vext_done, 1)
            for t, n in ((FZ, "fz"), (FW, "fw"), (GI, "gi"), (Win, "win"), (peT, "pet"), (Wp1, "wp1"), (Wp2, "wp2")):
                sp.dma_start(t[tuple(slice(None) for _ in t.shape)], dram[n]).then_inc(conv_loaded, 16)
            with sp.Fori(0, N_L0 // 2 - 1) as it:
                load(it * 2 + 2, 0, dram["w0"][bass.ds(it * 2 + 2, 1)].rearrange("a p c -> (a p) c"))
                load(it * 2 + 3, 1, dram["w0"][bass.ds(it * 2 + 3, 1)].rearrange("a p c -> (a p) c"))
            load(N_L0, 0, dram["w0"][N_L0])
            for i in range(4):
                load(U_FA + i, (U_FA + i) % 2, dram["wab"][i], plain=True)
            with sp.Fori(0, N_L1 // 2) as it:
                load(it * 2 + U_L1, 1, dram["w1"][bass.ds(it * 2, 1)].rearrange("a p c -> (a p) c"))
                load(it * 2 + U_L1 + 1, 0, dram["w1"][bass.ds(it * 2 + 1, 1)].rearrange("a p c -> (a p) c"))
            ov = out_d.rearrange("b (h p) d -> p (b h) d", p=P)
            for g in range(4):
                sp.wait_ge(evac_done, 4 * (M_L1 + 4 * N_L1) - 16 + 4 * (g + 1))
                sp.dma_start(ov[:, 4 * g:4 * g + 4, :], x[:, 4 * g:4 * g + 4, :]).then_inc(out_stored, 16)
            sp.wait_ge(out_stored, 64)

        @block.vector
        def _(dve):
            steps = [0]

            def link(ins):
                steps[0] += 1
                ins.then_inc(dve_step, 1)
                dve.wait_ge(dve_step, steps[0])

            lns = [0]

            def layernorm(src, dst, signal):
                for n in range(NT):
                    last = dve.bn_stats(st[:, n, :], src[:, n, :])
                link(last)
                for n in range(NT):
                    last = dve.bn_aggr(mv[:, n, :], st[:, n, :])
                link(last)
                dve.tensor_scalar(ve[:, :], mv[:, :, 1], EPS, None, ALU.add).then_inc(var_done, 1)
                lns[0] += 1
                dve.wait_ge(std_done, lns[0])
                link(dve.reciprocal(rs[:, :], sd[:, :]))
                link(dve.tensor_tensor(nt1[:, :], rs[:, :], rs[:, :], ALU.mult))
                link(dve.tensor_tensor(nt1[:, :], nt1[:, :], ve[:, :], ALU.mult))
                link(dve.tensor_scalar(nt1[:, :], nt1[:, :], -0.5, 1.5, ALU.mult, ALU.add))
                link(dve.tensor_tensor(rs[:, :], rs[:, :], nt1[:, :], ALU.mult))
                for n in range(NT):
                    last = dve.tensor_scalar(dst[:, n, :], src[:, n, :], mv[:, n, 0:1], rs[:, n:n + 1],
                                             ALU.subtract, ALU.mult)
                    if signal:
                        last.then_inc(norm_done, 1)
                if not signal:
                    link(last)

            dve.wait_ge(x_loaded, 16)
            layernorm(x, xn, True)
            dve.memset(ones[:, :], 1.0)
            dve.wait_ge(gates_copied, 1)
            dve.scalar_tensor_tensor(r1[64:, :], rg[64:, :], -1.0, rg[64:, :], ALU.mult, ALU.min).then_inc(negabs_done, 1)
            dve.wait_ge(softplus_done, 2)
            link(dve.scalar_tensor_tensor(r1[64:, :], rg[64:, :], 0.0, r3[64:, :], ALU.min, ALU.subtract))
            dve.tensor_tensor_scan(rF[64:, :], ones[64:, :], r1[64:, :], 0.0, ALU.mult, ALU.add).then_inc(logf_done, 1)
            dve.wait_ge(logf_moved, 1)
            link(dve.tensor_tensor(AE[0:64, :], rg[0:64, :], rF[0:64, :], ALU.subtract))
            link(dve.tensor_tensor_scan(rM[0:64, :], AE[0:64, :], AE[0:64, :], -3.0e38, ALU.max, ALU.max))
            link(dve.tensor_tensor(r3[0:64, :], rF[0:64, :], rM[0:64, :], ALU.add))
            dve.tensor_scalar(AE[64:, :], r3[0:64, :], -1.0, None, ALU.mult)
            link(dve.tensor_scalar(r1[0:64, :], rM[0:64, :], -1.0, None, ALU.mult))
            link(dve.tensor_copy(MHL[0:64, :], r1[0:64, :]))
            link(dve.tensor_tensor(r2[0:64, :], r1[0:64, :], f32(MHL[0:64, :]), ALU.subtract))
            dve.tensor_copy(MHL[64:, :], r2[0:64, :]).then_inc(rows_done, 1)

            def head_scale(b):
                o = ps[:, 4 + 2 * (b % 2):6 + 2 * (b % 2), 0:NH * (DH + 1)].rearrange("p s (h d) -> p s h d", h=NH)
                v = hN[:, b % 2, :].rearrange("p (s h d) -> p s h d", s=2, h=NH)
                dve.wait_ge(pv_done, 8 * (b + 1))
                wait(dve, head_centred, b - 1)
                link(dve.tensor_copy(den[:, :, :], o[:, :, :, DH]))
                link(dve.scalar_tensor_tensor(den[:, :, :], den[:, :, :], -1.0, den[:, :, :], ALU.mult, ALU.max))
                link(dve.tensor_tensor(den[:, :, :], den[:, :, :], eE[:, :, 8 * b:8 * b + 8], ALU.max))
                link(dve.tensor_scalar(den[:, :, :], den[:, :, :], 1e-6, None, ALU.add))
                link(dve.reciprocal(den[:, :, :], den[:, :, :]))
                link(dve.tensor_tensor(v, o[:, :, :, 0:DH], den[:, :, :].unsqueeze(3).to_broadcast([P, 2, NH, DH]), ALU.mult))
                link(dve.tensor_reduce(mean[:, b % 2, :, :], v, AXX, ALU.add))
                dve.tensor_scalar(mean[:, b % 2, :, :], mean[:, b % 2, :, :], 1.0 / DH, None, ALU.mult).then_inc(head_scaled, 1)

            def head_variance(b):
                q = hQ[:, b % 2, :].rearrange("p (s h d) -> p s h d", s=2, h=NH)
                dve.wait_ge(head_squared, b + 1)
                wait(dve, head_rstd, 2 * b)
                link(dve.tensor_reduce(var[:, :, :], q, AXX, ALU.add))
                dve.tensor_scalar(var[:, :, :], var[:, :, :], 1.0 / DH, EPS, ALU.mult, ALU.add).then_inc(head_var, 1)

            for i in range(B * NH):
                dve.wait_ge(qk_done, i + 1)
                dve.wait_ge(decay_done, i + 1)
                wait(dve, pv_done, i - 1)
                dve.scalar_tensor_tensor(Cm[:, i % 2, :], ps[:, i % 2, 0:384], float(DH) ** -0.5, Dm[:, i % 2, :],
                                         ALU.mult, ALU.mult).then_inc(mixed_done, 1)
                if i >= 8 and i % 8 == 1:
                    head_scale(i // 8 - 1)
                if i >= 8 and i % 8 == 5:
                    head_variance(i // 8 - 1)
            head_scale(B - 1)
            head_variance(B - 1)

            dve.wait_ge(const_loaded, 12 * 16)
            dve.wait_ge(window_done, 3)
            dve.wait_ge(pos2_done, 1)
            p2 = ps[:, 4:6, :].rearrange("p a (c d) -> p (a c) d", d=D)
            link(dve.tensor_tensor(wf[:, :, :], p2, bcv[:, 6:7, :].to_broadcast([P, 4, D]), ALU.add))
            for k in range(4):
                last = dve.tensor_scalar(wf[:, k, :], wf[:, k, :], wnd[:, k:k + 1], None, ALU.mult)
            last.then_inc(filt_done, 1)
            for b in range(B):
                dve.wait_ge(zlin_done, b + 1)
                last = dve.tensor_tensor(zn[:, b, :, :], ps[:, b, :].rearrange("p (r d) -> p r d", r=2),
                                         bcv[:, 3:4, :].to_broadcast([P, 2, D]), ALU.add)
                last.then_inc(zlin_copied, 1)
            dve.wait_ge(zlin_copied, B)
            zt = zn[:, :, :, :].rearrange("p b r d -> p (b r) d")
            layernorm(zt, zt, False)
            for g in range(4):
                v = zt[:, 4 * g:4 * g + 4, :]
                link(dve.tensor_tensor(v, v, bcv[:, 4:5, :].to_broadcast([P, 4, D]), ALU.mult))
                dve.tensor_tensor(v, v, bcv[:, 5:6, :].to_broadcast([P, 4, D]), ALU.add).then_inc(zaff_dve, 1)

            dve.wait_ge(filtF_copied, 1)
            dve.wait_ge(head_added, B)

            def spectrum(eng, t, out, mine, a, linker, signal):
                for q in range(4):
                    for fh in range(2):
                        n = 2 * q + fh
                        eng.wait_ge(zF_copied, n + 1)
                        wait(eng, inv_done, n - 1)
                        z = Zs[0:FT, n % 2, :, :].rearrange("p a (b d) -> p a b d", b=2)
                        o = out[0:FT, n % 2, :].rearrange("p (b d) -> p b d", b=2)
                        tt = [t[0:FT, s, :].rearrange("p (b d) -> p b d", b=2) for s in range(2)]
                        for s, (zi, wi, op) in enumerate(a):
                            w = WF[0:FT, s // 2, 2 * wi + fh:2 * wi + fh + 1, :].to_broadcast([FT, 2, D])
                            dst = o if s == 0 else tt[s % 2]
                            linker(eng.tensor_tensor(dst, z[:, 2 * (s // 2) + zi], w, ALU.mult))
                            if s:
                                last = eng.tensor_tensor(o, o, dst, op)
                                if s < 3:
                                    linker(last)
                        last.then_inc(signal, 1)

            spectrum(dve, tv, PR, 0, ((0, 0, None), (1, 1, ALU.subtract), (0, 0, ALU.add), (1, 1, ALU.subtract)), link, prod_re)

            def split_gates():
                link(dve.tensor_copy(wg0H[:, :, :], wg0[:, :, :]))
                link(dve.tensor_tensor(wg0L[:, :, :], wg0[:, :, :], f32(wg0H[:, :, :]), ALU.subtract))
                link(dve.tensor_copy(wg1H[:, :, :], wg1[:, :, :]))
                dve.tensor_tensor(wg1L[:, :, :], wg1[:, :, :], f32(wg1H[:, :, :]), ALU.subtract).then_inc(gate_split, 1)

            def high_parts(r):
                for j in range(8):
                    g, c = j // 2, j % 2
                    dve.wait_ge(xT_copied, 8 * r + j + 1)
                    dve.tensor_copy(xTH[:, c, g * 512:(g + 1) * 512], tF[:, j % 2, :]).then_inc(xT_high, 1)

            def step(n, b, muls):
                if muls is not None:
                    wait(dve, h_low, n - 1)
                    dve.wait_ge(silu_done, n + 1)
                    dve.tensor_tensor(hF[:, b, :], sg[:, b, :], ps[:, 2 + b, :], ALU.mult).then_inc(mul_done, 1)
                    dve.wait_ge(mul_done, n + 1 - muls)
                else:
                    dve.wait_ge(silu_done, n + 1)
                wait(dve, down_done, n - 1)
                dve.tensor_copy(hH[:, b, :], hF[:, b, :]).then_inc(h_high, 1)

            def evacuate(m, n, g, pair, dst, scale):
                dve.wait_ge(down_done, n + 1)
                wait(dve, evac_done, m * 4)
                for t in range(4):
                    tile = 4 * g + t
                    acc = ps[:, 4 + 2 * pair + t // 2, (t % 2) * 256:(t % 2) * 256 + 256]
                    if scale is None:
                        last = dve.tensor_tensor(dst[:, tile, :], acc, dst[:, tile, :], ALU.add)
                    else:
                        last = dve.scalar_tensor_tensor(dst[:, tile, :], acc, scale(tile), dst[:, tile, :], ALU.mult, ALU.add)
                    last.then_inc(evac_done, 1)

            dve.wait_ge(inv_copied, 8)
            layernorm(x, xn, True)
            split_gates()
            high_parts(0)
            lg = ps[:, 7, :].rearrange("p (n e) -> p n e", n=NT)
            m1 = sm[:, :, 0]

            def bc(ap, k):
                return ap.unsqueeze(2).to_broadcast([P, NT, k])

            dve.wait_ge(logits_done, 1)
            link(dve.tensor_reduce(m1, lg, AXX, ALU.max))
            dve.tensor_tensor(sc0[:, :, :], lg, bc(m1, E0), ALU.subtract).then_inc(shifted_done, 1)
            dve.wait_ge(exp_done, 1)
            link(dve.tensor_reduce(m1, sc0[:, :, :], AXX, ALU.add))
            link(dve.reciprocal(m1, m1))
            link(dve.tensor_tensor(sc0[:, :, :], sc0[:, :, :], bc(m1, E0), ALU.mult))
            for n in range(NT):
                last = dve.max(mx8[:, n, :], sc0[:, n, :])
            link(last)
            for n in range(NT):
                last = dve.max_index(ix8[:, n, :], mx8[:, n, :], sc0[:, n, :])
            link(last)
            link(dve.tensor_copy(ixf[:, :, :], ix8[:, :, :]))
            io = iot[:, :].unsqueeze(1).to_broadcast([P, NT, E0])
            link(dve.tensor_tensor(sc1[:, :, :], io, bc(ixf[:, :, 0], E0), ALU.is_equal))
            for k in range(1, TOPK):
                link(dve.tensor_tensor(sc2[:, :, :], io, bc(ixf[:, :, k], E0), ALU.is_equal))
                link(dve.tensor_tensor(sc1[:, :, :], sc1[:, :, :], sc2[:, :, :], ALU.add))
            dve.tensor_copy(selm[:, :, :], sc1[:, :, :]).then_inc(chosen_done, 1)
            link(dve.tensor_tensor(cw0[:, :, :], sc0[:, :, :], sc1[:, :, :], ALU.mult))
            dve.wait_ge(counts_done, 1)
            link(dve.memset(sc2[:, 0, :], 0.0))
            tot = ps[:, 5, :].rearrange("p (n e) -> p n e", n=NT)
            for n in range(1, NT):
                link(dve.tensor_tensor(sc2[:, n, :], sc2[:, n - 1, :], tot[:, n - 1, :], ALU.add))
            link(dve.tensor_tensor(sc2[:, :, :], ps[:, 6, :].rearrange("p (n e) -> p n e", n=NT), sc2[:, :, :], ALU.add))
            link(dve.tensor_scalar(sc2[:, :, :], sc2[:, :, :], float(CAP), None, ALU.is_lt))
            dve.tensor_tensor(cw0[:, :, :], cw0[:, :, :], sc2[:, :, :], ALU.mult).then_inc(cw_done, 1)
            dve.wait_ge(cw_done, 1)

            for i in range(8):
                step(i, i % 2, 0)
                if i in (2, 4, 6):
                    evacuate(i // 2 - 1, i - 1, i // 2 - 1, (i // 2 - 1) % 2, x, None)
            evacuate(3, 7, 3, 1, x, None)
            with dve.Fori(0, N_L0 // 2) as it:
                def routed(local):
                    evacuate(it * 16 + (M_L0 + local), it * 16 + (8 + local), local % 8 // 2, local % 2, x,
                             lambda tile: cw0[:, tile, bass.ds(it * 4 + (2 * (local // 8) + local % 2), 1)])
                for local in range(16):
                    step(it * 16 + (8 + local), local % 2, 0)
                    if local:
                        routed(local - 1)
                routed(15)

            def dense(u0, m0):
                for i in range(16):
                    step(8 * u0 + i, i % 2, None)
                    if i % 2 == 0 and i:
                        g = i // 2 - 1
                        evacuate(m0 + g, 8 * u0 + i - 1, g % 4, g % 2, ya, None)
                evacuate(m0 + 7, 8 * u0 + 15, 3, 1, ya, None)

            dve.wait_ge(evac_done, 4 * M_FA)
            layernorm(x, ya, False)
            layernorm(ya, xn, True)
            dve.wait_ge(norm_done, 3 * NT)
            link(dve.tensor_tensor(ya[:, :, :], ya[:, :, :], bcv[:, 0:1, :].to_broadcast([P, NT, D]), ALU.add))
            high_parts(1)
            dense(U_FA, M_FA)
            dve.wait_ge(evac_done, 4 * M_FB)
            link(dve.tensor_tensor(ya[:, :, :], ya[:, :, :], dcw[:, :, :], ALU.mult))
            layernorm(ya, xn, True)
            dve.wait_ge(norm_done, 4 * NT)
            link(dve.tensor_tensor(ya[:, :, :], ya[:, :, :], bcv[:, 1:2, :].to_broadcast([P, NT, D]), ALU.add))
            high_parts(2)
            dense(U_FB, M_FB)
            dve.wait_ge(evac_done, 4 * M_L1)
            link(dve.tensor_tensor(x[:, :, :], x[:, :, :], ya[:, :, :], ALU.add))

            layernorm(x, xn, True)
            high_parts(3)
            l1 = ps[:, 7, 0:NT * 16].rearrange("p (n a e) -> p n a e", n=NT, a=2)
            s1 = sc0[:, :, 0:16].rearrange("p n (a e) -> p n a e", a=2)
            smb = sm[:, :, :].unsqueeze(3).to_broadcast([P, NT, 2, E1])
            dve.wait_ge(logits_done, 2)
            link(dve.tensor_reduce(sm[:, :, :], l1, AXX, ALU.max))
            link(dve.tensor_tensor(s1, l1, smb, ALU.subtract))
            dve.tensor_scalar(s1[:, :, 1, :], s1[:, :, 1, :], 10.0, None, ALU.mult).then_inc(shifted_done, 1)
            dve.wait_ge(exp_done, 2)
            link(dve.tensor_reduce(sm[:, :, :], s1, AXX, ALU.add))
            link(dve.reciprocal(sm[:, :, :], sm[:, :, :]))
            link(dve.tensor_tensor(s1, s1, smb, ALU.mult))
            link(dve.tensor_tensor(sc1[:, :, 0:8], s1[:, :, 0, :], s1[:, :, 1, :], ALU.mult))
            link(dve.tensor_reduce(sm2[:, :], sc1[:, :, 0:8], AXX, ALU.add))
            link(dve.tensor_scalar(sm2[:, :], sm2[:, :], 1e-9, None, ALU.add))
            link(dve.reciprocal(sm2[:, :], sm2[:, :]))
            for a in range(2):
                last = dve.tensor_tensor(cw2[:, :, a:16:2], sc1[:, :, 0:8], bc(sm2[:, :], E1), ALU.mult)
            last.then_inc(cw_done, 1)
            dve.wait_ge(cw_done, 2)
            with dve.Fori(0, N_L1 // 2) as it:
                def mixed(local):
                    evacuate(it * 8 + (M_L1 + local // 2), it * 16 + (8 * U_L1 + local), local // 2 % 4, local // 2 % 2, x,
                             lambda tile: cw2[:, tile, bass.ds(it, 1)])
                for local in range(16):
                    step(it * 16 + (8 * U_L1 + local), local % 2, PLAIN)
                    if local and local % 2 == 0:
                        mixed(local - 1)
                mixed(15)

        @block.scalar
        def _(act):
            lns = [0]

            def deviation():
                lns[0] += 1
                act.wait_ge(var_done, lns[0])
                act.activation(sd[:, :], ve[:, :], ACT.Sqrt).then_inc(std_done, 1)

            def mix_copy(j, dst):
                act.wait_ge(mixT_done, j + 1)
                act.activation(dst, ps[:, j % 4, :], ACT.Identity).then_inc(mixT_copied, 1)

            for j in range(8):
                mix_copy(j, kT[:, j % 2, (j // 2) * 512:(j // 2 + 1) * 512])
            deviation()
            for j in range(8):
                mix_copy(8 + j, qT[:, j % 2, (j // 2) * 512:(j // 2 + 1) * 512])
            act.wait_ge(gates_done, 1)
            act.wait_ge(const_loaded, 12 * 16)
            act.activation(rg[:, :], ps[:, 4, 0:256], ACT.Identity, bias=gbias[:, :]).then_inc(gates_copied, 1)
            act.wait_ge(negabs_done, 1)
            act.activation(r2[64:, :], r1[64:, :], ACT.Exp).then_inc(softplus_done, 1)
            act.wait_ge(softplus_done, 1)
            act.activation(r3[64:, :], r2[64:, :], ACT.Ln, bias=1.0).then_inc(softplus_done, 1)
            act.wait_ge(logf_done, 1)
            act.activation(rF[0:64, :], rF[64:, :], ACT.Copy).then_inc(logf_moved, 1)
            act.wait_ge(rowsT_done, 1)
            rT = ps[:, 5, 0:256].rearrange("p (h r) -> p h r", h=2)
            act.activation(aT[:, :, :], rT[:, :, 0:64], ACT.Copy)
            act.activation(eE[:, :, :], rT[:, :, 64:128], ACT.Exp).then_inc(rowsT_copied, 1)
            act.wait_ge(rowsT_copied, 1)

            def square(b):
                act.wait_ge(head_centred, b + 1)
                wait(act, head_var, b - 1)
                act.activation(hQ[:, b % 2, :], hC[:, b % 2, :], ACT.Square).then_inc(head_squared, 1)

            def inverse_deviation(b):
                act.wait_ge(head_var, b + 1)
                wait(act, head_added, b - 1)
                act.activation(rstd[:, b % 2, :, :], var[:, :, :], ACT.Ln).then_inc(head_rstd, 1)
                act.wait_ge(head_rstd, 2 * b + 1)
                act.activation(rstd[:, b % 2, :, :], rstd[:, b % 2, :, :], ACT.Exp, scale=-0.5).then_inc(head_rstd, 1)

            for i in range(B * NH):
                act.wait_ge(arg_done, i + 1)
                wait(act, mixed_done, i - 1)
                act.activation(Dm[:, i % 2, 0:256], ps[:, 2 + i % 2, 0:256], ACT.Exp, bias=aT[:, 0, i:i + 1])
                act.activation(Dm[:, i % 2, 256:384], ps[:, 2 + i % 2, 256:384], ACT.Exp, bias=aT[:, 1, i:i + 1]).then_inc(decay_done, 1)
                if i >= 8 and i % 8 == 3:
                    square(i // 8 - 1)
                if i >= 8 and i % 8 == 7:
                    inverse_deviation(i // 8 - 1)
            square(B - 1)
            inverse_deviation(B - 1)

            act.activation(ea[:, :], alog[:, :], ACT.Exp).then_inc(window_done, 1)
            act.wait_ge(window_done, 1)
            act.activation(wnd[:, :], nl[:, :], ACT.Exp, scale=ea[:, :]).then_inc(window_done, 1)
            act.wait_ge(pos1_done, 1)
            for k in range(3):
                rows = P if k < 2 else 64
                last = act.activation(h1T[0:rows, k, :], ps[0:rows, k, :], ACT.Silu, bias=cols[0:rows, 16 + k:17 + k])
            last.then_inc(pos1_silu, 1)
            act.wait_ge(window_done, 2)
            act.activation(ea[:, :], alog[:, :], ACT.Copy).then_inc(window_done, 1)
            act.wait_ge(filtF_done, 1)
            act.activation(WF[0:FT, :, :, :].rearrange("p e f d -> p (e f d)"), ps[0:FT, 0:4, :].rearrange("p a c -> p (a c)"),
                           ACT.Copy).then_inc(filtF_copied, 1)
            deviation()

            def inverse_copy(q):
                for h in range(2):
                    act.wait_ge(inv_done, 2 * (q + 1))
                    act.activation(dcw[:, 4 * q + h:4 * q + 4:2, :], ps[:, 4 + 2 * (q % 2) + h, :].rearrange("p (b d) -> p b d", b=2),
                                   ACT.Copy).then_inc(inv_copied, 1)

            act.wait_ge(head_added, B)
            for n in range(8):
                act.wait_ge(zF_done, n + 1)
                wait(act, prod_re, n - 1)
                wait(act, prod_im, n - 1)
                act.activation(Zs[0:FT, n % 2, :, :], ps[0:FT, 0:4, :], ACT.Copy).then_inc(zF_copied, 1)
                if n >= 2 and n % 2 == 0:
                    inverse_copy(n // 2 - 1)
            inverse_copy(3)

            def transposed(r, gain=None, offset=None):
                for j in range(8):
                    c = j % 2
                    act.wait_ge(xT_done, 8 * r + j + 1)
                    wait(act, xT_high, 8 * r + j - 1)
                    wait(act, xT_low, 8 * r + j - 1)
                    if gain is None:
                        last = act.activation(tF[:, c, :], ps[:, j % 4, :], ACT.Identity)
                    else:
                        last = act.activation(tF[:, c, :], ps[:, j % 4, :], ACT.Identity,
                                              scale=cols[:, gain + c:gain + c + 1], bias=cols[:, offset + c:offset + c + 1])
                    last.then_inc(xT_copied, 1)

            def split_high(u, slot, loaded, plain=False):
                act.wait_ge(stage_loaded[slot], loaded)
                wait(act, down_done, (u - 1) * 8)
                act.activation(blocks(wH, slot, plain), blocks(wS, slot, plain), ACT.Copy).then_inc(w_high, 1)

            def silu(n, b, muls):
                wait(act, mul_done, n - 1 - muls)
                act.wait_ge(up_done, n + 1)
                act.activation(sg[:, b, :], ps[:, b, :], ACT.Silu).then_inc(silu_done, 1)

            deviation()
            transposed(0)
            act.wait_ge(shifted_done, 1)
            act.activation(sc0[:, :, :], sc0[:, :, :], ACT.Exp).then_inc(exp_done, 1)
            split_high(0, 0, 16)
            for i in range(8):
                silu(i, i % 2, 0)
                if i == 1:
                    split_high(1, 1, 16)
            with act.Fori(0, N_L0 // 2) as it:
                for local in range(16):
                    silu(it * 16 + (8 + local), local % 2, 0)
                    if local == 1:
                        split_high(it * 2 + 2, 0, it * 16 + 32)
                    if local == 9:
                        split_high(it * 2 + 3, 1, it * 16 + 32)

            def dense(u0, bias):
                for i in range(16):
                    n, b, u = 8 * u0 + i, i % 2, u0 + i // 8
                    c = 2 * (i // 8) + i % 2
                    act.wait_ge(up_done, n + 1)
                    act.wait_ge(h_low, n - 1)
                    act.activation(hF[:, b, :], ps[:, b, :], ACT.Silu, bias=cols[:, bias + c:bias + c + 1]).then_inc(silu_done, 1)
                    if i % 8 == 1:
                        split_high(u + 1, (u + 1) % 2, 16 * ((u + 1) // 2 + 1), plain=u + 1 < U_L1)

            deviation()
            deviation()
            transposed(1, 0, 2)
            dense(U_FA, 8)
            deviation()
            transposed(2, 4, 6)
            dense(U_FB, 12)
            deviation()
            transposed(3)
            act.wait_ge(shifted_done, 2)
            s1 = sc0[:, :, 0:16]
            act.activation(s1, s1, ACT.Exp).then_inc(exp_done, 1)

            def experts(it, last):
                for local in range(16):
                    silu(it * 16 + (8 * U_L1 + local), local % 2, PLAIN)
                    if local == 1:
                        split_high(it * 2 + (U_L1 + 1), 0, it * 16 + 16 * (U_L1 // 2 + 2))
                    if local == 9 and not last:
                        split_high(it * 2 + (U_L1 + 2), 1, it * 16 + 16 * (U_L1 // 2 + 2))

            with act.Fori(0, N_L1 // 2 - 1) as it:
                experts(it, False)
            experts(N_L1 // 2 - 1, True)

        @block.gpsimd
        def _(pool):
            steps = [0]

            def link(ins):
                steps[0] += 1
                ins.then_inc(pool_step, 1)
                pool.wait_ge(pool_step, steps[0])

            link(pool.memset(gateW[:, :, :, :], 0.0))
            pool.wait_ge(const_loaded, 12 * 16)
            link(pool.tensor_tensor(gwt[:, 2:4, :], gwt[:, 2:4, :], gwt[:, 4:6, :], ALU.add))
            for b in range(B):
                for a in range(2):
                    last = pool.tensor_copy(gateW[:, :, b, 64 * a + 8 * b:64 * a + 8 * b + 8], gwt[:, 0:4, 8 * a:8 * a + 8])
            last.then_inc(gatew_done, 1)
            pool.tensor_copy(idb[:, :], ident[:, :])
            link(pool.tensor_tensor(id2[:, :], ident[:, 0:64], ident[:, 64:128], ALU.add))
            pool.tensor_copy(sel[:, :, :], id2[:, :].unsqueeze(2).to_broadcast([P, 64, P])).then_inc(sel_done, 1)
            pool.wait_ge(ctx_loaded, 16)
            pool.memset(vext[:, :, :, DH:DH + 1], 1.0)
            pool.tensor_copy(vext[:, :, :, 0:DH], cx[:, :, :].rearrange("p n (h d) -> p n h d", h=NH)).then_inc(vext_done, 1)
            for b in range(B):
                v = hN[:, b % 2, :].rearrange("p (g d) -> p g d", d=DH)
                hc = hC[:, b % 2, :].rearrange("p (g d) -> p g d", d=DH)
                hr = hR[:, b % 2, :].rearrange("p (g d) -> p g d", d=DH)
                mb = mean[:, b % 2, :, :].rearrange("p s h -> p (s h)").unsqueeze(2).to_broadcast([P, 2 * NH, DH])
                rb = rstd[:, b % 2, :, :].rearrange("p s h -> p (s h)").unsqueeze(2).to_broadcast([P, 2 * NH, DH])
                pool.wait_ge(head_scaled, b + 1)
                pool.tensor_tensor(hc, v, mb, ALU.subtract).then_inc(head_centred, 1)
                pool.wait_ge(head_rstd, 2 * (b + 1))
                link(pool.tensor_tensor(hr, hc, rb, ALU.mult))
                h2 = hR[:, b % 2, :].rearrange("p (s d) -> p s d", s=2)
                link(pool.tensor_tensor(h2, h2, bcv[:, 2:3, :].to_broadcast([P, 2, D]), ALU.mult))
                pool.tensor_tensor(x[:, 2 * b:2 * b + 2, :], x[:, 2 * b:2 * b + 2, :], h2, ALU.add).then_inc(head_added, 1)

            pool.wait_ge(filtF_copied, 1)
            for q in range(4):
                for fh in range(2):
                    n = 2 * q + fh
                    pool.wait_ge(zF_copied, n + 1)
                    wait(pool, inv_done, n - 1)
                    z = Zs[0:FT, n % 2, :, :].rearrange("p a (b d) -> p a b d", b=2)
                    o = PI[0:FT, n % 2, :].rearrange("p (b d) -> p b d", b=2)
                    tt = [tp[0:FT, s, :].rearrange("p (b d) -> p b d", b=2) for s in range(2)]
                    for s, (zi, wi) in enumerate(((0, 1), (1, 0), (0, 1), (1, 0))):
                        w = WF[0:FT, s // 2, 2 * wi + fh:2 * wi + fh + 1, :].to_broadcast([FT, 2, D])
                        dst = o if s == 0 else tt[s % 2]
                        link(pool.tensor_tensor(dst, z[:, 2 * (s // 2) + zi], w, ALU.mult))
                        if s:
                            last = pool.tensor_tensor(o, o, dst, ALU.add)
                            if s < 3:
                                link(last)
                    last.then_inc(prod_im, 1)

            def low_parts(r):
                for j in range(8):
                    g, c = j // 2, j % 2
                    pool.wait_ge(xT_high, 8 * r + j + 1)
                    pool.tensor_tensor(xTL[:, c, g * 512:(g + 1) * 512], tF[:, j % 2, :],
                                       f32(xTH[:, c, g * 512:(g + 1) * 512]), ALU.subtract).then_inc(xT_low, 1)

            def split_low(u, slot, plain=False):
                pool.wait_ge(w_high, u + 1)
                pool.tensor_tensor(blocks(wL, slot, plain), blocks(wS, slot, plain), f32(blocks(wH, slot, plain)),
                                   ALU.subtract).then_inc(w_low, 1)

            def low(n, b):
                pool.wait_ge(h_high, n + 1)
                pool.tensor_tensor(hL[:, b, :], hF[:, b, :], f32(hH[:, b, :]), ALU.subtract).then_inc(h_low, 1)

            low_parts(0)
            split_low(0, 0)
            for i in range(8):
                low(i, i % 2)
                if i == 1:
                    split_low(1, 1)
            with pool.Fori(0, N_L0 // 2) as it:
                for local in range(16):
                    low(it * 16 + (8 + local), local % 2)
                    if local == 1:
                        split_low(it * 2 + 2, 0, False)
                    if local == 7:
                        pass
                    if local == 9:
                        split_low(it * 2 + 3, 1, False)

            def dense(u0):
                for i in range(16):
                    low(8 * u0 + i, i % 2)
                    if i % 8 == 1:
                        u = u0 + i // 8 + 1
                        split_low(u, u % 2, u < U_L1)

            low_parts(1)
            dense(U_FA)
            low_parts(2)
            dense(U_FB)
            low_parts(3)

            def experts(it, last):
                for local in range(16):
                    low(it * 16 + (8 * U_L1 + local), local % 2)
                    if local == 1:
                        split_low(it * 2 + (U_L1 + 1), 0)
                    if local == 9 and not last:
                        split_low(it * 2 + (U_L1 + 2), 1)

            with pool.Fori(0, N_L1 // 2 - 1) as it:
                experts(it, False)
            experts(N_L1 // 2 - 1, True)

        @block.tensor
        def _(pe):
            pe.wait_ge(const_loaded, 12 * 16)
            pe.wait_ge(ctx_loaded, 16)
            for j in range(16):
                src, g, c = (cx, xn)[j // 8], j % 8 // 2, j % 2
                wait(pe, mixT_copied, j - 3)
                if src is xn:
                    pe.wait_ge(norm_done, 4 * g + 4)
                for t in range(4):
                    last = pe.transpose(ps[:, j % 4, t * P:(t + 1) * P], src[:, 4 * g + t, c * P:(c + 1) * P], ident[:, :])
                last.then_inc(mixT_done, 1)
            pe.wait_ge(gatew_done, 1)
            pe.wait_ge(mixT_copied, 16)
            for b in range(B):
                for k in range(4):
                    rhs = (qT, kT)[k // 2][:, k % 2, b * SEQ:(b + 1) * SEQ]
                    last = pe.matmul(ps[:, 4, 0:SEQ], gateW[:, k, b, :], rhs, start=(b == 0 and k == 0), stop=(b == B - 1 and k == 3))
            last.then_inc(gates_done, 1)
            pe.wait_ge(rows_done, 1)
            for h in range(2):
                last = pe.transpose(ps[:, 5, h * P:(h + 1) * P], AE[:, h * P:(h + 1) * P], ident[:, :])
            last.then_inc(rowsT_done, 1)
            pe.wait_ge(sel_done, 1)
            pe.wait_ge(vext_done, 1)
            pe.wait_ge(rowsT_copied, 1)

            def scores(i):
                b, h = i // NH, i % NH
                c, r = h // 4, DH * (h % 4)
                t0 = b * SEQ
                wait(pe, mixed_done, i - 1)
                pe.matmul(ps[:, i % 2, 0:256], kT[r:r + DH, c, t0:t0 + P], qT[r:r + DH, c, t0:t0 + SEQ], start=True, stop=True)
                pe.matmul(ps[:, i % 2, 256:384], kT[r:r + DH, c, t0 + P:t0 + SEQ], qT[r:r + DH, c, t0 + P:t0 + SEQ],
                          start=True, stop=True).then_inc(qk_done, 1)
                wait(pe, decay_done, i - 1)
                pe.matmul(ps[:, 2 + i % 2, 0:384], idb[:, :], maskT[:, :], start=True, stop=False, skip_group_check=True)
                pe.matmul(ps[:, 2 + i % 2, 0:256], sel[:, i, :], MHL[:, :], start=False, stop=False, skip_group_check=True)
                pe.matmul(ps[:, 2 + i % 2, 256:384], sel[:, i, :], MHL[:, P:SEQ], start=False, stop=True,
                          skip_group_check=True).then_inc(arg_done, 1)

            def values(i):
                b, h = i // NH, i % NH
                o0, o1 = (ps[:, 4 + 2 * (b % 2) + s, h * (DH + 1):(h + 1) * (DH + 1)] for s in range(2))
                pe.wait_ge(mixed_done, i + 1)
                if h == 0:
                    wait(pe, head_scaled, b - 1)
                pe.matmul(o0, Cm[:, i % 2, 0:P], vext[:, 2 * b, h, :], start=True, stop=True)
                pe.matmul(o1, Cm[:, i % 2, P:2 * P], vext[:, 2 * b, h, :], start=True, stop=False)
                pe.matmul(o1, Cm[:, i % 2, 2 * P:3 * P], vext[:, 2 * b + 1, h, :], start=False, stop=True).then_inc(pv_done, 1)

            for i in range(B * NH):
                scores(i)
                if i:
                    values(i - 1)
            values(B * NH - 1)

            pe.wait_ge(conv_loaded, 7 * 16)
            pe.wait_ge(mixed_done, B * NH)
            pe.wait_ge(decay_done, B * NH)
            for k in range(3):
                rows = P if k < 2 else 64
                last = pe.matmul(ps[0:rows, k, :], Wp1[:, k * P:k * P + rows], peT[:, :], start=True, stop=True)
            last.then_inc(pos1_done, 1)
            pe.wait_ge(pos1_silu, 1)
            pe.wait_ge(head_scaled, B)
            for lt in range(4):
                first = 256 * (lt % 2) + lt // 2
                for k in range(3):
                    rows = P if k < 2 else 64
                    last = pe.matmul(ps[:, 4 + lt // 2, (lt % 2) * D:(lt % 2 + 1) * D], h1T[0:rows, k, first:first + 255:2],
                                     Wp2[0:rows, k, :], start=k == 0, stop=k == 2)
            last.then_inc(pos2_done, 1)
            pe.wait_ge(filt_done, 1)
            for e in range(2):
                for f in range(4):
                    for k in range(2):
                        last = pe.matmul(ps[0:FT, 2 * e + f // 2, (f % 2) * D:(f % 2 + 1) * D], FW[:, 2 * e + k, f, :],
                                         wf[:, 2 * e + k, :], start=k == 0, stop=k == 1)
            last.then_inc(filtF_done, 1)
            pe.wait_ge(filtF_copied, 1)
            for b in range(B):
                for r in range(2):
                    for k in range(2):
                        last = pe.matmul(ps[:, b, r * D:(r + 1) * D], kT[:, k, b * SEQ + r:(b + 1) * SEQ:2], Win[:, k, :],
                                         start=k == 0, stop=k == 1)
                last.then_inc(zlin_done, 1)

            def inverse(n):
                q, fh = n // 2, n % 2
                pe.wait_ge(prod_re, n + 1)
                pe.wait_ge(prod_im, n + 1)
                if fh == 0:
                    wait(pe, inv_copied, 2 * (q - 1))
                for h in range(2):
                    for ri, src in enumerate((PR, PI)):
                        last = pe.matmul(ps[:, 4 + 2 * (q % 2) + h, :], GI[0:FT, 2 * ri + fh, h * P:(h + 1) * P], src[0:FT, n % 2, :],
                                         start=(fh == 0 and ri == 0), stop=(fh == 1 and ri == 1))
                last.then_inc(inv_done, 1)

            pe.wait_ge(zlin_copied, B)
            for n in range(8):
                q, fh = n // 2, n % 2
                pe.wait_ge(zaff_dve, q + 1)
                wait(pe, zF_copied, n)
                for e in range(2):
                    for ri in range(2):
                        last = pe.matmul(ps[0:FT, 2 * e + ri, :].rearrange("p (b d) -> p b d", b=2), FZ[:, 2 * ri + fh, :],
                                         zn[:, 2 * q:2 * q + 2, e, :], start=True, stop=True)
                last.then_inc(zF_done, 1)
                if n:
                    inverse(n - 1)
            inverse(7)

            def transposes(r):
                for j in range(8):
                    g, c = j // 2, j % 2
                    if j >= 4:
                        pe.wait_ge(xT_copied, 8 * r + j - 3)
                    pe.wait_ge(norm_done, NT * (r + 1) + 4 * g + 4)
                    for t in range(4):
                        last = pe.transpose(ps[:, j % 4, t * P:(t + 1) * P], xn[:, 4 * g + t, c * P:(c + 1) * P], ident[:, :])
                    last.then_inc(xT_done, 1)

            def logits(r, gH, gL, width):
                pe.wait_ge(gate_split, 1)
                pe.wait_ge(xT_low, 8 * (r + 1))
                for n in range(NT):
                    q = 0
                    for k in range(2):
                        for a, g in ((xTH, gH), (xTL, gH), (xTH, gL)):
                            last = pe.matmul(ps[:, 7, n * width:(n + 1) * width], a[:, k, n * P:(n + 1) * P], g[:, k, :],
                                             start=q == 0, stop=q == 5)
                            q += 1
                last.then_inc(logits_done, 1)

            def up(n, local, u, slot, muls):
                g, c, b = local % 8 // 2, local % 2, local % 2
                if local % 8 == 0:
                    pe.wait_ge(w_low, u + 1)
                wait(pe, silu_done, n - 1)
                if muls is not None:
                    wait(pe, mul_done, n - 1 - muls)
                for half in range(2 if muls is not None else 1):
                    q = 0
                    for k in range(2):
                        col = half * BLK + k * D + c * P
                        for w, v in ((wH, xTH), (wL, xTH), (wH, xTL)):
                            last = pe.matmul(ps[:, 2 * half + b, :], w[:, slot, col:col + P], v[:, k, g * 512:(g + 1) * 512],
                                             start=q == 0, stop=q == 5)
                            q += 1
                last.then_inc(up_done, 1)

            def down(n, local, m, slot, pair, opens, closes):
                c, b = local % 2, local % 2
                pe.wait_ge(h_low, n + 1)
                if opens:
                    wait(pe, evac_done, (m - 1) * 4)
                for t in range(4):
                    o = ps[:, 4 + 2 * pair + t // 2, (t % 2) * D:(t % 2 + 1) * D]
                    col = 2 * BLK + c * D
                    for q, (h, w) in enumerate(((hH, wH), (hL, wH), (hH, wL))):
                        last = pe.matmul(o, h[:, b, t * P:(t + 1) * P], w[:, slot, col:col + D],
                                         start=(opens and t % 2 == 0 and q == 0), stop=(closes and q == 2), skip_group_check=True)
                last.then_inc(down_done, 1)

            transposes(0)
            logits(0, wg0H, wg0L, E0)
            pe.wait_ge(chosen_done, 1)
            rhs = selm[:, :, :].rearrange("p n e -> p (n e)")
            pe.matmul(ps[:, 6, :], tri[:, 0, :], rhs, start=True, stop=True)
            pe.matmul(ps[:, 5, :], tri[:, 1, :], rhs, start=True, stop=True).then_inc(counts_done, 1)
            pe.wait_ge(xT_copied, 8)

            def routed_up(it, local):
                up(it * 16 + (8 + local), local, it * 2 + (1 + local // 8), 1 - local // 8, 0)

            def routed_down(it, local):
                down(it * 16 + (8 + local), local, it * 16 + (M_L0 + local), 1 - local // 8, local % 2, True, True)

            up(0, 0, 0, 0, 0)
            pe.wait_ge(cw_done, 1)
            for i in range(8):
                if i < 7:
                    up(i + 1, i + 1, 0, 0, 0)
                else:
                    routed_up(0, 0)
                down(i, i, i // 2, 0, i // 2 % 2, i % 2 == 0, i % 2 == 1)

            def routed(it, last):
                for local in range(16):
                    if local < 15:
                        routed_up(it, local + 1)
                    elif not last:
                        routed_up(it + 1, 0)
                    routed_down(it, local)

            with pe.Fori(0, N_L0 // 2 - 1) as it:
                routed(it, False)
            routed(N_L0 // 2 - 1, True)

            def dense(u0, m0):
                for i in range(17):
                    if i < 16:
                        up(8 * u0 + i, i, u0 + i // 8, (u0 + i // 8) % 2, None)
                    if i:
                        j = i - 1
                        down(8 * u0 + j, j, m0 + j // 2, (u0 + j // 8) % 2, j // 2 % 2, j % 2 == 0, j % 2 == 1)

            transposes(1)
            pe.wait_ge(xT_low, 16)
            dense(U_FA, M_FA)
            transposes(2)
            pe.wait_ge(xT_low, 24)
            dense(U_FB, M_FB)
            transposes(3)
            logits(3, wg1H, wg1L, 16)

            def expert_up(it, local):
                up(it * 16 + (8 * U_L1 + local), local, it * 2 + (U_L1 + local // 8), 1 - local // 8, PLAIN)

            def expert_down(it, local):
                down(it * 16 + (8 * U_L1 + local), local, it * 8 + (M_L1 + local // 2), 1 - local // 8, local // 2 % 2,
                     local % 2 == 0, local % 2 == 1)

            def experts(it, last):
                for local in range(16):
                    if local < 15:
                        expert_up(it, local + 1)
                    elif not last:
                        expert_up(it + 1, 0)
                    expert_down(it, local)

            expert_up(0, 0)
            pe.wait_ge(cw_done, 2)
            with pe.Fori(0, N_L1 // 2 - 1) as it:
                experts(it, False)
            experts(N_L1 // 2 - 1, True)


def constants(np):
    n = 4 * FT
    w = 2 * np.pi * (np.arange(2 * FT) + 0.5) / n
    p = np.arange(P)

    def forward(pos):
        a = np.outer(pos, w)
        return np.concatenate([np.cos(a), -np.sin(a)], 1).reshape(len(pos), 4, FT)

    pos = np.arange(2 * P)
    odd = forward(pos + 1)
    fw = np.concatenate([forward(pos).reshape(2, P, 4, FT), odd.reshape(2, P, 4, FT)]).transpose(1, 0, 2, 3)
    a = np.outer(w, np.arange(D))
    gi = np.concatenate([np.cos(a), -np.sin(a)]).reshape(4, FT, D) * (2.0 / n)
    gfull = np.zeros((P, 4, D))
    gfull[:FT] = gi.transpose(1, 0, 2)
    t, s = np.arange(P)[:, None], np.arange(P)[None, :]
    mask = np.zeros((P, 3 * P))
    mask[:, 0:P] = mask[:, 2 * P:] = np.where(t <= s, 0.0, -1e30)
    tri = np.stack([(t < s) * 1.0, np.ones((P, P))], 1)
    nl = -np.stack([2 * p, 2 * (p + P), 2 * p + 1, 2 * (p + P) + 1], 1)
    f = np.float32
    return {"ident": np.eye(P).astype(f), "fz": forward(p).astype(f), "fw": fw.astype(f), "gi": gfull.astype(f),
            "maskT": mask, "tri": tri, "nl": nl.astype(f), "iot": np.tile(np.arange(E0), (P, 1)).astype(f)}


def kernel(**inputs):
    import ml_dtypes
    import numpy as np
    import concourse.bacc as bacc
    from concourse.bass_utils import run_bass_kernel_spmd as run

    nc = bacc.Bacc("TRN2", target_bir_lowering=False, num_devices=1)
    I = {k: np.asarray(v) for k, v in inputs.items()}

    def chunked(w):
        return w.reshape(2, P, -1).transpose(1, 0, 2)

    def column(v, k):
        return np.concatenate([v, np.zeros(P * k - len(v), v.dtype)]).reshape(k, P).T

    A = constants(np)
    A["maskT"] = A["maskT"].astype(ml_dtypes.bfloat16)
    A["tri"] = A["tri"].astype(ml_dtypes.bfloat16)
    A["x"], A["ctx"] = I["x"], I["ctx_1024"]
    gates = np.concatenate([I["L0_xattn_igate_w"], I["L0_xattn_fgate_w"]], 0).T
    A["gw"] = gates.reshape(6, P, 16).transpose(1, 0, 2)
    A["gbias"] = np.concatenate([np.tile(I["L0_xattn_igate_b"], B), np.tile(I["L0_xattn_fgate_b"], B)]).reshape(P, 1)
    rows = np.stack([I[n] for n in ("L1_xattn_b1b", "L1_xattn_b2b", "L0_xattn_norm_w", "L1_xattn_b_in", "L1_xattn_g_ln",
                                    "L1_xattn_beta_ln", "L1_xattn_bp2")])
    A["bcv"] = np.broadcast_to(rows[None], (P, 7, D))
    A["cols"] = np.concatenate([column(I["L1_xattn_" + n], k) for n, k in
                                (("g1", 2), ("be1", 2), ("g2", 2), ("be2", 2), ("b1a", 4), ("b2a", 4), ("bp1", 3))], 1)
    A["alog"] = np.broadcast_to(I["L1_xattn_a"].reshape(1, 1), (P, 1))
    A["win"] = chunked(I["L1_xattn_W_in"])
    A["pet"] = I["L1_xattn_pe"].T
    A["wp1"] = I["L1_xattn_Wp1"]
    wp2 = I["L1_xattn_Wp2"]
    A["wp2"] = np.concatenate([wp2, np.zeros((64, D), wp2.dtype)]).reshape(3, P, D).transpose(1, 0, 2)
    A["wg0"] = chunked(I["L0_ffn_Wg"])
    A["wg1"] = chunked(np.concatenate([I["L1_ffn_w_router"], I["L1_ffn_w_gating"]], 1))
    sh = np.concatenate([chunked(I["L0_ffn_" + n]).reshape(P, BLK) for n in ("Ws1", "Ws3", "Ws2")], 1)[None]
    rt = [I["L0_ffn_" + n].reshape(16, 2, 2, P, P).transpose(0, 3, 2, 1, 4).reshape(16, P, BLK) for n in ("W1", "W3")]
    rt.append(I["L0_ffn_W2"].reshape(16, 2, P, D).transpose(0, 2, 1, 3).reshape(16, P, BLK))
    A["w0"] = np.concatenate([sh, np.concatenate(rt, 2)])
    ab = []
    for n in ("1", "2"):
        a = I[f"L1_xattn_W{n}a"].reshape(2, P, 2, D).transpose(2, 1, 0, 3).reshape(2, P, BLK)
        b = I[f"L1_xattn_W{n}b"].reshape(2, 2, P, D).transpose(0, 2, 1, 3).reshape(2, P, BLK)
        ab.append(np.concatenate([a, b], 2))
    A["wab"] = np.concatenate(ab)
    gu = [I["L1_ffn_" + n].reshape(E1, 2, P, 4, D).transpose(0, 3, 2, 1, 4).reshape(N_L1, P, BLK) for n in ("w_gate", "w_up")]
    gu.append(I["L1_ffn_w_down"].reshape(E1, 4, 2, P, D).transpose(0, 1, 3, 2, 4).reshape(N_L1, P, BLK))
    A["w1"] = np.concatenate(gu, 2)
    A = {k: np.ascontiguousarray(v) for k, v in A.items()}
    dram = {k: nc.dram_tensor("in_" + k, v.shape, mybir.dt.from_np(v.dtype), kind="ExternalInput").ap() for k, v in A.items()}
    out = nc.dram_tensor("out_0", (B, SEQ, D), F32, kind="ExternalOutput").ap()
    build(nc, dram, out)
    r = run(nc, [{"in_" + k: v for k, v in A.items()}], core_ids=[0])
    return r.results[0]["out_0"]
```

```python
import concourse.bass as bass
from concourse import mybir
from contextlib import ExitStack

F32 = mybir.dt.float32
F32R = mybir.dt.float32r
BF16 = mybir.dt.bfloat16
U32 = mybir.dt.uint32
I32 = mybir.dt.int32
ALU = mybir.AluOpType
ACT = mybir.ActivationFunctionType
AXX = mybir.AxisListType.X

P = 128
B, SEQ, D = 8, 256, 256
NT = B * SEQ // P
NH, DH = 8, 32
E0, TOPK = 32, 4
CAP = 4 * (B * SEQ * TOPK) // E0
E1 = 8
FT = 96
BLK = 512
UW = 3 * BLK
EPS = 1e-5
ARENA = 210000 // 64 * 64

U_FA, U_FB, U_L1 = 1, 3, 5
N_L1 = 32
TILES = B * SEQ * TOPK // P + E0
PAIRS = TILES // 2
EW = 3 * D
FAR = float(1 << 20)
PLAIN = 32
M_FA = 4
M_FB = M_FA + 8
M_L1 = M_FB + 8


def build(nc, dram, out_d):
    ctx = ExitStack()
    with ctx:
        base = (nc.sbuf_base + 63) // 64 * 64
        ctx.enter_context(nc.sbuf_tensor("arena", [P, ARENA], mybir.dt.uint8))
        top = [base]
        start, end = {}, {}

        def at(name, shape, dt=F32, off=None):
            n = 2 if dt == BF16 else 4
            for s in shape[1:]:
                n *= s
            n = (n + 63) // 64 * 64
            if off is None:
                off = top[0]
                top[0] += n
            start[name], end[name] = off, off + n
            return nc.alloc_sbuf_tensor_at(name, shape, dt, offset=off)

        x = at("x", [P, NT, D])
        dcw = at("dcw", [P, NT, D])
        ya = at("ya", [P, NT, D])
        xn = at("xn", [P, NT, D])
        xTH = at("xTH", [P, 2, NT * P], F32R)
        xTL = at("xTL", [P, 2, NT * P], F32R)
        wS = at("wS", [P, 2, UW])
        wH = at("wH", [P, 2, UW], F32R)
        wL = at("wL", [P, 2, UW], F32R)
        sg = at("sg", [P, 2, 512])
        hF = at("hF", [P, 2, 512])
        hH = at("hH", [P, 2, 512], F32R)
        hL = at("hL", [P, 2, 512], F32R)
        tF = at("tF", [P, 2, 512])
        ident = at("ident", [P, P])
        bcv = at("bcv", [P, 7, D])
        cols = at("cols", [P, 19])
        sc0 = at("sc0", [P, NT, E0])
        sc1 = at("sc1", [P, NT, E0])
        sc2 = at("sc2", [P, NT, E0])
        sc3 = at("sc3", [P, NT, E0])
        selm = at("selm", [P, NT, E0], BF16)
        cw2 = at("cw2", [P, NT, 16])
        st = at("st", [P, NT, 6])
        mv = at("mv", [P, NT, 2])
        ve = at("ve", [P, NT])
        sd = at("sd", [P, NT])
        rs = at("rs", [P, NT])
        nt1 = at("nt1", [P, NT])
        sm = at("sm", [P, NT, 2])
        sm2 = at("sm2", [P, NT])
        mx8 = at("mx8", [P, NT, 8])
        ix8 = at("ix8", [P, NT, 8], U32)
        ixf = at("ixf", [P, NT, 8])
        iot = at("iot", [P, E0])
        tilen = at("tilen", [P, TILES])
        rt = at("rt", [P, 4, E0])
        cmp8 = at("cmp8", [P, E0, 8])
        slk = at("slk", [P, NT, TOPK])
        okk = at("okk", [P, NT, TOPK])
        wk = at("wk", [P, NT, TOPK])
        idS = at("idS", [P, NT, TOPK], U32)
        idG = at("idG", [P, NT, TOPK], U32)
        etf = at("etf", [1, 2, TILES])
        wordf = at("wordf", [1, PAIRS + 2])
        words = at("words", [1, PAIRS + 2], I32)
        ptab = at("ptab", [1, E0], I32)
        zcol = at("zcol", [P, 1])
        tri = at("tri", [P, 2, P], BF16)
        wg0 = at("wg0", [P, 2, E0])
        wg0H = at("wg0H", [P, 2, E0], F32R)
        wg0L = at("wg0L", [P, 2, E0], F32R)
        wg1 = at("wg1", [P, 2, 16])
        wg1H = at("wg1H", [P, 2, 16], F32R)
        wg1L = at("wg1L", [P, 2, 16], F32R)
        vext = at("vext", [P, NT, NH, DH + 1])
        maskT = at("maskT", [P, 384], BF16)
        idb = at("idb", [P, P], BF16)
        gwt = at("gwt", [P, 6, 16])
        gbias = at("gbias", [P, 1])
        aT = at("aT", [P, 2, 64])
        eE = at("eE", [P, 2, 64])
        den = at("den", [P, 2, NH])
        mean = at("mean", [P, 2, 2, NH])
        var = at("var", [P, 2, NH])
        rstd = at("rstd", [P, 2, 2, NH])
        alog = at("alog", [P, 1])
        ea = at("ea", [P, 1])
        nl = at("nl", [P, 4])
        wnd = at("wnd", [P, 4])
        assert top[0] - base <= ARENA, top[0] - base
        sel = at("sel", [P, 64, P], F32R, start["dcw"])
        qT = at("qT", [P, 2, NT * P], F32, start["xTH"])
        kT = at("kT", [P, 2, NT * P], F32, start["xTL"])
        gateW = at("gateW", [P, 4, B, P], F32, start["wH"])
        cx = at("cx", [P, NT, D], F32, end["gateW"])
        Dm = at("Dm", [P, 2, 384], F32, end["cx"])
        Cm = at("Cm", [P, 2, 384], F32, end["Dm"])
        rg = at("rg", [P, 256], F32, start["sc0"])
        r1 = at("r1", [P, 256], F32, end["rg"])
        r2 = at("r2", [P, 256], F32, end["r1"])
        r3 = at("r3", [P, 256], F32, end["r2"])
        rF = at("rF", [P, 256], F32, end["r3"])
        rM = at("rM", [P, 256], F32, end["rF"])
        AE = at("AE", [P, 256], F32, end["rM"])
        ones = at("ones", [P, 256], F32, end["AE"])
        MHL = at("MHL", [P, 256], F32R, end["ones"])
        id2 = at("id2", [P, 64], F32, end["MHL"])
        hN = at("hN", [P, 2, 512], F32, start["xn"])
        hC = at("hC", [P, 2, 512], F32, end["hN"])
        hQ = at("hQ", [P, 2, 512], F32, end["hC"])
        hR = at("hR", [P, 2, 512], F32, end["hQ"])
        eS = wS[:, :, :].rearrange("p s c -> p (s c)")
        eH = wH[:, :, :].rearrange("p s c -> p (s c)")
        eL = wL[:, :, :].rearrange("p s c -> p (s c)")
        xl = at("xl", [P, 4, 2, D], F32, start["ya"])
        yo = at("yo", [P, 4, 2, D], F32, end["xl"])
        rhH = at("rhH", [P, 2, 2, P], F32R, start["sg"])
        rhL = at("rhL", [P, 2, 2, P], F32R, end["rhH"])
        rs_ = at("rs_", [P, 2, 2, P], F32, start["hF"])
        rh = at("rh", [P, 2, 2, P], F32, end["rs_"])
        cmpt = at("cmpt", [1, TILES, E0], F32, start["ya"])
        yg = at("yg", [P, 4, TOPK, D], F32, start["vext"])
        assert end["yg"] <= end["vext"]
        zn = at("zn", [P, B, 2, D], F32, start["xTH"])
        Zs = at("Zs", [P, 2, 4, 512], F32, start["xn"])
        FZ = at("FZ", [P, 4, FT], F32, start["wH"])
        FW = at("FW", [P, 4, 4, FT], F32, end["FZ"])
        GI = at("GI", [P, 4, D], F32, end["FW"])
        Win = at("Win", [P, 2, D], F32, end["GI"])
        peT = at("peT", [64, 512], F32, end["Win"])
        Wp1 = at("Wp1", [64, 320], F32, end["peT"])
        Wp2 = at("Wp2", [P, 3, D], F32, end["Wp1"])
        h1T = at("h1T", [P, 3, 512], F32, end["Wp2"])
        wf = at("wf", [P, 4, D], F32, end["h1T"])
        WF = at("WF", [P, 2, 4, D], F32, start["sc0"])
        PR = at("PR", [P, 2, 512], F32, start["vext"])
        PI = at("PI", [P, 2, 512], F32, end["PR"])
        tv = at("tv", [P, 2, 512], F32, end["PI"])
        tp = at("tp", [P, 2, 512], F32, end["tv"])
        assert end["Cm"] <= end["tF"] and end["wf"] <= start["Dm"] and end["id2"] <= end["cw2"]
        assert end["hR"] <= end["xn"] and end["WF"] <= end["cw2"] and end["tp"] <= end["vext"]

        ps = ctx.enter_context(nc.psum_tensor("ps", [P, 8, 512], F32))

        def sem(name):
            return ctx.enter_context(nc.semaphore(name))

        x_loaded = sem("x_loaded")
        ctx_loaded = sem("ctx_loaded")
        const_loaded = sem("const_loaded")
        conv_loaded = sem("conv_loaded")
        stage_loaded = [sem("stage0_loaded"), sem("stage1_loaded")]
        out_stored = sem("out_stored")
        var_done = sem("var_done")
        std_done = sem("std_done")
        norm_done = sem("norm_done")
        dve_step = sem("dve_step")
        pool_step = sem("pool_step")
        act_step = sem("act_step")
        gatew_done = sem("gatew_done")
        sel_done = sem("sel_done")
        vext_done = sem("vext_done")
        mixT_done = sem("mixT_done")
        mixT_copied = sem("mixT_copied")
        gates_done = sem("gates_done")
        gates_copied = sem("gates_copied")
        negabs_done = sem("negabs_done")
        softplus_done = sem("softplus_done")
        logf_done = sem("logf_done")
        logf_moved = sem("logf_moved")
        rows_done = sem("rows_done")
        rowsT_done = sem("rowsT_done")
        rowsT_copied = sem("rowsT_copied")
        qk_done = sem("qk_done")
        arg_done = sem("arg_done")
        decay_done = sem("decay_done")
        mixed_done = sem("mixed_done")
        pv_done = sem("pv_done")
        head_scaled = sem("head_scaled")
        head_centred = sem("head_centred")
        head_squared = sem("head_squared")
        head_var = sem("head_var")
        head_rstd = sem("head_rstd")
        head_added = sem("head_added")
        pos1_done = sem("pos1_done")
        pos1_silu = sem("pos1_silu")
        window_done = sem("window_done")
        pos2_done = sem("pos2_done")
        filt_done = sem("filt_done")
        filtF_done = sem("filtF_done")
        filtF_copied = sem("filtF_copied")
        zlin_done = sem("zlin_done")
        zlin_copied = sem("zlin_copied")
        zaff_dve = sem("zaff_dve")
        zF_done = sem("zF_done")
        zF_copied = sem("zF_copied")
        prod_re = sem("prod_re")
        prod_im = sem("prod_im")
        inv_done = sem("inv_done")
        inv_copied = sem("inv_copied")
        xT_done = sem("xT_done")
        xT_copied = sem("xT_copied")
        xT_high = sem("xT_high")
        xT_low = sem("xT_low")
        gate_split = sem("gate_split")
        logits_done = sem("logits_done")
        shifted_done = sem("shifted_done")
        exp_done = sem("exp_done")
        chosen_done = sem("chosen_done")
        counts_done = sem("counts_done")
        cw_done = sem("cw_done")
        xs_d = nc.dram_tensor("slots_in", (TILES * P, D), F32, kind="Internal").ap()
        ys_d = nc.dram_tensor("slots_out", (TILES * P, D), F32, kind="Internal").ap()
        counts_read = sem("counts_read")
        slots_done = sem("slots_done")
        table_done = sem("table_done")
        zero_done = sem("zero_done")
        zeros_stored = sem("zeros_stored")
        scattered = sem("scattered")
        estage_loaded = [sem(f"estage{i}_loaded") for i in range(4)]
        ew_high = sem("ew_high")
        ew_ready = sem("ew_ready")
        tile_loaded = [sem(f"tile{i}_loaded") for i in range(4)]
        tile_stored = [sem(f"tile{i}_stored") for i in range(4)]
        tT_done = sem("tT_done")
        tT_high = sem("tT_high")
        tT_low = sem("tT_low")
        tU_done = sem("tU_done")
        tS_done = sem("tS_done")
        tM_done = sem("tM_done")
        tHT_done = sem("tHT_done")
        tH_high = sem("tH_high")
        tH_low = sem("tH_low")
        tY_done = sem("tY_done")
        tile_done = sem("tile_done")
        gathered = [sem(f"gathered{i}") for i in range(4)]
        combined = sem("combined")
        w_high = sem("w_high")
        w_low = sem("w_low")
        up_done = sem("up_done")
        silu_done = sem("silu_done")
        mul_done = sem("mul_done")
        h_high = sem("h_high")
        h_low = sem("h_low")
        down_done = sem("down_done")
        evac_done = sem("evac_done")

        block = ctx.enter_context(nc.Block())

        def wait(eng, s, value):
            if not (isinstance(value, int) and value <= 0):
                eng.wait_ge(s, value)

        def pairs_done(k):
            return 0 if isinstance(k, int) and k <= 0 else k * 2 + 1

        def f32(ap):
            return ap.bitcast(F32)

        def blocks(t, slot, plain):
            v = t[:, slot, :].rearrange("p (a c) -> p a c", c=BLK)
            return v[:, 0:3:2, :] if plain else v

        @block.sync
        def _(sp):
            xv = dram["x"].rearrange("b (h p) d -> p (b h) d", p=P)
            cv = dram["ctx"].rearrange("b (h p) d -> p (b h) d", p=P)
            sp.dma_start(ident[:, :], dram["ident"]).then_inc(const_loaded, 16)
            sp.dma_start(x[:, :, :], xv).then_inc(x_loaded, 16)
            sp.dma_start(cx[:, :, :], cv).then_inc(ctx_loaded, 16)
            for t, n in ((gwt, "gw"), (gbias, "gbias"), (maskT, "maskT"), (bcv, "bcv"), (cols, "cols"), (iot, "iot"), (tilen, "tilen"),
                         (tri, "tri"), (wg0, "wg0"), (wg1, "wg1"), (alog, "alog"), (nl, "nl")):
                sp.dma_start(t[tuple(slice(None) for _ in t.shape)], dram[n]).then_inc(const_loaded, 16)

            def load(u, slot, src, plain=False):
                wait(sp, w_low, u - 1)
                sp.dma_start(blocks(wS, slot, plain), src.rearrange("p (a c) -> p a c", c=BLK)).then_inc(stage_loaded[slot], 16)

            load(0, 0, dram["w0"][0])
            sp.wait_ge(zero_done, 1)
            zv = xs_d.rearrange("(a p c) d -> a p (c d)", p=P, c=UW // D)
            for a in range(TILES * D // UW):
                sp.dma_start(zv[a], wS[:, 1, :]).then_inc(zeros_stored, 16)
            sp.wait_ge(gates_done, 1)
            sp.wait_ge(vext_done, 1)
            for t, n in ((FZ, "fz"), (FW, "fw"), (GI, "gi"), (Win, "win"), (peT, "pet"), (Wp1, "wp1"), (Wp2, "wp2")):
                sp.dma_start(t[tuple(slice(None) for _ in t.shape)], dram[n]).then_inc(conv_loaded, 16)
            sp.wait_ge(zeros_stored, 16 * (TILES * D // UW))

            def load_expert(e, slot, ready):
                if isinstance(e, int) and e == 2:
                    sp.wait_ge(w_low, 1)
                if ready is not None:
                    sp.wait_ge(ew_ready, ready)
                src = dram["wr"][e] if isinstance(e, int) else dram["wr"][bass.ds(e, 1)].rearrange("a p c -> (a p) c")
                sp.dma_start(eS[:, slot * EW:(slot + 1) * EW], src).then_inc(estage_loaded[slot], 16)

            for e in range(4):
                load_expert(e, (e + 2) % 4, None)
            with sp.Fori(1, E0 // 4) as it:
                for e in range(4):
                    load_expert(it * 4 + e, (e + 2) % 4, it * 4 + (e - 3))
            sp.wait_ge(ew_ready, E0)
            for i in range(4):
                load(U_FA + i, (U_FA + i) % 2, dram["wab"][i], plain=True)
            with sp.Fori(0, N_L1 // 2) as it:
                load(it * 2 + U_L1, 1, dram["w1"][bass.ds(it * 2, 1)].rearrange("a p c -> (a p) c"))
                load(it * 2 + U_L1 + 1, 0, dram["w1"][bass.ds(it * 2 + 1, 1)].rearrange("a p c -> (a p) c"))
            ov = out_d.rearrange("b (h p) d -> p (b h) d", p=P)
            for g in range(4):
                sp.wait_ge(evac_done, 4 * (M_L1 + 4 * N_L1) - 16 + 4 * (g + 1))
                sp.dma_start(ov[:, 4 * g:4 * g + 4, :], x[:, 4 * g:4 * g + 4, :]).then_inc(out_stored, 16)
            sp.wait_ge(out_stored, 64)

        @block.vector
        def _(dve):
            steps = [0]

            def link(ins):
                steps[0] += 1
                ins.then_inc(dve_step, 1)
                dve.wait_ge(dve_step, steps[0])

            lns = [0]

            def layernorm(src, dst, signal):
                for n in range(NT):
                    last = dve.bn_stats(st[:, n, :], src[:, n, :])
                link(last)
                for n in range(NT):
                    last = dve.bn_aggr(mv[:, n, :], st[:, n, :])
                link(last)
                dve.tensor_scalar(ve[:, :], mv[:, :, 1], EPS, None, ALU.add).then_inc(var_done, 1)
                lns[0] += 1
                dve.wait_ge(std_done, lns[0])
                link(dve.reciprocal(rs[:, :], sd[:, :]))
                link(dve.tensor_tensor(nt1[:, :], rs[:, :], rs[:, :], ALU.mult))
                link(dve.tensor_tensor(nt1[:, :], nt1[:, :], ve[:, :], ALU.mult))
                link(dve.tensor_scalar(nt1[:, :], nt1[:, :], -0.5, 1.5, ALU.mult, ALU.add))
                link(dve.tensor_tensor(rs[:, :], rs[:, :], nt1[:, :], ALU.mult))
                for n in range(NT):
                    last = dve.tensor_scalar(dst[:, n, :], src[:, n, :], mv[:, n, 0:1], rs[:, n:n + 1],
                                             ALU.subtract, ALU.mult)
                    if signal:
                        last.then_inc(norm_done, 1)
                if not signal:
                    link(last)

            def layernorm_group(src, dst, g, signal):
                tiles = range(4 * g, 4 * g + 4)
                r = slice(4 * g, 4 * g + 4)
                for n in tiles:
                    last = dve.bn_stats(st[:, n, :], src[:, n, :])
                link(last)
                for n in tiles:
                    last = dve.bn_aggr(mv[:, n, :], st[:, n, :])
                link(last)
                dve.tensor_scalar(ve[:, r], mv[:, r, 1], EPS, None, ALU.add).then_inc(var_done, 1)
                lns[0] += 1
                dve.wait_ge(std_done, lns[0])
                link(dve.reciprocal(rs[:, r], sd[:, r]))
                link(dve.tensor_tensor(nt1[:, r], rs[:, r], rs[:, r], ALU.mult))
                link(dve.tensor_tensor(nt1[:, r], nt1[:, r], ve[:, r], ALU.mult))
                link(dve.tensor_scalar(nt1[:, r], nt1[:, r], -0.5, 1.5, ALU.mult, ALU.add))
                link(dve.tensor_tensor(rs[:, r], rs[:, r], nt1[:, r], ALU.mult))
                for n in tiles:
                    last = dve.tensor_scalar(dst[:, n, :], src[:, n, :], mv[:, n, 0:1], rs[:, n:n + 1], ALU.subtract, ALU.mult)
                    if signal:
                        last.then_inc(norm_done, 1)
                if not signal:
                    link(last)

            dve.wait_ge(x_loaded, 16)
            layernorm(x, xn, True)
            dve.memset(ones[:, :], 1.0)
            dve.wait_ge(gates_copied, 1)
            dve.scalar_tensor_tensor(r1[64:, :], rg[64:, :], -1.0, rg[64:, :], ALU.mult, ALU.min).then_inc(negabs_done, 1)
            dve.wait_ge(softplus_done, 2)
            link(dve.scalar_tensor_tensor(r1[64:, :], rg[64:, :], 0.0, r3[64:, :], ALU.min, ALU.subtract))
            dve.tensor_tensor_scan(rF[64:, :], ones[64:, :], r1[64:, :], 0.0, ALU.mult, ALU.add).then_inc(logf_done, 1)
            dve.wait_ge(logf_moved, 1)
            link(dve.tensor_tensor(AE[0:64, :], rg[0:64, :], rF[0:64, :], ALU.subtract))
            link(dve.tensor_tensor_scan(rM[0:64, :], AE[0:64, :], AE[0:64, :], -3.0e38, ALU.max, ALU.max))
            link(dve.tensor_tensor(r3[0:64, :], rF[0:64, :], rM[0:64, :], ALU.add))
            dve.tensor_scalar(AE[64:, :], r3[0:64, :], -1.0, None, ALU.mult)
            link(dve.tensor_scalar(r1[0:64, :], rM[0:64, :], -1.0, None, ALU.mult))
            link(dve.tensor_copy(MHL[0:64, :], r1[0:64, :]))
            link(dve.tensor_tensor(r2[0:64, :], r1[0:64, :], f32(MHL[0:64, :]), ALU.subtract))
            dve.tensor_copy(MHL[64:, :], r2[0:64, :]).then_inc(rows_done, 1)

            def head_scale(b):
                o = ps[:, 4 + 2 * (b % 2):6 + 2 * (b % 2), 0:NH * (DH + 1)].rearrange("p s (h d) -> p s h d", h=NH)
                v = hN[:, b % 2, :].rearrange("p (s h d) -> p s h d", s=2, h=NH)
                dve.wait_ge(pv_done, 8 * (b + 1))
                wait(dve, head_centred, b - 1)
                link(dve.tensor_copy(den[:, :, :], o[:, :, :, DH]))
                link(dve.scalar_tensor_tensor(den[:, :, :], den[:, :, :], -1.0, den[:, :, :], ALU.mult, ALU.max))
                link(dve.tensor_tensor(den[:, :, :], den[:, :, :], eE[:, :, 8 * b:8 * b + 8], ALU.max))
                link(dve.tensor_scalar(den[:, :, :], den[:, :, :], 1e-6, None, ALU.add))
                link(dve.reciprocal(den[:, :, :], den[:, :, :]))
                link(dve.tensor_tensor(v, o[:, :, :, 0:DH], den[:, :, :].unsqueeze(3).to_broadcast([P, 2, NH, DH]), ALU.mult))
                link(dve.tensor_reduce(mean[:, b % 2, :, :], v, AXX, ALU.add))
                dve.tensor_scalar(mean[:, b % 2, :, :], mean[:, b % 2, :, :], 1.0 / DH, None, ALU.mult).then_inc(head_scaled, 1)

            def head_variance(b):
                q = hQ[:, b % 2, :].rearrange("p (s h d) -> p s h d", s=2, h=NH)
                dve.wait_ge(head_squared, b + 1)
                wait(dve, head_rstd, 2 * b)
                link(dve.tensor_reduce(var[:, :, :], q, AXX, ALU.add))
                dve.tensor_scalar(var[:, :, :], var[:, :, :], 1.0 / DH, EPS, ALU.mult, ALU.add).then_inc(head_var, 1)

            for i in range(B * NH):
                dve.wait_ge(qk_done, i + 1)
                dve.wait_ge(decay_done, i + 1)
                wait(dve, pv_done, i - 1)
                dve.scalar_tensor_tensor(Cm[:, i % 2, :], ps[:, i % 2, 0:384], float(DH) ** -0.5, Dm[:, i % 2, :],
                                         ALU.mult, ALU.mult).then_inc(mixed_done, 1)
                if i >= 8 and i % 8 == 1:
                    head_scale(i // 8 - 1)
                if i >= 8 and i % 8 == 5:
                    head_variance(i // 8 - 1)
            head_scale(B - 1)
            head_variance(B - 1)

            dve.wait_ge(const_loaded, 13 * 16)
            dve.wait_ge(window_done, 3)
            dve.wait_ge(pos2_done, 1)
            p2 = ps[:, 4:6, :].rearrange("p a (c d) -> p (a c) d", d=D)
            link(dve.tensor_tensor(wf[:, :, :], p2, bcv[:, 6:7, :].to_broadcast([P, 4, D]), ALU.add))
            for k in range(4):
                last = dve.tensor_scalar(wf[:, k, :], wf[:, k, :], wnd[:, k:k + 1], None, ALU.mult)
            last.then_inc(filt_done, 1)
            for b in range(B):
                dve.wait_ge(zlin_done, b + 1)
                last = dve.tensor_tensor(zn[:, b, :, :], ps[:, b, :].rearrange("p (r d) -> p r d", r=2),
                                         bcv[:, 3:4, :].to_broadcast([P, 2, D]), ALU.add)
                last.then_inc(zlin_copied, 1)
            dve.wait_ge(zlin_copied, B)
            zt = zn[:, :, :, :].rearrange("p b r d -> p (b r) d")
            layernorm(zt, zt, False)
            for g in range(4):
                v = zt[:, 4 * g:4 * g + 4, :]
                link(dve.tensor_tensor(v, v, bcv[:, 4:5, :].to_broadcast([P, 4, D]), ALU.mult))
                dve.tensor_tensor(v, v, bcv[:, 5:6, :].to_broadcast([P, 4, D]), ALU.add).then_inc(zaff_dve, 1)

            dve.wait_ge(filtF_copied, 1)
            dve.wait_ge(head_added, B)

            def spectrum(eng, t, out, mine, a, linker, signal):
                for q in range(4):
                    for fh in range(2):
                        n = 2 * q + fh
                        eng.wait_ge(zF_copied, n + 1)
                        wait(eng, inv_done, n - 1)
                        z = Zs[0:FT, n % 2, :, :].rearrange("p a (b d) -> p a b d", b=2)
                        o = out[0:FT, n % 2, :].rearrange("p (b d) -> p b d", b=2)
                        tt = [t[0:FT, s, :].rearrange("p (b d) -> p b d", b=2) for s in range(2)]
                        for s, (zi, wi, op) in enumerate(a):
                            w = WF[0:FT, s // 2, 2 * wi + fh:2 * wi + fh + 1, :].to_broadcast([FT, 2, D])
                            dst = o if s == 0 else tt[s % 2]
                            linker(eng.tensor_tensor(dst, z[:, 2 * (s // 2) + zi], w, ALU.mult))
                            if s:
                                last = eng.tensor_tensor(o, o, dst, op)
                                if s < 3:
                                    linker(last)
                        last.then_inc(signal, 1)

            spectrum(dve, tv, PR, 0, ((0, 0, None), (1, 1, ALU.subtract), (0, 0, ALU.add), (1, 1, ALU.subtract)), link, prod_re)

            def split_gates():
                link(dve.tensor_copy(wg0H[:, :, :], wg0[:, :, :]))
                link(dve.tensor_tensor(wg0L[:, :, :], wg0[:, :, :], f32(wg0H[:, :, :]), ALU.subtract))
                link(dve.tensor_copy(wg1H[:, :, :], wg1[:, :, :]))
                dve.tensor_tensor(wg1L[:, :, :], wg1[:, :, :], f32(wg1H[:, :, :]), ALU.subtract).then_inc(gate_split, 1)

            def high_parts(r, groups=range(4)):
                for j in range(2 * groups[0], 2 * groups[-1] + 2):
                    g, c = j // 2, j % 2
                    dve.wait_ge(xT_copied, 8 * r + j + 1)
                    dve.tensor_copy(xTH[:, c, g * 512:(g + 1) * 512], tF[:, j % 2, :]).then_inc(xT_high, 1)

            def step(n, b, muls):
                if muls is not None:
                    wait(dve, h_low, n - 1)
                    dve.wait_ge(silu_done, n + 1)
                    dve.tensor_tensor(hF[:, b, :], sg[:, b, :], ps[:, 2 + b, :], ALU.mult).then_inc(mul_done, 1)
                    dve.wait_ge(mul_done, n + 1 - muls)
                else:
                    dve.wait_ge(silu_done, n + 1)
                wait(dve, down_done, n - 1)
                dve.tensor_copy(hH[:, b, :], hF[:, b, :]).then_inc(h_high, 1)

            def evacuate(m, n, g, pair, dst, scale):
                dve.wait_ge(down_done, n + 1)
                wait(dve, evac_done, m * 4)
                for t in range(4):
                    tile = 4 * g + t
                    acc = ps[:, 4 + 2 * pair + t // 2, (t % 2) * 256:(t % 2) * 256 + 256]
                    if scale is None:
                        last = dve.tensor_tensor(dst[:, tile, :], acc, dst[:, tile, :], ALU.add)
                    else:
                        last = dve.scalar_tensor_tensor(dst[:, tile, :], acc, scale(tile), dst[:, tile, :], ALU.mult, ALU.add)
                    last.then_inc(evac_done, 1)

            dve.wait_ge(inv_copied, 8)
            layernorm(x, xn, True)
            split_gates()
            high_parts(0)
            lg = ps[:, 7, :].rearrange("p (n e) -> p n e", n=NT)
            m1 = sm[:, :, 0]

            def bc(ap, k):
                return ap.unsqueeze(2).to_broadcast([P, NT, k])

            dve.wait_ge(logits_done, 1)
            link(dve.tensor_reduce(m1, lg, AXX, ALU.max))
            dve.tensor_tensor(sc0[:, :, :], lg, bc(m1, E0), ALU.subtract).then_inc(shifted_done, 1)
            dve.wait_ge(exp_done, 1)
            link(dve.tensor_reduce(m1, sc0[:, :, :], AXX, ALU.add))
            link(dve.reciprocal(m1, m1))
            link(dve.tensor_tensor(sc0[:, :, :], sc0[:, :, :], bc(m1, E0), ALU.mult))
            for n in range(NT):
                last = dve.max(mx8[:, n, :], sc0[:, n, :])
            link(last)
            for n in range(NT):
                last = dve.max_index(ix8[:, n, :], mx8[:, n, :], sc0[:, n, :])
            link(last)
            link(dve.tensor_copy(ixf[:, :, :], ix8[:, :, :]))
            io = iot[:, :].unsqueeze(1).to_broadcast([P, NT, E0])
            link(dve.tensor_tensor(sc1[:, :, :], io, bc(ixf[:, :, 0], E0), ALU.is_equal))
            for k in range(1, TOPK):
                link(dve.tensor_tensor(sc2[:, :, :], io, bc(ixf[:, :, k], E0), ALU.is_equal))
                link(dve.tensor_tensor(sc1[:, :, :], sc1[:, :, :], sc2[:, :, :], ALU.add))
            dve.tensor_copy(selm[:, :, :], sc1[:, :, :]).then_inc(chosen_done, 1)
            dve.wait_ge(counts_done, 1)
            link(dve.memset(sc2[:, 0, :], 0.0))
            tot = ps[:, 5, :].rearrange("p (n e) -> p n e", n=NT)
            for n in range(1, NT):
                link(dve.tensor_tensor(sc2[:, n, :], sc2[:, n - 1, :], tot[:, n - 1, :], ALU.add))
            link(dve.tensor_tensor(rt[:, 0, :], sc2[:, NT - 1, :], tot[:, NT - 1, :], ALU.add))
            dve.tensor_tensor(sc2[:, :, :], ps[:, 6, :].rearrange("p (n e) -> p n e", n=NT), sc2[:, :, :], ALU.add).then_inc(counts_read, 1)
            dve.wait_ge(counts_read, 1)
            link(dve.tensor_scalar(rt[:, 0, :], rt[:, 0, :], float(CAP), None, ALU.min))
            link(dve.tensor_scalar(cmp8[:, 0, :], tilen[:, 0:8], float(P), None, ALU.mult))
            link(dve.tensor_copy(cmp8[:, 1:E0, :], cmp8[:, 0:1, :].to_broadcast([P, E0 - 1, 8])))
            link(dve.tensor_tensor(cmp8[:, :, :], rt[:, 0, :].unsqueeze(2).to_broadcast([P, E0, 8]), cmp8[:, :, :], ALU.is_gt))
            link(dve.tensor_reduce(rt[:, 1, :], cmp8[:, :, :], AXX, ALU.add))
            link(dve.memset(rt[:, 0, :], 1.0))
            link(dve.tensor_tensor_scan(rt[:, 2, :], rt[:, 0, :], rt[:, 1, :], 0.0, ALU.mult, ALU.add))
            link(dve.tensor_tensor(rt[:, 3, :], rt[:, 2, :], rt[:, 1, :], ALU.subtract))
            link(dve.tensor_scalar(rt[:, 3, :], rt[:, 3, :], float(P), None, ALU.mult))
            link(dve.tensor_scalar(sc3[:, :, :], sc2[:, :, :], float(CAP), FAR, ALU.is_ge, ALU.mult))
            link(dve.tensor_tensor(sc2[:, :, :], sc2[:, :, :], sc3[:, :, :], ALU.add))
            link(dve.tensor_tensor(sc2[:, :, :], sc2[:, :, :], rt[:, 3:4, :].to_broadcast([P, NT, E0]), ALU.add))
            for k in range(TOPK):
                link(dve.tensor_tensor(sc1[:, :, :], io, bc(ixf[:, :, k], E0), ALU.is_equal))
                link(dve.tensor_tensor(sc1[:, :, :], sc1[:, :, :], sc2[:, :, :], ALU.mult))
                link(dve.tensor_reduce(slk[:, :, k], sc1[:, :, :], AXX, ALU.add))
            link(dve.tensor_scalar(okk[:, :, :], slk[:, :, :], 0.5 * FAR, None, ALU.is_lt))
            dve.tensor_copy(idS[:, :, :], slk[:, :, :]).then_inc(slots_done, 1)
            dve.tensor_tensor(wk[:, :, :], mx8[:, :, 0:TOPK], okk[:, :, :], ALU.mult)
            link(dve.tensor_tensor(slk[:, :, :], slk[:, :, :], okk[:, :, :], ALU.mult))
            dve.tensor_copy(idG[:, :, :], slk[:, :, :]).then_inc(slots_done, 1)
            link(dve.tensor_tensor(cmpt[:, :, :], rt[0:1, 2:3, :].to_broadcast([1, TILES, E0]),
                                   tilen[0:1, :].unsqueeze(2).to_broadcast([1, TILES, E0]), ALU.is_le))
            link(dve.tensor_reduce(etf[:, 0, :], cmpt[:, :, :], AXX, ALU.add))
            link(dve.tensor_scalar(etf[:, 0, :], etf[:, 0, :], float(E0 - 1), None, ALU.min))
            quads = cmpt[:, :, 0:8]
            link(dve.tensor_scalar(rt[0:1, 0, 0:8], tilen[0:1, 0:8], 4.0, 2.0, ALU.mult, ALU.add))
            link(dve.tensor_tensor(quads, etf[:, 0, :].unsqueeze(2).to_broadcast([1, TILES, 8]),
                                   rt[0:1, 0:1, 0:8].to_broadcast([1, TILES, 8]), ALU.is_ge))
            link(dve.tensor_reduce(etf[:, 1, :], quads, AXX, ALU.add))
            link(dve.scalar_tensor_tensor(etf[:, 1, :], etf[:, 1, :], -4.0, etf[:, 0, :], ALU.mult, ALU.add))
            link(dve.tensor_scalar(etf[:, 1, :], etf[:, 1, :], 2.0, None, ALU.add))
            link(dve.scalar_tensor_tensor(etf[:, 1, 0:PAIRS], etf[:, 1, 1::2], 16.0, etf[:, 1, 0::2], ALU.mult, ALU.add))
            link(dve.tensor_scalar(etf[:, 1, 0:PAIRS], etf[:, 1, 0:PAIRS], float(EW // D * 256), None, ALU.mult))
            link(dve.tensor_scalar(wordf[:, 0:PAIRS], etf[:, 0, 1::2], 1.0, None, ALU.add))
            link(dve.memset(wordf[:, PAIRS:], 0.0))
            link(dve.tensor_tensor(wordf[:, 0:PAIRS], wordf[:, 0:PAIRS], etf[:, 1, 0:PAIRS], ALU.add))
            link(dve.scalar_tensor_tensor(wordf[:, 2:], etf[:, 1, 0:PAIRS], 256.0, wordf[:, 2:], ALU.mult, ALU.add))
            link(dve.tensor_scalar(rt[0:1, 3, :], rt[0:1, 2, :], 1.0, None, ALU.add))
            dve.tensor_copy(ptab[:, :], rt[0:1, 3, :])
            dve.tensor_copy(words[:, :], wordf[:, :]).then_inc(table_done, 1)

            for i in range(8):
                step(i, i % 2, 0)
                if i in (2, 4, 6):
                    evacuate(i // 2 - 1, i - 1, i // 2 - 1, (i // 2 - 1) % 2, x, None)
            evacuate(3, 7, 3, 1, x, None)
            dve.wait_ge(evac_done, 4 * M_FA)

            def tile_low(q, b):
                dve.wait_ge(tT_high, q + 1)
                wait(dve, tU_done, q - 1)
                dve.tensor_tensor(hL[:, b, :], ps[:, b, :], f32(hH[:, b, :]), ALU.subtract).then_inc(tT_low, 1)

            def tile_mul(q, b):
                dve.wait_ge(tS_done, q + 1)
                wait(dve, tHT_done, q - 1)
                dve.tensor_tensor(rh[:, b, :, :], rs_[:, b, :, :], ps[:, 2 + b, :].rearrange("p (t c) -> p t c", t=2)[:, :, P:],
                                  ALU.mult).then_inc(tM_done, 1)

            def hidden_low(q, b):
                dve.wait_ge(tH_high, q + 1)
                wait(dve, tile_done, pairs_done(q - 1))
                dve.tensor_tensor(rhL[:, b, :, :], ps[:, 4 + b, 0:D].rearrange("p (t c) -> p t c", t=2), f32(rhH[:, b, :, :]),
                                  ALU.subtract).then_inc(tH_low, 1)

            def tile_out(q, b, ring, stored):
                dve.wait_ge(tile_done, pairs_done(q + 1))
                if stored is not None:
                    dve.wait_ge(tile_stored[ring], stored)
                dve.tensor_copy(yo[:, ring, :, :], ps[:, 6 + b, :].rearrange("p (t d) -> p t d", t=2)).then_inc(tY_done, 1)

            tile_low(0, 0)
            tile_low(1, 1)
            tile_mul(0, 0)

            def body(it, first=False, last=False):
                for j in range(4):
                    q = it * 4 + j
                    if not (last and j >= 2):
                        tile_low(q + 2, j % 2)
                    if not (last and j == 3):
                        tile_mul(q + 1, (j + 1) % 2)
                    hidden_low(q, j % 2)
                    if not (first and j == 0):
                        ring = (j + 3) % 4
                        filled = it if j else it - 1
                        tile_out(q - 1, (j + 1) % 2, ring, None if first or (isinstance(filled, int) and filled < 1) else filled * 16)

            body(0, first=True)
            body(1)
            with dve.Fori(2, PAIRS // 4 - 1) as it:
                body(it)
            body(PAIRS // 4 - 1, last=True)
            tile_out(PAIRS - 1, 1, 3, (PAIRS // 4 - 1) * 16)
            for n in range(NT):
                dve.wait_ge(gathered[n % 4], 64 * (n // 4 + 1))
                for k in range(TOPK):
                    last = dve.scalar_tensor_tensor(x[:, n, :], yg[:, n % 4, k, :], wk[:, n, k:k + 1], x[:, n, :], ALU.mult, ALU.add)
                    if k < TOPK - 1:
                        link(last)
                last.then_inc(combined, 1)
                if n % 4 == 3:
                    g = n // 4
                    dve.wait_ge(combined, n + 1)
                    layernorm_group(x, ya, g, False)
                    layernorm_group(ya, xn, g, True)
                    dve.wait_ge(norm_done, 2 * NT + 4 * g + 4)
                    t = ya[:, 4 * g:4 * g + 4, :]
                    link(dve.tensor_tensor(t, t, bcv[:, 0:1, :].to_broadcast([P, 4, D]), ALU.add))
                    if g:
                        high_parts(1, [g - 1])
            high_parts(1, [3])

            def dense(u0, m0):
                for i in range(16):
                    step(8 * u0 + i, i % 2, None)
                    if i % 2 == 0 and i:
                        g = i // 2 - 1
                        evacuate(m0 + g, 8 * u0 + i - 1, g % 4, g % 2, ya, None)
                evacuate(m0 + 7, 8 * u0 + 15, 3, 1, ya, None)

            dense(U_FA, M_FA)
            dve.wait_ge(evac_done, 4 * M_FB)
            link(dve.tensor_tensor(ya[:, :, :], ya[:, :, :], dcw[:, :, :], ALU.mult))
            layernorm(ya, xn, True)
            dve.wait_ge(norm_done, 4 * NT)
            link(dve.tensor_tensor(ya[:, :, :], ya[:, :, :], bcv[:, 1:2, :].to_broadcast([P, NT, D]), ALU.add))
            high_parts(2)
            dense(U_FB, M_FB)
            dve.wait_ge(evac_done, 4 * M_L1)
            link(dve.tensor_tensor(x[:, :, :], x[:, :, :], ya[:, :, :], ALU.add))

            layernorm(x, xn, True)
            high_parts(3)
            l1 = ps[:, 7, 0:NT * 16].rearrange("p (n a e) -> p n a e", n=NT, a=2)
            s1 = sc0[:, :, 0:16].rearrange("p n (a e) -> p n a e", a=2)
            smb = sm[:, :, :].unsqueeze(3).to_broadcast([P, NT, 2, E1])
            dve.wait_ge(logits_done, 2)
            link(dve.tensor_reduce(sm[:, :, :], l1, AXX, ALU.max))
            link(dve.tensor_tensor(s1, l1, smb, ALU.subtract))
            dve.tensor_scalar(s1[:, :, 1, :], s1[:, :, 1, :], 10.0, None, ALU.mult).then_inc(shifted_done, 1)
            dve.wait_ge(exp_done, 2)
            link(dve.tensor_reduce(sm[:, :, :], s1, AXX, ALU.add))
            link(dve.reciprocal(sm[:, :, :], sm[:, :, :]))
            link(dve.tensor_tensor(s1, s1, smb, ALU.mult))
            link(dve.tensor_tensor(sc1[:, :, 0:8], s1[:, :, 0, :], s1[:, :, 1, :], ALU.mult))
            link(dve.tensor_reduce(sm2[:, :], sc1[:, :, 0:8], AXX, ALU.add))
            link(dve.tensor_scalar(sm2[:, :], sm2[:, :], 1e-9, None, ALU.add))
            link(dve.reciprocal(sm2[:, :], sm2[:, :]))
            for a in range(2):
                last = dve.tensor_tensor(cw2[:, :, a:16:2], sc1[:, :, 0:8], bc(sm2[:, :], E1), ALU.mult)
            last.then_inc(cw_done, 1)
            dve.wait_ge(cw_done, 1)
            with dve.Fori(0, N_L1 // 2) as it:
                def mixed(local):
                    evacuate(it * 8 + (M_L1 + local // 2), it * 16 + (8 * U_L1 + local), local // 2 % 4, local // 2 % 2, x,
                             lambda tile: cw2[:, tile, bass.ds(it, 1)])
                for local in range(16):
                    step(it * 16 + (8 * U_L1 + local), local % 2, PLAIN)
                    if local and local % 2 == 0:
                        mixed(local - 1)
                mixed(15)

        @block.scalar
        def _(act):
            lns = [0]

            def deviation():
                lns[0] += 1
                act.wait_ge(var_done, lns[0])
                act.activation(sd[:, :], ve[:, :], ACT.Sqrt).then_inc(std_done, 1)

            def deviation_group(g):
                lns[0] += 1
                act.wait_ge(var_done, lns[0])
                act.activation(sd[:, 4 * g:4 * g + 4], ve[:, 4 * g:4 * g + 4], ACT.Sqrt).then_inc(std_done, 1)

            def mix_copy(j, dst):
                act.wait_ge(mixT_done, j + 1)
                act.activation(dst, ps[:, j % 4, :], ACT.Identity).then_inc(mixT_copied, 1)

            for j in range(8):
                mix_copy(j, kT[:, j % 2, (j // 2) * 512:(j // 2 + 1) * 512])
            deviation()
            for j in range(8):
                mix_copy(8 + j, qT[:, j % 2, (j // 2) * 512:(j // 2 + 1) * 512])
            act.wait_ge(gates_done, 1)
            act.wait_ge(const_loaded, 13 * 16)
            act.activation(rg[:, :], ps[:, 4, 0:256], ACT.Identity, bias=gbias[:, :]).then_inc(gates_copied, 1)
            act.wait_ge(negabs_done, 1)
            act.activation(r2[64:, :], r1[64:, :], ACT.Exp).then_inc(softplus_done, 1)
            act.wait_ge(softplus_done, 1)
            act.activation(r3[64:, :], r2[64:, :], ACT.Ln, bias=1.0).then_inc(softplus_done, 1)
            act.wait_ge(logf_done, 1)
            act.activation(rF[0:64, :], rF[64:, :], ACT.Copy).then_inc(logf_moved, 1)
            act.wait_ge(rowsT_done, 1)
            rT = ps[:, 5, 0:256].rearrange("p (h r) -> p h r", h=2)
            act.activation(aT[:, :, :], rT[:, :, 0:64], ACT.Copy)
            act.activation(eE[:, :, :], rT[:, :, 64:128], ACT.Exp).then_inc(rowsT_copied, 1)
            act.wait_ge(rowsT_copied, 1)

            def square(b):
                act.wait_ge(head_centred, b + 1)
                wait(act, head_var, b - 1)
                act.activation(hQ[:, b % 2, :], hC[:, b % 2, :], ACT.Square).then_inc(head_squared, 1)

            def inverse_deviation(b):
                act.wait_ge(head_var, b + 1)
                wait(act, head_added, b - 1)
                act.activation(rstd[:, b % 2, :, :], var[:, :, :], ACT.Ln).then_inc(head_rstd, 1)
                act.wait_ge(head_rstd, 2 * b + 1)
                act.activation(rstd[:, b % 2, :, :], rstd[:, b % 2, :, :], ACT.Exp, scale=-0.5).then_inc(head_rstd, 1)

            for i in range(B * NH):
                act.wait_ge(arg_done, i + 1)
                wait(act, mixed_done, i - 1)
                act.activation(Dm[:, i % 2, 0:256], ps[:, 2 + i % 2, 0:256], ACT.Exp, bias=aT[:, 0, i:i + 1])
                act.activation(Dm[:, i % 2, 256:384], ps[:, 2 + i % 2, 256:384], ACT.Exp, bias=aT[:, 1, i:i + 1]).then_inc(decay_done, 1)
                if i >= 8 and i % 8 == 3:
                    square(i // 8 - 1)
                if i >= 8 and i % 8 == 7:
                    inverse_deviation(i // 8 - 1)
            square(B - 1)
            inverse_deviation(B - 1)

            act.activation(ea[:, :], alog[:, :], ACT.Exp).then_inc(window_done, 1)
            act.wait_ge(window_done, 1)
            act.activation(wnd[:, :], nl[:, :], ACT.Exp, scale=ea[:, :]).then_inc(window_done, 1)
            act.wait_ge(pos1_done, 1)
            for k in range(3):
                rows = P if k < 2 else 64
                last = act.activation(h1T[0:rows, k, :], ps[0:rows, k, :], ACT.Silu, bias=cols[0:rows, 16 + k:17 + k])
            last.then_inc(pos1_silu, 1)
            act.wait_ge(window_done, 2)
            act.activation(ea[:, :], alog[:, :], ACT.Copy).then_inc(window_done, 1)
            act.wait_ge(filtF_done, 1)
            act.activation(WF[0:FT, :, :, :].rearrange("p e f d -> p (e f d)"), ps[0:FT, 0:4, :].rearrange("p a c -> p (a c)"),
                           ACT.Copy).then_inc(filtF_copied, 1)
            deviation()

            def inverse_copy(q):
                for h in range(2):
                    act.wait_ge(inv_done, 2 * (q + 1))
                    act.activation(dcw[:, 4 * q + h:4 * q + 4:2, :], ps[:, 4 + 2 * (q % 2) + h, :].rearrange("p (b d) -> p b d", b=2),
                                   ACT.Copy).then_inc(inv_copied, 1)

            act.wait_ge(head_added, B)
            for n in range(8):
                act.wait_ge(zF_done, n + 1)
                wait(act, prod_re, n - 1)
                wait(act, prod_im, n - 1)
                act.activation(Zs[0:FT, n % 2, :, :], ps[0:FT, 0:4, :], ACT.Copy).then_inc(zF_copied, 1)
                if n >= 2 and n % 2 == 0:
                    inverse_copy(n // 2 - 1)
            inverse_copy(3)

            def transposed(r, gain=None, offset=None, groups=range(4)):
                for j in range(2 * groups[0], 2 * groups[-1] + 2):
                    c = j % 2
                    act.wait_ge(xT_done, 8 * r + j + 1)
                    wait(act, xT_high, 8 * r + j - 1)
                    wait(act, xT_low, 8 * r + j - 1)
                    if gain is None:
                        last = act.activation(tF[:, c, :], ps[:, j % 4, :], ACT.Identity)
                    else:
                        last = act.activation(tF[:, c, :], ps[:, j % 4, :], ACT.Identity,
                                              scale=cols[:, gain + c:gain + c + 1], bias=cols[:, offset + c:offset + c + 1])
                    last.then_inc(xT_copied, 1)

            def split_high(u, slot, loaded, plain=False):
                act.wait_ge(stage_loaded[slot], loaded)
                if isinstance(u, int) and u in (1, 2):
                    act.wait_ge(tile_done, TILES + 1)
                wait(act, down_done, (u - 1) * 8)
                act.activation(blocks(wH, slot, plain), blocks(wS, slot, plain), ACT.Copy).then_inc(w_high, 1)

            def silu(n, b, muls):
                wait(act, mul_done, n - 1 - muls)
                act.wait_ge(up_done, n + 1)
                act.activation(sg[:, b, :], ps[:, b, :], ACT.Silu).then_inc(silu_done, 1)

            deviation()
            transposed(0)
            act.wait_ge(shifted_done, 1)
            act.activation(sc0[:, :, :], sc0[:, :, :], ACT.Exp).then_inc(exp_done, 1)
            split_high(0, 0, 16)
            for i in range(8):
                silu(i, i % 2, 0)
            xsv = xs_d.rearrange("(q t p) d -> q p t d", t=2, p=P)
            ysv = ys_d.rearrange("(q t p) d -> q p t d", t=2, p=P)

            def pair_of(v, q):
                return v[q] if isinstance(q, int) else v[bass.ds(q, 1)].rearrange("a p t d -> (a p) t d")

            def load_pair(q, ring):
                wait(act, tT_done, q - 3)
                act.dma_start(xl[:, ring, :, :], pair_of(xsv, q)).then_inc(tile_loaded[ring], 16)

            def store_pair(q, ring):
                act.wait_ge(tY_done, q + 1)
                act.dma_start(pair_of(ysv, q), yo[:, ring, :, :]).then_inc(tile_stored[ring], 16)

            def tile_high(q, b):
                act.wait_ge(tT_done, q + 1)
                wait(act, tU_done, q - 1)
                act.activation(hH[:, b, :], ps[:, b, :], ACT.Copy).then_inc(tT_high, 1)

            def tile_silu(q, b):
                act.wait_ge(tU_done, q + 1)
                wait(act, tM_done, q - 1)
                act.activation(rs_[:, b, :, :], ps[:, 2 + b, :].rearrange("p (t c) -> p t c", t=2)[:, :, 0:P], ACT.Silu).then_inc(tS_done, 1)

            def hidden_high(q, b):
                act.wait_ge(tHT_done, q + 1)
                wait(act, tile_done, pairs_done(q - 1))
                act.activation(rhH[:, b, :, :], ps[:, 4 + b, 0:D].rearrange("p (t c) -> p t c", t=2), ACT.Copy).then_inc(tH_high, 1)

            act.wait_ge(scattered, 64 * 16)
            act.wait_ge(evac_done, 4 * M_FA)
            act.wait_ge(h_low, 8)
            act.wait_ge(table_done, 1)
            for q in range(4):
                load_pair(q, q)
            tile_high(0, 0)
            tile_high(1, 1)
            tile_silu(0, 0)

            def body(it, first=False, last=False):
                for j in range(4):
                    q = it * 4 + j
                    if not (last and j >= 2):
                        tile_high(q + 2, j % 2)
                    if not (last and j == 3):
                        tile_silu(q + 1, (j + 1) % 2)
                    hidden_high(q, j % 2)
                    if not last:
                        load_pair(q + 4, j)
                    if not (first and j < 2):
                        store_pair(q - 2, (j + 2) % 4)

            body(0, first=True)
            with act.Fori(1, PAIRS // 4 - 1) as it:
                body(it)
            body(PAIRS // 4 - 1, last=True)
            store_pair(PAIRS - 2, 2)
            store_pair(PAIRS - 1, 3)
            split_high(1, 1, 16, plain=True)

            def dense(u0, bias):
                for i in range(16):
                    n, b, u = 8 * u0 + i, i % 2, u0 + i // 8
                    c = 2 * (i // 8) + i % 2
                    act.wait_ge(up_done, n + 1)
                    act.wait_ge(h_low, n - 1)
                    act.activation(hF[:, b, :], ps[:, b, :], ACT.Silu, bias=cols[:, bias + c:bias + c + 1]).then_inc(silu_done, 1)
                    if i % 8 == 1:
                        split_high(u + 1, (u + 1) % 2, 16 * ((u + 1) // 2 + 1), plain=u + 1 < U_L1)

            for g in range(4):
                deviation_group(g)
                deviation_group(g)
                transposed(1, 0, 2, [g])
            dense(U_FA, 8)
            deviation()
            transposed(2, 4, 6)
            dense(U_FB, 12)
            deviation()
            transposed(3)
            act.wait_ge(shifted_done, 2)
            s1 = sc0[:, :, 0:16]
            act.activation(s1, s1, ACT.Exp).then_inc(exp_done, 1)

            def experts(it, last):
                for local in range(16):
                    silu(it * 16 + (8 * U_L1 + local), local % 2, PLAIN)
                    if local == 1:
                        split_high(it * 2 + (U_L1 + 1), 0, it * 16 + 16 * (U_L1 // 2 + 2))
                    if local == 9 and not last:
                        split_high(it * 2 + (U_L1 + 2), 1, it * 16 + 16 * (U_L1 // 2 + 2))

            with act.Fori(0, N_L1 // 2 - 1) as it:
                experts(it, False)
            experts(N_L1 // 2 - 1, True)

        @block.gpsimd
        def _(pool):
            steps = [0]

            def link(ins):
                steps[0] += 1
                ins.then_inc(pool_step, 1)
                pool.wait_ge(pool_step, steps[0])

            pool.memset(wS[:, 1, :], 0.0).then_inc(zero_done, 1)
            link(pool.memset(zcol[:, :], 0.0))
            link(pool.memset(gateW[:, :, :, :], 0.0))
            pool.wait_ge(const_loaded, 13 * 16)
            link(pool.tensor_tensor(gwt[:, 2:4, :], gwt[:, 2:4, :], gwt[:, 4:6, :], ALU.add))
            for b in range(B):
                for a in range(2):
                    last = pool.tensor_copy(gateW[:, :, b, 64 * a + 8 * b:64 * a + 8 * b + 8], gwt[:, 0:4, 8 * a:8 * a + 8])
            last.then_inc(gatew_done, 1)
            pool.tensor_copy(idb[:, :], ident[:, :])
            link(pool.tensor_tensor(id2[:, :], ident[:, 0:64], ident[:, 64:128], ALU.add))
            pool.tensor_copy(sel[:, :, :], id2[:, :].unsqueeze(2).to_broadcast([P, 64, P])).then_inc(sel_done, 1)
            pool.wait_ge(ctx_loaded, 16)
            pool.memset(vext[:, :, :, DH:DH + 1], 1.0)
            pool.tensor_copy(vext[:, :, :, 0:DH], cx[:, :, :].rearrange("p n (h d) -> p n h d", h=NH)).then_inc(vext_done, 1)
            for b in range(B):
                v = hN[:, b % 2, :].rearrange("p (g d) -> p g d", d=DH)
                hc = hC[:, b % 2, :].rearrange("p (g d) -> p g d", d=DH)
                hr = hR[:, b % 2, :].rearrange("p (g d) -> p g d", d=DH)
                mb = mean[:, b % 2, :, :].rearrange("p s h -> p (s h)").unsqueeze(2).to_broadcast([P, 2 * NH, DH])
                rb = rstd[:, b % 2, :, :].rearrange("p s h -> p (s h)").unsqueeze(2).to_broadcast([P, 2 * NH, DH])
                pool.wait_ge(head_scaled, b + 1)
                pool.tensor_tensor(hc, v, mb, ALU.subtract).then_inc(head_centred, 1)
                pool.wait_ge(head_rstd, 2 * (b + 1))
                link(pool.tensor_tensor(hr, hc, rb, ALU.mult))
                h2 = hR[:, b % 2, :].rearrange("p (s d) -> p s d", s=2)
                link(pool.tensor_tensor(h2, h2, bcv[:, 2:3, :].to_broadcast([P, 2, D]), ALU.mult))
                pool.tensor_tensor(x[:, 2 * b:2 * b + 2, :], x[:, 2 * b:2 * b + 2, :], h2, ALU.add).then_inc(head_added, 1)

            pool.wait_ge(filtF_copied, 1)
            for q in range(4):
                for fh in range(2):
                    n = 2 * q + fh
                    pool.wait_ge(zF_copied, n + 1)
                    wait(pool, inv_done, n - 1)
                    z = Zs[0:FT, n % 2, :, :].rearrange("p a (b d) -> p a b d", b=2)
                    o = PI[0:FT, n % 2, :].rearrange("p (b d) -> p b d", b=2)
                    tt = [tp[0:FT, s, :].rearrange("p (b d) -> p b d", b=2) for s in range(2)]
                    for s, (zi, wi) in enumerate(((0, 1), (1, 0), (0, 1), (1, 0))):
                        w = WF[0:FT, s // 2, 2 * wi + fh:2 * wi + fh + 1, :].to_broadcast([FT, 2, D])
                        dst = o if s == 0 else tt[s % 2]
                        link(pool.tensor_tensor(dst, z[:, 2 * (s // 2) + zi], w, ALU.mult))
                        if s:
                            last = pool.tensor_tensor(o, o, dst, ALU.add)
                            if s < 3:
                                link(last)
                    last.then_inc(prod_im, 1)

            def low_parts(r, groups=range(4)):
                for j in range(2 * groups[0], 2 * groups[-1] + 2):
                    g, c = j // 2, j % 2
                    pool.wait_ge(xT_high, 8 * r + j + 1)
                    pool.tensor_tensor(xTL[:, c, g * 512:(g + 1) * 512], tF[:, j % 2, :],
                                       f32(xTH[:, c, g * 512:(g + 1) * 512]), ALU.subtract).then_inc(xT_low, 1)

            def split_low(u, slot, plain=False):
                pool.wait_ge(w_high, u + 1)
                pool.tensor_tensor(blocks(wL, slot, plain), blocks(wS, slot, plain), f32(blocks(wH, slot, plain)),
                                   ALU.subtract).then_inc(w_low, 1)

            def low(n, b):
                pool.wait_ge(h_high, n + 1)
                pool.tensor_tensor(hL[:, b, :], hF[:, b, :], f32(hH[:, b, :]), ALU.subtract).then_inc(h_low, 1)

            def split_expert(ring, e, loaded, ahead):
                cols_ = slice(ring * EW, (ring + 1) * EW)
                if ahead is not None:
                    pool.wait_ge(tile_done, pool.value_load(ptab[0:1, ahead], min_val=1, max_val=TILES + 1))
                pool.wait_ge(estage_loaded[ring], loaded)
                pool.tensor_tensor(eH[:, cols_], eS[:, cols_], zcol[:, :].to_broadcast([P, EW]), ALU.add).then_inc(ew_high, 1)
                pool.wait_ge(ew_high, e + 1)
                pool.tensor_tensor(eL[:, cols_], eS[:, cols_], f32(eH[:, cols_]), ALU.subtract).then_inc(ew_ready, 1)

            low_parts(0)
            split_low(0, 0)
            for e in range(2):
                split_expert(e + 2, e, 16, None)
            pool.wait_ge(slots_done, 2)
            pool.wait_ge(zeros_stored, 16 * (TILES * D // UW))
            for i in range(8):
                low(i, i % 2)
                for n in range(2 * i, 2 * i + 2):
                    for k in range(TOPK):
                        pool.indirect_dma_start(xs_d, bass.IndirectOffsetOnAxis(ap=idS[:, n, k:k + 1], axis=0), xn[:, n, :], None,
                                                bounds_check=TILES * P - 1, oob_is_err=False).then_inc(scattered, 16)
            pool.wait_ge(table_done, 1)
            pool.wait_ge(evac_done, 4 * M_FA)
            for e in range(2, 4):
                split_expert(e - 2, e, 16, None)
            with pool.Fori(1, E0 // 4) as it:
                for e in range(4):
                    split_expert((e + 2) % 4, it * 4 + e, it * 16 + 16, bass.ds(it * 4 + (e - 4), 1))
            pool.wait_ge(slots_done, 2)
            for i in range(4):
                pool.wait_ge(tile_stored[i], PAIRS // 4 * 16)
            for n in range(NT):
                wait(pool, combined, n - 3)
                for k in range(TOPK):
                    pool.indirect_dma_start(yg[:, n % 4, k, :], None, ys_d, bass.IndirectOffsetOnAxis(ap=idG[:, n, k:k + 1], axis=0),
                                            bounds_check=TILES * P - 1, oob_is_err=False).then_inc(gathered[n % 4], 16)
                if n % 4 == 3 and n > 3:
                    low_parts(1, [n // 4 - 1])
            low_parts(1, [3])
            split_low(1, 1, True)

            def dense(u0):
                for i in range(16):
                    low(8 * u0 + i, i % 2)
                    if i % 8 == 1:
                        u = u0 + i // 8 + 1
                        split_low(u, u % 2, u < U_L1)

            dense(U_FA)
            low_parts(2)
            dense(U_FB)
            low_parts(3)

            def experts(it, last):
                for local in range(16):
                    low(it * 16 + (8 * U_L1 + local), local % 2)
                    if local == 1:
                        split_low(it * 2 + (U_L1 + 1), 0)
                    if local == 9 and not last:
                        split_low(it * 2 + (U_L1 + 2), 1)

            with pool.Fori(0, N_L1 // 2 - 1) as it:
                experts(it, False)
            experts(N_L1 // 2 - 1, True)

        @block.tensor
        def _(pe):
            pe.wait_ge(const_loaded, 13 * 16)
            pe.wait_ge(ctx_loaded, 16)
            for j in range(16):
                src, g, c = (cx, xn)[j // 8], j % 8 // 2, j % 2
                wait(pe, mixT_copied, j - 3)
                if src is xn:
                    pe.wait_ge(norm_done, 4 * g + 4)
                for t in range(4):
                    last = pe.transpose(ps[:, j % 4, t * P:(t + 1) * P], src[:, 4 * g + t, c * P:(c + 1) * P], ident[:, :])
                last.then_inc(mixT_done, 1)
            pe.wait_ge(gatew_done, 1)
            pe.wait_ge(mixT_copied, 16)
            for b in range(B):
                for k in range(4):
                    rhs = (qT, kT)[k // 2][:, k % 2, b * SEQ:(b + 1) * SEQ]
                    last = pe.matmul(ps[:, 4, 0:SEQ], gateW[:, k, b, :], rhs, start=(b == 0 and k == 0), stop=(b == B - 1 and k == 3))
            last.then_inc(gates_done, 1)
            pe.wait_ge(rows_done, 1)
            for h in range(2):
                last = pe.transpose(ps[:, 5, h * P:(h + 1) * P], AE[:, h * P:(h + 1) * P], ident[:, :])
            last.then_inc(rowsT_done, 1)
            pe.wait_ge(sel_done, 1)
            pe.wait_ge(vext_done, 1)
            pe.wait_ge(rowsT_copied, 1)

            def scores(i):
                b, h = i // NH, i % NH
                c, r = h // 4, DH * (h % 4)
                t0 = b * SEQ
                wait(pe, mixed_done, i - 1)
                pe.matmul(ps[:, i % 2, 0:256], kT[r:r + DH, c, t0:t0 + P], qT[r:r + DH, c, t0:t0 + SEQ], start=True, stop=True)
                pe.matmul(ps[:, i % 2, 256:384], kT[r:r + DH, c, t0 + P:t0 + SEQ], qT[r:r + DH, c, t0 + P:t0 + SEQ],
                          start=True, stop=True).then_inc(qk_done, 1)
                wait(pe, decay_done, i - 1)
                pe.matmul(ps[:, 2 + i % 2, 0:384], idb[:, :], maskT[:, :], start=True, stop=False, skip_group_check=True)
                pe.matmul(ps[:, 2 + i % 2, 0:256], sel[:, i, :], MHL[:, :], start=False, stop=False, skip_group_check=True)
                pe.matmul(ps[:, 2 + i % 2, 256:384], sel[:, i, :], MHL[:, P:SEQ], start=False, stop=True,
                          skip_group_check=True).then_inc(arg_done, 1)

            def values(i):
                b, h = i // NH, i % NH
                o0, o1 = (ps[:, 4 + 2 * (b % 2) + s, h * (DH + 1):(h + 1) * (DH + 1)] for s in range(2))
                pe.wait_ge(mixed_done, i + 1)
                if h == 0:
                    wait(pe, head_scaled, b - 1)
                pe.matmul(o0, Cm[:, i % 2, 0:P], vext[:, 2 * b, h, :], start=True, stop=True)
                pe.matmul(o1, Cm[:, i % 2, P:2 * P], vext[:, 2 * b, h, :], start=True, stop=False)
                pe.matmul(o1, Cm[:, i % 2, 2 * P:3 * P], vext[:, 2 * b + 1, h, :], start=False, stop=True).then_inc(pv_done, 1)

            for i in range(B * NH):
                scores(i)
                if i:
                    values(i - 1)
            values(B * NH - 1)

            pe.wait_ge(conv_loaded, 7 * 16)
            pe.wait_ge(mixed_done, B * NH)
            pe.wait_ge(decay_done, B * NH)
            for k in range(3):
                rows = P if k < 2 else 64
                last = pe.matmul(ps[0:rows, k, :], Wp1[:, k * P:k * P + rows], peT[:, :], start=True, stop=True)
            last.then_inc(pos1_done, 1)
            pe.wait_ge(pos1_silu, 1)
            pe.wait_ge(head_scaled, B)
            for lt in range(4):
                first = 256 * (lt % 2) + lt // 2
                for k in range(3):
                    rows = P if k < 2 else 64
                    last = pe.matmul(ps[:, 4 + lt // 2, (lt % 2) * D:(lt % 2 + 1) * D], h1T[0:rows, k, first:first + 255:2],
                                     Wp2[0:rows, k, :], start=k == 0, stop=k == 2)
            last.then_inc(pos2_done, 1)
            pe.wait_ge(filt_done, 1)
            for e in range(2):
                for f in range(4):
                    for k in range(2):
                        last = pe.matmul(ps[0:FT, 2 * e + f // 2, (f % 2) * D:(f % 2 + 1) * D], FW[:, 2 * e + k, f, :],
                                         wf[:, 2 * e + k, :], start=k == 0, stop=k == 1)
            last.then_inc(filtF_done, 1)
            pe.wait_ge(filtF_copied, 1)
            for b in range(B):
                for r in range(2):
                    for k in range(2):
                        last = pe.matmul(ps[:, b, r * D:(r + 1) * D], kT[:, k, b * SEQ + r:(b + 1) * SEQ:2], Win[:, k, :],
                                         start=k == 0, stop=k == 1)
                last.then_inc(zlin_done, 1)

            def inverse(n):
                q, fh = n // 2, n % 2
                pe.wait_ge(prod_re, n + 1)
                pe.wait_ge(prod_im, n + 1)
                if fh == 0:
                    wait(pe, inv_copied, 2 * (q - 1))
                for h in range(2):
                    for ri, src in enumerate((PR, PI)):
                        last = pe.matmul(ps[:, 4 + 2 * (q % 2) + h, :], GI[0:FT, 2 * ri + fh, h * P:(h + 1) * P], src[0:FT, n % 2, :],
                                         start=(fh == 0 and ri == 0), stop=(fh == 1 and ri == 1))
                last.then_inc(inv_done, 1)

            pe.wait_ge(zlin_copied, B)
            for n in range(8):
                q, fh = n // 2, n % 2
                pe.wait_ge(zaff_dve, q + 1)
                wait(pe, zF_copied, n)
                for e in range(2):
                    for ri in range(2):
                        last = pe.matmul(ps[0:FT, 2 * e + ri, :].rearrange("p (b d) -> p b d", b=2), FZ[:, 2 * ri + fh, :],
                                         zn[:, 2 * q:2 * q + 2, e, :], start=True, stop=True)
                last.then_inc(zF_done, 1)
                if n:
                    inverse(n - 1)
            inverse(7)

            def transposes(r):
                for j in range(8):
                    g, c = j // 2, j % 2
                    if j >= 4:
                        pe.wait_ge(xT_copied, 8 * r + j - 3)
                    pe.wait_ge(norm_done, NT * (r + 1) + 4 * g + 4)
                    for t in range(4):
                        last = pe.transpose(ps[:, j % 4, t * P:(t + 1) * P], xn[:, 4 * g + t, c * P:(c + 1) * P], ident[:, :])
                    last.then_inc(xT_done, 1)

            def logits(r, gH, gL, width):
                pe.wait_ge(gate_split, 1)
                pe.wait_ge(xT_low, 8 * (r + 1))
                for n in range(NT):
                    q = 0
                    for k in range(2):
                        for a, g in ((xTH, gH), (xTL, gH), (xTH, gL)):
                            last = pe.matmul(ps[:, 7, n * width:(n + 1) * width], a[:, k, n * P:(n + 1) * P], g[:, k, :],
                                             start=q == 0, stop=q == 5)
                            q += 1
                last.then_inc(logits_done, 1)

            def up(n, local, u, slot, muls):
                g, c, b = local % 8 // 2, local % 2, local % 2
                if local % 8 == 0:
                    pe.wait_ge(w_low, u + 1)
                wait(pe, silu_done, n - 1)
                if muls is not None:
                    wait(pe, mul_done, n - 1 - muls)
                for half in range(2 if muls is not None else 1):
                    q = 0
                    for k in range(2):
                        col = half * BLK + k * D + c * P
                        for w, v in ((wH, xTH), (wL, xTH), (wH, xTL)):
                            last = pe.matmul(ps[:, 2 * half + b, :], w[:, slot, col:col + P], v[:, k, g * 512:(g + 1) * 512],
                                             start=q == 0, stop=q == 5)
                            q += 1
                last.then_inc(up_done, 1)

            def down(n, local, m, slot, pair, opens, closes):
                c, b = local % 2, local % 2
                pe.wait_ge(h_low, n + 1)
                if opens:
                    wait(pe, evac_done, (m - 1) * 4)
                for t in range(4):
                    o = ps[:, 4 + 2 * pair + t // 2, (t % 2) * D:(t % 2 + 1) * D]
                    col = 2 * BLK + c * D
                    for q, (h, w) in enumerate(((hH, wH), (hL, wH), (hH, wL))):
                        last = pe.matmul(o, h[:, b, t * P:(t + 1) * P], w[:, slot, col:col + D],
                                         start=(opens and t % 2 == 0 and q == 0), stop=(closes and q == 2), skip_group_check=True)
                last.then_inc(down_done, 1)

            transposes(0)
            logits(0, wg0H, wg0L, E0)
            pe.wait_ge(chosen_done, 1)
            rhs = selm[:, :, :].rearrange("p n e -> p (n e)")
            pe.matmul(ps[:, 6, :], tri[:, 0, :], rhs, start=True, stop=True)
            pe.matmul(ps[:, 5, :], tri[:, 1, :], rhs, start=True, stop=True).then_inc(counts_done, 1)
            pe.wait_ge(xT_copied, 8)

            for i in range(9):
                if i < 8:
                    up(i, i, 0, 0, 0)
                if i == 1:
                    pe.wait_ge(counts_read, 1)
                if i:
                    j = i - 1
                    down(j, j, j // 2, 0, j // 2 % 2, j % 2 == 0, j % 2 == 1)

            def tile_transpose(q, b, ring, loaded):
                pe.wait_ge(tile_loaded[ring], loaded)
                wait(pe, tT_low, q - 1)
                for t in range(2):
                    for k in range(2):
                        last = pe.transpose(ps[:, b, (2 * t + k) * P:(2 * t + k + 1) * P], xl[:, ring, t, k * P:(k + 1) * P], ident[:, :])
                return last.then_inc(tT_done, 1)

            def word(i):
                return pe.value_load(words[0:1, slice(i, i + 1) if isinstance(i, int) else bass.ds(i, 1)], min_val=0, max_val=(1 << 24) - 1)

            def place(v):
                return (v & 0xF00).with_bounds(min_val=0, max_val=3 * EW)

            def tile_up(q, b, v):
                pe.wait_ge(tT_low, q + 1)
                wait(pe, tM_done, q - 1)
                pe.wait_ge(ew_ready, v & 255)
                offs = [place(v), place(v >> 4)]
                for t in range(2):
                    off = offs[t]
                    i = 0
                    for k in range(2):
                        for h, w in ((hH, eH), (hL, eH), (hH, eL)):
                            last = pe.matmul(ps[:, 2 + b, t * D:(t + 1) * D], h[:, b, (2 * t + k) * P:(2 * t + k + 1) * P],
                                             w[:, bass.ds(off + k * D, D)], start=i == 0, stop=i == 5)
                            i += 1
                last.then_inc(tU_done, 1)

            def hidden_transpose(q, b):
                pe.wait_ge(tM_done, q + 1)
                wait(pe, tH_low, q - 1)
                for t in range(2):
                    last = pe.transpose(ps[:, 4 + b, t * P:(t + 1) * P], rh[:, b, t, :], ident[:, :])
                last.then_inc(tHT_done, 1)

            def tile_down(q, b, v):
                offs = [place(v >> 8), place(v >> 12)]
                pe.wait_ge(tH_low, q + 1)
                wait(pe, tY_done, q - 1)
                for t in range(2):
                    off = offs[t]
                    for i, (h, w) in enumerate(((rhH, eH), (rhL, eH), (rhH, eL))):
                        last = pe.matmul(ps[:, 6 + b, t * D:(t + 1) * D], h[:, b, t, :], w[:, bass.ds(off + 2 * D, D)],
                                         start=i == 0, stop=i == 2)
                    last.then_inc(tile_done, 1)

            pe.wait_ge(evac_done, 4 * M_FA)
            tile_transpose(0, 0, 0, 16)
            tile_transpose(1, 1, 1, 16)
            pe.wait_ge(tT_done, 2)
            pe.sem_inc(tile_done, 1)
            tile_up(0, 0, word(0))

            def body(it, first=False, last=False):
                v = word(it * 4 + 1)
                for j in range(4):
                    q = it * 4 + j
                    if not (last and j >= 2):
                        tile_transpose(q + 2, j % 2, (j + 2) % 4, it * 16 + (16 if j < 2 else 32))
                    if not (last and j == 3):
                        tile_up(q + 1, (j + 1) % 2, v)
                    after = word(it * 4 + (j + 2)) if j < 3 else None
                    hidden_transpose(q, j % 2)
                    if not (first and j == 0):
                        tile_down(q - 1, (j + 1) % 2, v)
                    v = after

            body(0, first=True)
            with pe.Fori(1, PAIRS // 4 - 1) as it:
                body(it)
            body(PAIRS // 4 - 1, last=True)
            tile_down(PAIRS - 1, 1, word(PAIRS + 1))

            def dense(u0, m0):
                for i in range(17):
                    if i < 16:
                        up(8 * u0 + i, i, u0 + i // 8, (u0 + i // 8) % 2, None)
                    if i:
                        j = i - 1
                        down(8 * u0 + j, j, m0 + j // 2, (u0 + j // 8) % 2, j // 2 % 2, j % 2 == 0, j % 2 == 1)

            transposes(1)
            pe.wait_ge(xT_low, 16)
            dense(U_FA, M_FA)
            transposes(2)
            pe.wait_ge(xT_low, 24)
            dense(U_FB, M_FB)
            transposes(3)
            logits(3, wg1H, wg1L, 16)

            def expert_up(it, local):
                up(it * 16 + (8 * U_L1 + local), local, it * 2 + (U_L1 + local // 8), 1 - local // 8, PLAIN)

            def expert_down(it, local):
                down(it * 16 + (8 * U_L1 + local), local, it * 8 + (M_L1 + local // 2), 1 - local // 8, local // 2 % 2,
                     local % 2 == 0, local % 2 == 1)

            def experts(it, last):
                for local in range(16):
                    if local < 15:
                        expert_up(it, local + 1)
                    elif not last:
                        expert_up(it + 1, 0)
                    expert_down(it, local)

            expert_up(0, 0)
            pe.wait_ge(cw_done, 1)
            with pe.Fori(0, N_L1 // 2 - 1) as it:
                experts(it, False)
            experts(N_L1 // 2 - 1, True)


def constants(np):
    n = 4 * FT
    w = 2 * np.pi * (np.arange(2 * FT) + 0.5) / n
    p = np.arange(P)

    def forward(pos):
        a = np.outer(pos, w)
        return np.concatenate([np.cos(a), -np.sin(a)], 1).reshape(len(pos), 4, FT)

    pos = np.arange(2 * P)
    odd = forward(pos + 1)
    fw = np.concatenate([forward(pos).reshape(2, P, 4, FT), odd.reshape(2, P, 4, FT)]).transpose(1, 0, 2, 3)
    a = np.outer(w, np.arange(D))
    gi = np.concatenate([np.cos(a), -np.sin(a)]).reshape(4, FT, D) * (2.0 / n)
    gfull = np.zeros((P, 4, D))
    gfull[:FT] = gi.transpose(1, 0, 2)
    t, s = np.arange(P)[:, None], np.arange(P)[None, :]
    mask = np.zeros((P, 3 * P))
    mask[:, 0:P] = mask[:, 2 * P:] = np.where(t <= s, 0.0, -1e30)
    tri = np.stack([(t < s) * 1.0, np.ones((P, P))], 1)
    nl = -np.stack([2 * p, 2 * (p + P), 2 * p + 1, 2 * (p + P) + 1], 1)
    f = np.float32
    return {"ident": np.eye(P).astype(f), "fz": forward(p).astype(f), "fw": fw.astype(f), "gi": gfull.astype(f),
            "maskT": mask, "tri": tri, "nl": nl.astype(f), "iot": np.tile(np.arange(E0), (P, 1)).astype(f),
            "tilen": np.tile(np.arange(TILES), (P, 1)).astype(f)}


def kernel(**inputs):
    import ml_dtypes
    import numpy as np
    import concourse.bacc as bacc
    from concourse.bass_utils import run_bass_kernel_spmd as run

    nc = bacc.Bacc("TRN2", target_bir_lowering=False, num_devices=1)
    I = {k: np.asarray(v) for k, v in inputs.items()}

    def chunked(w):
        return w.reshape(2, P, -1).transpose(1, 0, 2)

    def column(v, k):
        return np.concatenate([v, np.zeros(P * k - len(v), v.dtype)]).reshape(k, P).T

    A = constants(np)
    A["maskT"] = A["maskT"].astype(ml_dtypes.bfloat16)
    A["tri"] = A["tri"].astype(ml_dtypes.bfloat16)
    A["x"], A["ctx"] = I["x"], I["ctx_1024"]
    gates = np.concatenate([I["L0_xattn_igate_w"], I["L0_xattn_fgate_w"]], 0).T
    A["gw"] = gates.reshape(6, P, 16).transpose(1, 0, 2)
    A["gbias"] = np.concatenate([np.tile(I["L0_xattn_igate_b"], B), np.tile(I["L0_xattn_fgate_b"], B)]).reshape(P, 1)
    rows = np.stack([I[n] for n in ("L1_xattn_b1b", "L1_xattn_b2b", "L0_xattn_norm_w", "L1_xattn_b_in", "L1_xattn_g_ln",
                                    "L1_xattn_beta_ln", "L1_xattn_bp2")])
    A["bcv"] = np.broadcast_to(rows[None], (P, 7, D))
    A["cols"] = np.concatenate([column(I["L1_xattn_" + n], k) for n, k in
                                (("g1", 2), ("be1", 2), ("g2", 2), ("be2", 2), ("b1a", 4), ("b2a", 4), ("bp1", 3))], 1)
    A["alog"] = np.broadcast_to(I["L1_xattn_a"].reshape(1, 1), (P, 1))
    A["win"] = chunked(I["L1_xattn_W_in"])
    A["pet"] = I["L1_xattn_pe"].T
    A["wp1"] = I["L1_xattn_Wp1"]
    wp2 = I["L1_xattn_Wp2"]
    A["wp2"] = np.concatenate([wp2, np.zeros((64, D), wp2.dtype)]).reshape(3, P, D).transpose(1, 0, 2)
    A["wg0"] = chunked(I["L0_ffn_Wg"])
    A["wg1"] = chunked(np.concatenate([I["L1_ffn_w_router"], I["L1_ffn_w_gating"]], 1))
    sh = np.concatenate([chunked(I["L0_ffn_" + n]).reshape(P, BLK) for n in ("Ws1", "Ws3", "Ws2")], 1)[None]
    A["w0"] = sh
    w13 = np.stack([I["L0_ffn_W1"], I["L0_ffn_W3"]], 2).reshape(E0, 2, P, D).transpose(0, 2, 1, 3).reshape(E0, P, BLK)
    A["wr"] = np.concatenate([w13, I["L0_ffn_W2"]], 2)
    ab = []
    for n in ("1", "2"):
        a = I[f"L1_xattn_W{n}a"].reshape(2, P, 2, D).transpose(2, 1, 0, 3).reshape(2, P, BLK)
        b = I[f"L1_xattn_W{n}b"].reshape(2, 2, P, D).transpose(0, 2, 1, 3).reshape(2, P, BLK)
        ab.append(np.concatenate([a, b], 2))
    A["wab"] = np.concatenate(ab)
    gu = [I["L1_ffn_" + n].reshape(E1, 2, P, 4, D).transpose(0, 3, 2, 1, 4).reshape(N_L1, P, BLK) for n in ("w_gate", "w_up")]
    gu.append(I["L1_ffn_w_down"].reshape(E1, 4, 2, P, D).transpose(0, 1, 3, 2, 4).reshape(N_L1, P, BLK))
    A["w1"] = np.concatenate(gu, 2)
    A = {k: np.ascontiguousarray(v) for k, v in A.items()}
    dram = {k: nc.dram_tensor("in_" + k, v.shape, mybir.dt.from_np(v.dtype), kind="ExternalInput").ap() for k, v in A.items()}
    out = nc.dram_tensor("out_0", (B, SEQ, D), F32, kind="ExternalOutput").ap()
    build(nc, dram, out)
    r = run(nc, [{"in_" + k: v for k, v in A.items()}], core_ids=[0])
    return r.results[0]["out_0"]
```

```python
import concourse.bass as bass
from concourse import mybir
from contextlib import ExitStack

F32 = mybir.dt.float32
F32R = mybir.dt.float32r
BF16 = mybir.dt.bfloat16
U32 = mybir.dt.uint32
I32 = mybir.dt.int32
ALU = mybir.AluOpType
ACT = mybir.ActivationFunctionType
AXX = mybir.AxisListType.X

P = 128
B, SEQ, D = 8, 256, 256
NT = B * SEQ // P
NH, DH = 8, 32
E0, TOPK = 32, 4
CAP = 4 * (B * SEQ * TOPK) // E0
E1 = 8
FT = 96
IM_POOL = 176
BLK = 512
UW = 3 * BLK
EPS = 1e-5
ARENA = 210000 // 64 * 64

U_FA, U_FB, U_L1 = 1, 3, 5
N_L1 = 32
TILES = B * SEQ * TOPK // P + E0
PAIRS = TILES // 2
EW = 3 * D
FAR = float(1 << 20)
U8 = 8
PLAIN = 32
M_FA = 4
M_FB = M_FA + 8
M_L1 = M_FB + 8


def build(nc, dram, out_d):
    ctx = ExitStack()
    with ctx:
        base = (nc.sbuf_base + 63) // 64 * 64
        ctx.enter_context(nc.sbuf_tensor("arena", [P, ARENA], mybir.dt.uint8))
        top = [base]
        start, end = {}, {}

        def at(name, shape, dt=F32, off=None):
            n = 2 if dt == BF16 else 4
            for s in shape[1:]:
                n *= s
            n = (n + 63) // 64 * 64
            if off is None:
                off = top[0]
                top[0] += n
            start[name], end[name] = off, off + n
            return nc.alloc_sbuf_tensor_at(name, shape, dt, offset=off)

        x = at("x", [P, NT, D])
        dcw = at("dcw", [P, NT, D])
        ya = at("ya", [P, NT, D])
        xn = at("xn", [P, NT, D])
        xTH = at("xTH", [P, 2, NT * P], F32R)
        xTL = at("xTL", [P, 2, NT * P], F32R)
        wS = at("wS", [P, 2, UW])
        wH = at("wH", [P, 2, UW], F32R)
        wL = at("wL", [P, 2, UW], F32R)
        sg = at("sg", [P, 2, 512])
        hF = at("hF", [P, 2, 512])
        hH = at("hH", [P, 2, 512], F32R)
        hL = at("hL", [P, 2, 512], F32R)
        tF = at("tF", [P, 2, 512])
        ident = at("ident", [P, P])
        bcv = at("bcv", [P, 7, D])
        cols = at("cols", [P, 19])
        sc0 = at("sc0", [P, NT, E0])
        sc1 = at("sc1", [P, NT, E0])
        sc2 = at("sc2", [P, NT, E0])
        sc3 = at("sc3", [P, NT, E0])
        selm = at("selm", [P, NT, E0], BF16)
        cw2 = at("cw2", [P, NT, 16])
        st = at("st", [P, NT, 6])
        mv = at("mv", [P, NT, 2])
        ve = at("ve", [P, NT])
        sd = at("sd", [P, NT])
        rs = at("rs", [P, NT])
        nt1 = at("nt1", [P, NT])
        sm = at("sm", [P, NT, 2])
        sm2 = at("sm2", [P, NT])
        mx8 = at("mx8", [P, NT, 8])
        ix8 = at("ix8", [P, NT, 8], U32)
        ixf = at("ixf", [P, NT, 8])
        iot = at("iot", [P, E0])
        tilen = at("tilen", [P, TILES])
        rt = at("rt", [P, 4, E0])
        cmp8 = at("cmp8", [P, E0, 8])
        slk = at("slk", [P, NT, TOPK])
        okk = at("okk", [P, NT, TOPK])
        wk = at("wk", [P, NT, TOPK])
        idS = at("idS", [P, NT, TOPK], U32)
        idG = at("idG", [P, NT, TOPK], U32)
        etf = at("etf", [1, 2, TILES])
        wordf = at("wordf", [1, PAIRS + 2])
        words = at("words", [1, PAIRS + 2], I32)
        ptab = at("ptab", [1, E0], I32)
        zcol = at("zcol", [P, 1])
        tri = at("tri", [P, 2, P], BF16)
        wg0 = at("wg0", [P, 2, E0])
        wg0H = at("wg0H", [P, 2, E0], F32R)
        wg0L = at("wg0L", [P, 2, E0], F32R)
        wg1 = at("wg1", [P, 2, 16])
        wg1H = at("wg1H", [P, 2, 16], F32R)
        wg1L = at("wg1L", [P, 2, 16], F32R)
        vext = at("vext", [P, NT, NH, DH + 1])
        maskT = at("maskT", [P, 384], BF16)
        idb = at("idb", [P, P], BF16)
        gwt = at("gwt", [P, 6, 16])
        gbias = at("gbias", [P, 1])
        aT = at("aT", [P, 2, 64])
        eE = at("eE", [P, 2, 64])
        den = at("den", [P, 2, NH])
        mean = at("mean", [P, 2, 2, NH])
        var = at("var", [P, B, 2, NH])
        rstd = at("rstd", [P, B, 2, NH])
        alog = at("alog", [P, 1])
        ea = at("ea", [P, 1])
        nl = at("nl", [P, 4])
        wnd = at("wnd", [P, 4])
        assert top[0] - base <= ARENA, top[0] - base
        sel = at("sel", [P, 64, P], F32R, start["dcw"])
        qT = at("qT", [P, 2, NT * P], F32, start["xTH"])
        kT = at("kT", [P, 2, NT * P], F32, start["xTL"])
        qM = at("qM", [P, 12, SEQ], F32, start["wS"])
        gateW = at("gateW", [P, 4, B, P], F32, start["wH"])
        cx = at("cx", [P, NT, D], F32, end["gateW"])
        Dm = at("Dm", [P, 2, 384], F32, end["cx"])
        Cm = at("Cm", [P, 3, 384], F32, end["Dm"])
        rg = at("rg", [P, 256], F32, start["sc0"])
        r1 = at("r1", [P, 256], F32, end["rg"])
        r2 = at("r2", [P, 256], F32, end["r1"])
        r3 = at("r3", [P, 256], F32, end["r2"])
        rF = at("rF", [P, 256], F32, end["r3"])
        rM = at("rM", [P, 256], F32, end["rF"])
        AE = at("AE", [P, 256], F32, end["rM"])
        ones = at("ones", [P, 256], F32, end["AE"])
        MHL = at("MHL", [P, 256], F32R, end["ones"])
        id2 = at("id2", [P, 64], F32, end["MHL"])
        hC = at("hC", [P, B, 512], F32, start["xn"])
        eS = wS[:, :, :].rearrange("p s c -> p (s c)")
        eH = wH[:, :, :].rearrange("p s c -> p (s c)")
        eL = wL[:, :, :].rearrange("p s c -> p (s c)")
        xl = at("xl", [P, 4, 2, D], F32, start["ya"])
        yo = at("yo", [P, 4, 2, D], F32, end["xl"])
        rhH = at("rhH", [P, 2, 2, P], F32R, start["sg"])
        rhL = at("rhL", [P, 2, 2, P], F32R, end["rhH"])
        rs_ = at("rs_", [P, 2, 2, P], F32, start["hF"])
        rh = at("rh", [P, 2, 2, P], F32, end["rs_"])
        cmpt = at("cmpt", [1, TILES, E0], F32, start["ya"])
        lgT = at("lgT", [E0, NT * P], F32, start["ya"])
        yg = at("yg", [P, 4, TOPK, D], F32, start["vext"])
        assert end["yg"] <= end["vext"]
        zn = at("zn", [P, B, 2, D], F32, start["xTH"])
        Zs = at("Zs", [P, 2, 4, 512], F32, start["xn"])
        FZ = at("FZ", [P, 4, FT], F32, start["wH"])
        FW = at("FW", [P, 4, 4, FT], F32, end["FZ"])
        GI = at("GI", [P, 4, D], F32, end["FW"])
        Win = at("Win", [P, 2, D], F32, end["GI"])
        peT = at("peT", [64, 512], F32, end["Win"])
        Wp1 = at("Wp1", [64, 320], F32, end["peT"])
        Wp2 = at("Wp2", [P, 3, D], F32, end["Wp1"])
        h1T = at("h1T", [P, 3, 512], F32, end["Wp2"])
        wf = at("wf", [P, 4, D], F32, end["h1T"])
        hN = at("hN", [P, 2, 512], F32, start["h1T"])
        hQ = at("hQ", [P, 2, 512], F32, end["hN"])
        WF = at("WF", [P, 2, 4, D], F32, start["sc0"])
        PR = at("PR", [P, 2, 512], F32, start["vext"])
        PI = at("PI", [P, 2, 512], F32, end["PR"])
        tv = at("tv", [P, 2, 512], F32, end["PI"])
        tp = at("tp", [P, 2, 512], F32, end["tv"])
        assert end["Cm"] <= end["tF"] and end["wf"] <= start["Dm"] and end["id2"] <= end["cw2"]
        assert end["hC"] <= end["xn"] and end["hQ"] <= end["wf"] and end["WF"] <= end["cw2"] and end["tp"] <= end["vext"]

        ps = ctx.enter_context(nc.psum_tensor("ps", [P, 8, 512], F32))

        def sem(name):
            return ctx.enter_context(nc.semaphore(name))

        x_loaded = sem("x_loaded")
        ctx_loaded = sem("ctx_loaded")
        const_loaded = sem("const_loaded")
        conv_loaded = sem("conv_loaded")
        stage_loaded = [sem("stage0_loaded"), sem("stage1_loaded")]
        out_stored = sem("out_stored")
        var_done = sem("var_done")
        std_done = sem("std_done")
        norm_done = sem("norm_done")
        dve_step = sem("dve_step")
        pool_step = sem("pool_step")
        act_step = sem("act_step")
        gatew_done = sem("gatew_done")
        id2_done = sem("id2_done")
        sel_done = sem("sel_done")
        vext_done = sem("vext_done")
        mixT_done = sem("mixT_done")
        mixT_copied = sem("mixT_copied")
        gates_done = sem("gates_done")
        gates_copied = sem("gates_copied")
        negabs_done = sem("negabs_done")
        softplus_done = sem("softplus_done")
        logf_done = sem("logf_done")
        logf_moved = sem("logf_moved")
        rows_done = sem("rows_done")
        rowsT_done = sem("rowsT_done")
        rowsT_copied = sem("rowsT_copied")
        q_masked = sem("q_masked")
        qk_done = sem("qk_done")
        arg_done = sem("arg_done")
        decay_done = sem("decay_done")
        mixed_done = sem("mixed_done")
        pv_done = sem("pv_done")
        head_read = sem("head_read")
        head_scaled = sem("head_scaled")
        head_centred = sem("head_centred")
        head_squared = sem("head_squared")
        head_var = sem("head_var")
        head_rstd = sem("head_rstd")
        head_added = sem("head_added")
        pos1_done = sem("pos1_done")
        pos1_silu = sem("pos1_silu")
        window_done = sem("window_done")
        pos2_done = sem("pos2_done")
        filt_done = sem("filt_done")
        filtF_done = sem("filtF_done")
        filtF_copied = sem("filtF_copied")
        zlin_done = sem("zlin_done")
        zlin_copied = sem("zlin_copied")
        zaff_dve = sem("zaff_dve")
        zF_done = sem("zF_done")
        zF_copied = sem("zF_copied")
        prod_dve = sem("prod_dve")
        prod_pool = sem("prod_pool")
        inv_done = sem("inv_done")
        inv_copied = sem("inv_copied")
        xT_done = sem("xT_done")
        xT_copied = sem("xT_copied")
        xT_high = sem("xT_high")
        xT_low = sem("xT_low")
        gate_split = sem("gate_split")
        logitsT_done = sem("logitsT_done")
        logitsT_copied = sem("logitsT_copied")
        logits_done = sem("logits_done")
        shifted_done = sem("shifted_done")
        exp_done = sem("exp_done")
        chosen_done = sem("chosen_done")
        counts_done = sem("counts_done")
        cw_done = sem("cw_done")
        bias_added = sem("bias_added")
        xs_d = nc.dram_tensor("slots_in", (TILES * P, D), F32, kind="Internal").ap()
        ys_d = nc.dram_tensor("slots_out", (TILES * P, D), F32, kind="Internal").ap()
        counts_read = sem("counts_read")
        slots_done = sem("slots_done")
        table_done = sem("table_done")
        zero_done = sem("zero_done")
        zeros_stored = sem("zeros_stored")
        scattered = sem("scattered")
        estage_loaded = [sem(f"estage{i}_loaded") for i in range(4)]
        ew_high = sem("ew_high")
        ew_ready = sem("ew_ready")
        tile_loaded = [sem(f"tile{i}_loaded") for i in range(4)]
        tile_stored = [sem(f"tile{i}_stored") for i in range(4)]
        tT_done = sem("tT_done")
        tT_high = sem("tT_high")
        tT_low = sem("tT_low")
        tU_done = sem("tU_done")
        tS_done = sem("tS_done")
        tM_done = sem("tM_done")
        tHT_done = sem("tHT_done")
        tH_high = sem("tH_high")
        tH_low = sem("tH_low")
        tY_done = sem("tY_done")
        tile_done = sem("tile_done")
        gathered = [sem(f"gathered{i}") for i in range(4)]
        combined = sem("combined")
        w_high = sem("w_high")
        w_low = sem("w_low")
        up_done = sem("up_done")
        silu_done = sem("silu_done")
        mul_done = sem("mul_done")
        h_high = sem("h_high")
        shared_low = sem("shared_low")
        h_low = sem("h_low")
        down_done = sem("down_done")
        evac_done = sem("evac_done")

        block = ctx.enter_context(nc.Block())

        def wait(eng, s, value):
            if not (isinstance(value, int) and value <= 0):
                eng.wait_ge(s, value)

        def wait_low(eng, value):
            if not isinstance(value, int) or value > U8:
                eng.wait_ge(h_low, value - U8)
            elif value > 0:
                eng.wait_ge(shared_low, value)

        def pairs_done(k):
            return 0 if isinstance(k, int) and k <= 0 else k * 2 + 1

        def f32(ap):
            return ap.bitcast(F32)

        def blocks(t, slot, plain):
            v = t[:, slot, :].rearrange("p (a c) -> p a c", c=BLK)
            return v[:, 0:3:2, :] if plain else v

        @block.sync
        def _(sp):
            xv = dram["x"].rearrange("b (h p) d -> p (b h) d", p=P)
            cv = dram["ctx"].rearrange("b (h p) d -> p (b h) d", p=P)
            sp.dma_start(ident[:, :], dram["ident"]).then_inc(const_loaded, 16)
            sp.dma_start(x[:, :, :], xv).then_inc(x_loaded, 16)
            sp.dma_start(cx[:, :, :], cv).then_inc(ctx_loaded, 16)
            for t, n in ((gwt, "gw"), (gbias, "gbias"), (maskT, "maskT"), (bcv, "bcv"), (cols, "cols"), (iot, "iot"), (tilen, "tilen"),
                         (tri, "tri"), (wg0, "wg0"), (wg1, "wg1"), (alog, "alog"), (nl, "nl")):
                sp.dma_start(t[tuple(slice(None) for _ in t.shape)], dram[n]).then_inc(const_loaded, 16)

            def load(u, slot, src, plain=False):
                wait(sp, w_low, u - 1)
                sp.dma_start(blocks(wS, slot, plain), src.rearrange("p (a c) -> p a c", c=BLK)).then_inc(stage_loaded[slot], 16)

            sp.wait_ge(zero_done, 1)
            zv = xs_d.rearrange("(a p c) d -> a p (c d)", p=P, c=UW // D)
            for a in range(TILES * D // UW):
                sp.dma_start(zv[a], qM[:, 6:12, :].rearrange("p i c -> p (i c)")).then_inc(zeros_stored, 16)
            sp.wait_ge(gates_done, 1)
            sp.wait_ge(vext_done, 1)
            for t, n in ((FZ, "fz"), (FW, "fw"), (GI, "gi"), (Win, "win"), (peT, "pet"), (Wp1, "wp1"), (Wp2, "wp2")):
                sp.dma_start(t[tuple(slice(None) for _ in t.shape)], dram[n]).then_inc(conv_loaded, 16)
            sp.wait_ge(qk_done, B * NH)
            load(0, 0, dram["w0"][0])
            sp.wait_ge(zeros_stored, 16 * (TILES * D // UW))

            def load_expert(e, slot, ready):
                if isinstance(e, int) and e == 2:
                    sp.wait_ge(w_low, 1)
                if ready is not None:
                    sp.wait_ge(ew_ready, ready)
                src = dram["wr"][e] if isinstance(e, int) else dram["wr"][bass.ds(e, 1)].rearrange("a p c -> (a p) c")
                sp.dma_start(eS[:, slot * EW:(slot + 1) * EW], src).then_inc(estage_loaded[slot], 16)

            for e in range(4):
                load_expert(e, (e + 2) % 4, None)
            with sp.Fori(1, E0 // 4) as it:
                for e in range(4):
                    load_expert(it * 4 + e, (e + 2) % 4, it * 4 + (e - 3))
            sp.wait_ge(ew_ready, E0)
            for i in range(4):
                load(U_FA + i, (U_FA + i) % 2, dram["wab"][i], plain=True)
            with sp.Fori(0, N_L1 // 2) as it:
                load(it * 2 + U_L1, 1, dram["w1"][bass.ds(it * 2, 1)].rearrange("a p c -> (a p) c"))
                load(it * 2 + U_L1 + 1, 0, dram["w1"][bass.ds(it * 2 + 1, 1)].rearrange("a p c -> (a p) c"))
            ov = out_d.rearrange("b (h p) d -> p (b h) d", p=P)
            for g in range(4):
                sp.wait_ge(evac_done, 4 * (M_L1 + 4 * N_L1) - 16 + 4 * (g + 1))
                sp.dma_start(ov[:, 4 * g:4 * g + 4, :], x[:, 4 * g:4 * g + 4, :]).then_inc(out_stored, 16)
            sp.wait_ge(out_stored, 64)

        @block.vector
        def _(dve):
            steps = [0]

            def link(ins):
                steps[0] += 1
                ins.then_inc(dve_step, 1)
                dve.wait_ge(dve_step, steps[0])

            lns = [0]

            def layernorm(src, dst, counted=False, between=None):
                if not counted:
                    for n in range(NT):
                        last = dve.bn_stats(st[:, n, :], src[:, n, :])
                    link(last)
                for n in range(NT):
                    last = dve.bn_aggr(mv[:, n, :], st[:, n, :])
                link(last)
                dve.tensor_scalar(ve[:, :], mv[:, :, 1], EPS, None, ALU.add).then_inc(var_done, 1)
                lns[0] += 1
                dve.wait_ge(std_done, lns[0])
                link(dve.reciprocal(rs[:, :], sd[:, :]))
                link(dve.tensor_tensor(nt1[:, :], rs[:, :], rs[:, :], ALU.mult))
                link(dve.tensor_tensor(nt1[:, :], nt1[:, :], ve[:, :], ALU.mult))
                link(dve.tensor_scalar(nt1[:, :], nt1[:, :], -0.5, 1.5, ALU.mult, ALU.add))
                link(dve.tensor_tensor(rs[:, :], rs[:, :], nt1[:, :], ALU.mult))
                for n in range(NT):
                    dve.tensor_scalar(dst[:, n, :], src[:, n, :], mv[:, n, 0:1], rs[:, n:n + 1],
                                      ALU.subtract, ALU.mult).then_inc(norm_done, 1)
                    if between is not None and n % 4 == 3 and n > 4:
                        high_parts(between, [n // 4 - 1])
                if between is not None:
                    high_parts(between, [3])

            def statistics(src, g):
                for n in range(4 * g, 4 * g + 4):
                    last = dve.bn_stats(st[:, n, :], src[:, n, :])
                link(last)

            def layernorm_group(src, dst, g, signal):
                tiles = range(4 * g, 4 * g + 4)
                r = slice(4 * g, 4 * g + 4)
                statistics(src, g)
                for n in tiles:
                    last = dve.bn_aggr(mv[:, n, :], st[:, n, :])
                link(last)
                dve.tensor_scalar(ve[:, r], mv[:, r, 1], EPS, None, ALU.add).then_inc(var_done, 1)
                lns[0] += 1
                dve.wait_ge(std_done, lns[0])
                link(dve.reciprocal(rs[:, r], sd[:, r]))
                link(dve.tensor_tensor(nt1[:, r], rs[:, r], rs[:, r], ALU.mult))
                link(dve.tensor_tensor(nt1[:, r], nt1[:, r], ve[:, r], ALU.mult))
                link(dve.tensor_scalar(nt1[:, r], nt1[:, r], -0.5, 1.5, ALU.mult, ALU.add))
                link(dve.tensor_tensor(rs[:, r], rs[:, r], nt1[:, r], ALU.mult))
                for n in tiles:
                    last = dve.tensor_scalar(dst[:, n, :], src[:, n, :], mv[:, n, 0:1], rs[:, n:n + 1], ALU.subtract, ALU.mult)
                    if signal:
                        last.then_inc(norm_done, 1)
                if not signal:
                    link(last)

            dve.wait_ge(x_loaded, 16)
            layernorm(x, xn)
            dve.memset(ones[:, :], 1.0)
            dve.wait_ge(ctx_loaded, 16)
            dve.memset(vext[:, :, :, DH:DH + 1], 1.0)
            dve.tensor_copy(vext[:, :, :, 0:DH], cx[:, :, :].rearrange("p n (h d) -> p n h d", h=NH)).then_inc(vext_done, 1)
            dve.wait_ge(id2_done, 1)
            dve.tensor_copy(sel[:, :, :], id2[:, :].unsqueeze(2).to_broadcast([P, 64, P])).then_inc(sel_done, 1)
            dve.wait_ge(gates_copied, 1)
            dve.scalar_tensor_tensor(r1[64:, :], rg[64:, :], -1.0, rg[64:, :], ALU.mult, ALU.min).then_inc(negabs_done, 1)
            dve.wait_ge(softplus_done, 2)
            link(dve.scalar_tensor_tensor(r1[64:, :], rg[64:, :], 0.0, r3[64:, :], ALU.min, ALU.subtract))
            dve.tensor_tensor_scan(rF[64:, :], ones[64:, :], r1[64:, :], 0.0, ALU.mult, ALU.add).then_inc(logf_done, 1)
            dve.wait_ge(logf_moved, 1)
            link(dve.tensor_tensor(AE[0:64, :], rg[0:64, :], rF[0:64, :], ALU.subtract))
            link(dve.tensor_tensor_scan(rM[0:64, :], AE[0:64, :], AE[0:64, :], -3.0e38, ALU.max, ALU.max))
            link(dve.tensor_tensor(r3[0:64, :], rF[0:64, :], rM[0:64, :], ALU.add))
            dve.tensor_scalar(AE[64:, :], r3[0:64, :], -1.0, None, ALU.mult)
            link(dve.tensor_scalar(r1[0:64, :], rM[0:64, :], -1.0, None, ALU.mult))
            link(dve.tensor_copy(MHL[0:64, :], r1[0:64, :]))
            link(dve.tensor_tensor(r2[0:64, :], r1[0:64, :], f32(MHL[0:64, :]), ALU.subtract))
            dve.tensor_copy(MHL[64:, :], r2[0:64, :]).then_inc(rows_done, 1)

            def head_normaliser(b, o):
                dve.wait_ge(pv_done, 8 * (b + 1))
                link(dve.tensor_copy(den[:, :, :], o[:, :, :, DH]))
                link(dve.scalar_tensor_tensor(den[:, :, :], den[:, :, :], -1.0, den[:, :, :], ALU.mult, ALU.max))
                link(dve.tensor_tensor(den[:, :, :], den[:, :, :], eE[:, :, 8 * b:8 * b + 8], ALU.max))
                link(dve.tensor_scalar(den[:, :, :], den[:, :, :], 1e-6, None, ALU.add))
                link(dve.reciprocal(den[:, :, :], den[:, :, :]))

            def head_work(b, part):
                o = ps[:, 4 + 2 * (b % 2):6 + 2 * (b % 2), 0:NH * (DH + 1)].rearrange("p s (h d) -> p s h d", h=NH)
                v = hN[:, b % 2, :].rearrange("p (s h d) -> p s h d", s=2, h=NH)
                if part == 0:
                    head_normaliser(b, o)
                if part == 1:
                    wait(dve, head_centred, b - 1)
                    dve.tensor_tensor(v, o[:, :, :, 0:DH], den[:, :, :].unsqueeze(3).to_broadcast([P, 2, NH, DH]),
                                      ALU.mult).then_inc(head_read, 1)
                if part == 2:
                    dve.wait_ge(head_read, b + 1)
                    link(dve.tensor_reduce(mean[:, b % 2, :, :], v, AXX, ALU.add))
                    dve.tensor_scalar(mean[:, b % 2, :, :], mean[:, b % 2, :, :], 1.0 / DH, None, ALU.mult).then_inc(head_scaled, 1)
                if part == 3:
                    dve.wait_ge(head_squared, b + 1)
                    q = hQ[:, b % 2, :].rearrange("p (s h d) -> p s h d", s=2, h=NH)
                    link(dve.tensor_reduce(var[:, b, :, :], q, AXX, ALU.add))
                    dve.tensor_scalar(var[:, b, :, :], var[:, b, :, :], 1.0 / DH, EPS, ALU.mult, ALU.add).then_inc(head_var, 1)

            for i in range(B * NH):
                dve.wait_ge(qk_done, i + 1)
                dve.wait_ge(decay_done, i + 1)
                wait(dve, pv_done, i - 2)
                dve.scalar_tensor_tensor(Cm[:, i % 3, :], ps[:, i % 2, 0:384], float(DH) ** -0.5, Dm[:, i % 2, :],
                                         ALU.mult, ALU.mult).then_inc(mixed_done, 1)
                if i >= 8 and i % 8 in (2, 3, 4, 7):
                    head_work(i // 8 - 1, (2, 3, 4, 7).index(i % 8))
            for part in range(4):
                head_work(B - 1, part)

            dve.wait_ge(const_loaded, 13 * 16)
            dve.wait_ge(window_done, 3)
            dve.wait_ge(pos2_done, 1)
            p2 = ps[:, 4:6, :].rearrange("p a (c d) -> p (a c) d", d=D)
            link(dve.tensor_tensor(wf[:, :, :], p2, bcv[:, 6:7, :].to_broadcast([P, 4, D]), ALU.add))
            for k in range(4):
                last = dve.tensor_scalar(wf[:, k, :], wf[:, k, :], wnd[:, k:k + 1], None, ALU.mult)
            last.then_inc(filt_done, 1)
            for b in range(B):
                dve.wait_ge(zlin_done, b + 1)
                last = dve.tensor_tensor(zn[:, b, :, :], ps[:, b, :].rearrange("p (r d) -> p r d", r=2),
                                         bcv[:, 3:4, :].to_broadcast([P, 2, D]), ALU.add)
                last.then_inc(zlin_copied, 1)
            dve.wait_ge(zlin_copied, B)
            zt = zn[:, :, :, :].rearrange("p b r d -> p (b r) d")
            for g in range(4):
                layernorm_group(zt, zt, g, False)
                v = zt[:, 4 * g:4 * g + 4, :]
                link(dve.tensor_tensor(v, v, bcv[:, 4:5, :].to_broadcast([P, 4, D]), ALU.mult))
                dve.tensor_tensor(v, v, bcv[:, 5:6, :].to_broadcast([P, 4, D]), ALU.add).then_inc(zaff_dve, 1)

            dve.wait_ge(filtF_copied, 1)
            dve.wait_ge(head_added, B)

            for n in range(8):
                fh = n % 2
                dve.wait_ge(zF_copied, n + 1)
                wait(dve, inv_done, n - 1)
                for out, t, first, terms in ((PR, tv, 0, ((0, 0, None), (1, 1, ALU.subtract), (0, 0, ALU.add), (1, 1, ALU.subtract))),
                                             (PI, tv, IM_POOL, ((0, 1, None), (1, 0, ALU.add), (0, 1, ALU.add), (1, 0, ALU.add)))):
                    z = Zs[0:FT, n % 2, :, :].rearrange("p a (b d) -> p a b d", b=2)[:, :, :, first:]
                    o = out[0:FT, n % 2, :].rearrange("p (b d) -> p b d", b=2)[:, :, first:]
                    for s, (zi, wi, op) in enumerate(terms):
                        w = WF[0:FT, s // 2, 2 * wi + fh:2 * wi + fh + 1, first:].to_broadcast([FT, 2, D - first])
                        dst = o if s == 0 else t[0:FT, s % 2, :].rearrange("p (b d) -> p b d", b=2)[:, :, first:]
                        link(dve.tensor_tensor(dst, z[:, 2 * (s // 2) + zi], w, ALU.mult))
                        if s:
                            last = dve.tensor_tensor(o, o, dst, op)
                            if s < 3 or first == 0:
                                link(last)
                last.then_inc(prod_dve, 1)

            def split_gates():
                link(dve.tensor_copy(wg0H[:, :, :], wg0[:, :, :]))
                link(dve.tensor_tensor(wg0L[:, :, :], wg0[:, :, :], f32(wg0H[:, :, :]), ALU.subtract))
                link(dve.tensor_copy(wg1H[:, :, :], wg1[:, :, :]))
                dve.tensor_tensor(wg1L[:, :, :], wg1[:, :, :], f32(wg1H[:, :, :]), ALU.subtract).then_inc(gate_split, 1)

            def high_parts(r, groups=range(4)):
                for j in range(2 * groups[0], 2 * groups[-1] + 2):
                    g, c = j // 2, j % 2
                    dve.wait_ge(xT_copied, 8 * r + j + 1)
                    dve.tensor_copy(xTH[:, c, g * 512:(g + 1) * 512], tF[:, j % 2, :]).then_inc(xT_high, 1)

            def step(n, b, muls):
                if muls is not None:
                    wait_low(dve, n - 1)
                    dve.wait_ge(silu_done, n + 1)
                    dve.tensor_tensor(hF[:, b, :], sg[:, b, :], ps[:, 2 + b, :], ALU.mult).then_inc(mul_done, 1)
                    dve.wait_ge(mul_done, n + 1 - muls)
                else:
                    dve.wait_ge(silu_done, n + 1)
                wait(dve, down_done, n - 1)
                dve.tensor_copy(hH[:, b, :], hF[:, b, :]).then_inc(h_high, 1)

            def evacuate(m, n, g, pair, dst, scale):
                dve.wait_ge(down_done, n + 1)
                wait(dve, evac_done, m * 4)
                for t in range(4):
                    tile = 4 * g + t
                    acc = ps[:, 4 + 2 * pair + t // 2, (t % 2) * 256:(t % 2) * 256 + 256]
                    if scale is None:
                        last = dve.tensor_tensor(dst[:, tile, :], acc, dst[:, tile, :], ALU.add)
                    else:
                        last = dve.scalar_tensor_tensor(dst[:, tile, :], acc, scale(tile), dst[:, tile, :], ALU.mult, ALU.add)
                    last.then_inc(evac_done, 1)

            split_gates()
            for g in range(4):
                statistics(x, g)
            dve.wait_ge(inv_copied, 8)
            layernorm(x, xn, counted=True, between=0)
            lg = ps[:, 4, :].rearrange("p (n e) -> p n e", n=NT)
            m1 = sm[:, :, 0]

            def bc(ap, k):
                return ap.unsqueeze(2).to_broadcast([P, NT, k])

            dve.wait_ge(logits_done, 1)
            link(dve.tensor_reduce(m1, lg, AXX, ALU.max))
            dve.tensor_tensor(sc0[:, :, :], lg, bc(m1, E0), ALU.subtract).then_inc(shifted_done, 1)
            dve.wait_ge(exp_done, 1)
            link(dve.tensor_reduce(m1, sc0[:, :, :], AXX, ALU.add))
            link(dve.reciprocal(m1, m1))
            link(dve.tensor_tensor(sc0[:, :, :], sc0[:, :, :], bc(m1, E0), ALU.mult))
            for n in range(NT):
                last = dve.max(mx8[:, n, :], sc0[:, n, :])
            link(last)
            for n in range(NT):
                last = dve.max_index(ix8[:, n, :], mx8[:, n, :], sc0[:, n, :])
            link(last)
            link(dve.tensor_copy(ixf[:, :, :], ix8[:, :, :]))
            io = iot[:, :].unsqueeze(1).to_broadcast([P, NT, E0])
            link(dve.tensor_tensor(sc1[:, :, :], io, bc(ixf[:, :, 0], E0), ALU.is_equal))
            for k in range(1, TOPK):
                link(dve.tensor_tensor(sc2[:, :, :], io, bc(ixf[:, :, k], E0), ALU.is_equal))
                link(dve.tensor_tensor(sc1[:, :, :], sc1[:, :, :], sc2[:, :, :], ALU.add))
            dve.tensor_copy(selm[:, :, :], sc1[:, :, :]).then_inc(chosen_done, 1)
            dve.wait_ge(counts_done, 1)
            link(dve.memset(sc2[:, 0, :], 0.0))
            tot = ps[:, 5, :].rearrange("p (n e) -> p n e", n=NT)
            for n in range(1, NT):
                link(dve.tensor_tensor(sc2[:, n, :], sc2[:, n - 1, :], tot[:, n - 1, :], ALU.add))
            link(dve.tensor_tensor(rt[:, 0, :], sc2[:, NT - 1, :], tot[:, NT - 1, :], ALU.add))
            dve.tensor_tensor(sc2[:, :, :], ps[:, 6, :].rearrange("p (n e) -> p n e", n=NT), sc2[:, :, :], ALU.add).then_inc(counts_read, 1)
            dve.wait_ge(counts_read, 1)
            link(dve.tensor_scalar(rt[:, 0, :], rt[:, 0, :], float(CAP), None, ALU.min))
            link(dve.tensor_scalar(cmp8[:, 0, :], tilen[:, 0:8], float(P), None, ALU.mult))
            link(dve.tensor_copy(cmp8[:, 1:E0, :], cmp8[:, 0:1, :].to_broadcast([P, E0 - 1, 8])))
            link(dve.tensor_tensor(cmp8[:, :, :], rt[:, 0, :].unsqueeze(2).to_broadcast([P, E0, 8]), cmp8[:, :, :], ALU.is_gt))
            link(dve.tensor_reduce(rt[:, 1, :], cmp8[:, :, :], AXX, ALU.add))
            link(dve.memset(rt[:, 0, :], 1.0))
            link(dve.tensor_tensor_scan(rt[:, 2, :], rt[:, 0, :], rt[:, 1, :], 0.0, ALU.mult, ALU.add))
            link(dve.tensor_tensor(rt[:, 3, :], rt[:, 2, :], rt[:, 1, :], ALU.subtract))
            link(dve.tensor_scalar(rt[:, 3, :], rt[:, 3, :], float(P), None, ALU.mult))
            link(dve.tensor_scalar(sc3[:, :, :], sc2[:, :, :], float(CAP), FAR, ALU.is_ge, ALU.mult))
            link(dve.tensor_tensor(sc2[:, :, :], sc2[:, :, :], sc3[:, :, :], ALU.add))
            link(dve.tensor_tensor(sc2[:, :, :], sc2[:, :, :], rt[:, 3:4, :].to_broadcast([P, NT, E0]), ALU.add))
            for k in range(TOPK):
                link(dve.tensor_tensor(sc1[:, :, :], io, bc(ixf[:, :, k], E0), ALU.is_equal))
                link(dve.tensor_tensor(sc1[:, :, :], sc1[:, :, :], sc2[:, :, :], ALU.mult))
                link(dve.tensor_reduce(slk[:, :, k], sc1[:, :, :], AXX, ALU.add))
                dve.tensor_copy(idS[:, :, k], slk[:, :, k]).then_inc(slots_done, 1)
            link(dve.tensor_scalar(okk[:, :, :], slk[:, :, :], 0.5 * FAR, None, ALU.is_lt))
            dve.tensor_tensor(wk[:, :, :], mx8[:, :, 0:TOPK], okk[:, :, :], ALU.mult)
            link(dve.tensor_tensor(slk[:, :, :], slk[:, :, :], okk[:, :, :], ALU.mult))
            dve.tensor_copy(idG[:, :, :], slk[:, :, :]).then_inc(slots_done, 1)
            link(dve.tensor_tensor(cmpt[:, :, :], rt[0:1, 2:3, :].to_broadcast([1, TILES, E0]),
                                   tilen[0:1, :].unsqueeze(2).to_broadcast([1, TILES, E0]), ALU.is_le))
            link(dve.tensor_reduce(etf[:, 0, :], cmpt[:, :, :], AXX, ALU.add))
            link(dve.tensor_scalar(etf[:, 0, :], etf[:, 0, :], float(E0 - 1), None, ALU.min))
            quads = cmpt[:, :, 0:8]
            link(dve.tensor_scalar(rt[0:1, 0, 0:8], tilen[0:1, 0:8], 4.0, 2.0, ALU.mult, ALU.add))
            link(dve.tensor_tensor(quads, etf[:, 0, :].unsqueeze(2).to_broadcast([1, TILES, 8]),
                                   rt[0:1, 0:1, 0:8].to_broadcast([1, TILES, 8]), ALU.is_ge))
            link(dve.tensor_reduce(etf[:, 1, :], quads, AXX, ALU.add))
            link(dve.scalar_tensor_tensor(etf[:, 1, :], etf[:, 1, :], -4.0, etf[:, 0, :], ALU.mult, ALU.add))
            link(dve.tensor_scalar(etf[:, 1, :], etf[:, 1, :], 2.0, None, ALU.add))
            link(dve.scalar_tensor_tensor(etf[:, 1, 0:PAIRS], etf[:, 1, 1::2], 16.0, etf[:, 1, 0::2], ALU.mult, ALU.add))
            link(dve.tensor_scalar(etf[:, 1, 0:PAIRS], etf[:, 1, 0:PAIRS], float(EW // D * 256), None, ALU.mult))
            link(dve.tensor_scalar(wordf[:, 0:PAIRS], etf[:, 0, 1::2], 1.0, None, ALU.add))
            link(dve.memset(wordf[:, PAIRS:], 0.0))
            link(dve.tensor_tensor(wordf[:, 0:PAIRS], wordf[:, 0:PAIRS], etf[:, 1, 0:PAIRS], ALU.add))
            link(dve.scalar_tensor_tensor(wordf[:, 2:], etf[:, 1, 0:PAIRS], 256.0, wordf[:, 2:], ALU.mult, ALU.add))
            link(dve.tensor_scalar(rt[0:1, 3, :], rt[0:1, 2, :], 1.0, None, ALU.add))
            dve.tensor_copy(ptab[:, :], rt[0:1, 3, :])
            dve.tensor_copy(words[:, :], wordf[:, :]).then_inc(table_done, 1)

            for i in range(8):
                step(i, i % 2, 0)
                dve.wait_ge(h_high, i + 1)
                dve.tensor_tensor(hL[:, i % 2, :], hF[:, i % 2, :], f32(hH[:, i % 2, :]), ALU.subtract).then_inc(shared_low, 1)
                if i in (2, 4, 6):
                    evacuate(i // 2 - 1, i - 1, i // 2 - 1, (i // 2 - 1) % 2, x, None)
            evacuate(3, 7, 3, 1, x, None)
            dve.wait_ge(evac_done, 4 * M_FA)

            def tile_low(q, b):
                dve.wait_ge(tT_high, q + 1)
                wait(dve, tU_done, q - 1)
                dve.tensor_tensor(hL[:, b, :], ps[:, b, :], f32(hH[:, b, :]), ALU.subtract).then_inc(tT_low, 1)

            def tile_mul(q, b):
                dve.wait_ge(tS_done, q + 1)
                wait(dve, tHT_done, q - 1)
                dve.tensor_tensor(rh[:, b, :, :], rs_[:, b, :, :], ps[:, 2 + b, :].rearrange("p (t c) -> p t c", t=2)[:, :, P:],
                                  ALU.mult).then_inc(tM_done, 1)

            def hidden_low(q, b):
                dve.wait_ge(tH_high, q + 1)
                wait(dve, tile_done, pairs_done(q - 1))
                dve.tensor_tensor(rhL[:, b, :, :], ps[:, 4 + b, 0:D].rearrange("p (t c) -> p t c", t=2), f32(rhH[:, b, :, :]),
                                  ALU.subtract).then_inc(tH_low, 1)

            def tile_out(q, b, ring, stored):
                dve.wait_ge(tile_done, pairs_done(q + 1))
                if stored is not None:
                    dve.wait_ge(tile_stored[ring], stored)
                dve.tensor_copy(yo[:, ring, :, :], ps[:, 6 + b, :].rearrange("p (t d) -> p t d", t=2)).then_inc(tY_done, 1)

            tile_low(0, 0)
            tile_low(1, 1)
            tile_mul(0, 0)

            def body(it, first=False, last=False):
                for j in range(4):
                    q = it * 4 + j
                    if not (last and j >= 2):
                        tile_low(q + 2, j % 2)
                    if not (last and j == 3):
                        tile_mul(q + 1, (j + 1) % 2)
                    hidden_low(q, j % 2)
                    if not (first and j == 0):
                        ring = (j + 3) % 4
                        filled = it if j else it - 1
                        tile_out(q - 1, (j + 1) % 2, ring, None if first or (isinstance(filled, int) and filled < 1) else filled * 16)

            body(0, first=True)
            body(1)
            with dve.Fori(2, PAIRS // 4 - 1) as it:
                body(it)
            body(PAIRS // 4 - 1, last=True)
            tile_out(PAIRS - 1, 1, 3, (PAIRS // 4 - 1) * 16)
            for n in range(NT):
                dve.wait_ge(gathered[n % 4], 64 * (n // 4 + 1))
                for k in range(TOPK):
                    last = dve.scalar_tensor_tensor(x[:, n, :], yg[:, n % 4, k, :], wk[:, n, k:k + 1], x[:, n, :], ALU.mult, ALU.add)
                    if k < TOPK - 1:
                        link(last)
                last.then_inc(combined, 1)
                if n % 4 == 1 and n > 4:
                    high_parts(1, [n // 4 - 1])
                if n % 4 == 3:
                    g = n // 4
                    dve.wait_ge(combined, n + 1)
                    layernorm_group(x, ya, g, False)
                    layernorm_group(ya, xn, g, True)
            high_parts(1, [3])

            def dense(u0, m0, biases, after):
                for i in range(16):
                    step(8 * u0 + i, i % 2, None)
                    if i % 2 == 0 and i:
                        g = i // 2 - 1
                        if g < 4:
                            dve.wait_ge(bias_added, biases + g + 1)
                        evacuate(m0 + g, 8 * u0 + i - 1, g % 4, g % 2, ya, None)
                    if i > 10 and i % 2:
                        after(i // 2 - 5)
                evacuate(m0 + 7, 8 * u0 + 15, 3, 1, ya, None)
                after(3)

            def times_filtered(g):
                t = ya[:, 4 * g:4 * g + 4, :]
                dve.wait_ge(evac_done, 4 * (M_FB - 3 + g))
                link(dve.tensor_tensor(t, t, dcw[:, 4 * g:4 * g + 4, :], ALU.mult))
                statistics(ya, g)

            def add_residual(g):
                t = x[:, 4 * g:4 * g + 4, :]
                dve.wait_ge(evac_done, 4 * (M_L1 - 3 + g))
                link(dve.tensor_tensor(t, t, ya[:, 4 * g:4 * g + 4, :], ALU.add))
                statistics(x, g)

            dense(U_FA, M_FA, 0, times_filtered)
            layernorm(ya, xn, counted=True, between=2)
            dense(U_FB, M_FB, 4, add_residual)
            layernorm(x, xn, counted=True, between=3)
            l1 = ps[:, 4, 0:NT * 16].rearrange("p (n a e) -> p n a e", n=NT, a=2)
            s1 = sc0[:, :, 0:16].rearrange("p n (a e) -> p n a e", a=2)
            smb = sm[:, :, :].unsqueeze(3).to_broadcast([P, NT, 2, E1])
            dve.wait_ge(logits_done, 2)
            link(dve.tensor_reduce(sm[:, :, :], l1, AXX, ALU.max))
            link(dve.tensor_tensor(s1, l1, smb, ALU.subtract))
            dve.tensor_scalar(s1[:, :, 1, :], s1[:, :, 1, :], 10.0, None, ALU.mult).then_inc(shifted_done, 1)
            dve.wait_ge(exp_done, 2)
            link(dve.tensor_reduce(sm[:, :, :], s1, AXX, ALU.add))
            link(dve.reciprocal(sm[:, :, :], sm[:, :, :]))
            link(dve.tensor_tensor(s1, s1, smb, ALU.mult))
            link(dve.tensor_tensor(sc1[:, :, 0:8], s1[:, :, 0, :], s1[:, :, 1, :], ALU.mult))
            link(dve.tensor_reduce(sm2[:, :], sc1[:, :, 0:8], AXX, ALU.add))
            link(dve.tensor_scalar(sm2[:, :], sm2[:, :], 1e-9, None, ALU.add))
            link(dve.reciprocal(sm2[:, :], sm2[:, :]))
            for a in range(2):
                last = dve.tensor_tensor(cw2[:, :, a:16:2], sc1[:, :, 0:8], bc(sm2[:, :], E1), ALU.mult)
            last.then_inc(cw_done, 1)
            dve.wait_ge(cw_done, 1)
            with dve.Fori(0, N_L1 // 2) as it:
                def mixed(local):
                    evacuate(it * 8 + (M_L1 + local // 2), it * 16 + (8 * U_L1 + local), local // 2 % 4, local // 2 % 2, x,
                             lambda tile: cw2[:, tile, bass.ds(it, 1)])
                for local in range(16):
                    step(it * 16 + (8 * U_L1 + local), local % 2, PLAIN)
                    if local and local % 2 == 0:
                        mixed(local - 1)
                mixed(15)

        @block.scalar
        def _(act):
            lns = [0]

            def deviation():
                lns[0] += 1
                act.wait_ge(var_done, lns[0])
                act.activation(sd[:, :], ve[:, :], ACT.Sqrt).then_inc(std_done, 1)

            def deviation_group(g):
                lns[0] += 1
                act.wait_ge(var_done, lns[0])
                act.activation(sd[:, 4 * g:4 * g + 4], ve[:, 4 * g:4 * g + 4], ACT.Sqrt).then_inc(std_done, 1)

            def mix_copy(j, dst):
                act.wait_ge(mixT_done, j + 1)
                act.activation(dst, ps[:, j % 4, :], ACT.Identity).then_inc(mixT_copied, 1)

            for j in range(8):
                mix_copy(j, kT[:, j % 2, (j // 2) * 512:(j // 2 + 1) * 512])
            deviation()
            for j in range(8):
                mix_copy(8 + j, qT[:, j % 2, (j // 2) * 512:(j // 2 + 1) * 512])
            act.wait_ge(gates_done, 1)
            act.wait_ge(const_loaded, 13 * 16)
            act.activation(rg[:, :], ps[:, 4, 0:256], ACT.Identity, bias=gbias[:, :]).then_inc(gates_copied, 1)
            act.wait_ge(negabs_done, 1)
            act.activation(r2[64:, :], r1[64:, :], ACT.Exp).then_inc(softplus_done, 1)
            act.wait_ge(softplus_done, 1)
            act.activation(r3[64:, :], r2[64:, :], ACT.Ln, bias=1.0).then_inc(softplus_done, 1)
            act.wait_ge(logf_done, 1)
            act.activation(rF[0:64, :], rF[64:, :], ACT.Copy).then_inc(logf_moved, 1)
            act.wait_ge(rowsT_done, 1)
            rT = ps[:, 5, 0:256].rearrange("p (h r) -> p h r", h=2)
            act.activation(aT[:, :, :], rT[:, :, 0:64], ACT.Copy)
            act.activation(eE[:, :, :], rT[:, :, 64:128], ACT.Exp).then_inc(rowsT_copied, 1)
            act.wait_ge(rowsT_copied, 1)

            def square(b):
                act.wait_ge(head_centred, b + 1)
                wait(act, head_var, b - 1)
                act.activation(hQ[:, b % 2, :], hC[:, b, :], ACT.Square).then_inc(head_squared, 1)

            for i in range(B * NH):
                act.wait_ge(arg_done, i + 1)
                wait(act, mixed_done, i - 1)
                act.activation(Dm[:, i % 2, 0:256], ps[:, 2 + i % 2, 0:256], ACT.Exp, bias=aT[:, 0, i:i + 1])
                act.activation(Dm[:, i % 2, 256:384], ps[:, 2 + i % 2, 256:384], ACT.Exp, bias=aT[:, 1, i:i + 1]).then_inc(decay_done, 1)
                if i >= 8 and i % 8 == 6:
                    square(i // 8 - 1)
            square(B - 1)
            act.wait_ge(head_var, B)
            act.activation(rstd[:, :, :, :], var[:, :, :, :], ACT.Ln).then_inc(head_rstd, 1)
            act.wait_ge(head_rstd, 1)
            act.activation(rstd[:, :, :, :], rstd[:, :, :, :], ACT.Exp, scale=-0.5).then_inc(head_rstd, 1)

            act.activation(ea[:, :], alog[:, :], ACT.Exp).then_inc(window_done, 1)
            act.wait_ge(window_done, 1)
            act.activation(wnd[:, :], nl[:, :], ACT.Exp, scale=ea[:, :]).then_inc(window_done, 1)
            act.wait_ge(pos1_done, 1)
            for k in range(3):
                rows = P if k < 2 else 64
                last = act.activation(h1T[0:rows, k, :], ps[0:rows, k, :], ACT.Silu, bias=cols[0:rows, 16 + k:17 + k])
            last.then_inc(pos1_silu, 1)
            act.wait_ge(window_done, 2)
            act.activation(ea[:, :], alog[:, :], ACT.Copy).then_inc(window_done, 1)
            act.wait_ge(filtF_done, 1)
            act.activation(WF[0:FT, :, :, :].rearrange("p e f d -> p (e f d)"), ps[0:FT, 0:4, :].rearrange("p a c -> p (a c)"),
                           ACT.Copy).then_inc(filtF_copied, 1)
            for g in range(4):
                deviation_group(g)

            def inverse_copy(q):
                for h in range(2):
                    act.wait_ge(inv_done, 2 * (q + 1))
                    act.activation(dcw[:, 4 * q + h:4 * q + 4:2, :], ps[:, 4 + 2 * (q % 2) + h, :].rearrange("p (b d) -> p b d", b=2),
                                   ACT.Copy).then_inc(inv_copied, 1)

            act.wait_ge(head_added, B)
            for n in range(8):
                act.wait_ge(zF_done, n + 1)
                wait(act, prod_dve, n - 1)
                wait(act, prod_pool, n - 1)
                act.activation(Zs[0:FT, n % 2, :, :], ps[0:FT, 0:4, :], ACT.Copy).then_inc(zF_copied, 1)
                if n >= 2 and n % 2 == 0:
                    inverse_copy(n // 2 - 1)
            inverse_copy(3)

            def transposed(r, gain=None, offset=None, groups=range(4)):
                for j in range(2 * groups[0], 2 * groups[-1] + 2):
                    c = j % 2
                    act.wait_ge(xT_done, 8 * r + j + 1)
                    wait(act, xT_high, 8 * r + j - 1)
                    wait(act, xT_low, 8 * r + j - 1)
                    if gain is None:
                        last = act.activation(tF[:, c, :], ps[:, j % 4, :], ACT.Identity)
                    else:
                        last = act.activation(tF[:, c, :], ps[:, j % 4, :], ACT.Identity,
                                              scale=cols[:, gain + c:gain + c + 1], bias=cols[:, offset + c:offset + c + 1])
                    last.then_inc(xT_copied, 1)

            def copy_logits(q, width):
                for g in range(4):
                    act.wait_ge(logitsT_done, 4 * q + g + 1)
                    act.activation(lgT[0:width, g * 512:(g + 1) * 512], ps[0:width, 4 + g, :], ACT.Copy).then_inc(logitsT_copied, 1)

            def split_high(u, slot, loaded, plain=False):
                act.wait_ge(stage_loaded[slot], loaded)
                if isinstance(u, int) and u in (1, 2):
                    act.wait_ge(tile_done, TILES + 1)
                wait(act, down_done, (u - 1) * 8)
                act.activation(blocks(wH, slot, plain), blocks(wS, slot, plain), ACT.Copy).then_inc(w_high, 1)

            def silu(n, b, muls):
                wait(act, mul_done, n - 1 - muls)
                act.wait_ge(up_done, n + 1)
                act.activation(sg[:, b, :], ps[:, b, :], ACT.Silu).then_inc(silu_done, 1)

            deviation()
            transposed(0)
            copy_logits(0, E0)
            act.wait_ge(shifted_done, 1)
            act.activation(sc0[:, :, :], sc0[:, :, :], ACT.Exp).then_inc(exp_done, 1)
            split_high(0, 0, 16)
            for i in range(8):
                silu(i, i % 2, 0)
            xsv = xs_d.rearrange("(q t p) d -> q p t d", t=2, p=P)
            ysv = ys_d.rearrange("(q t p) d -> q p t d", t=2, p=P)

            def pair_of(v, q):
                return v[q] if isinstance(q, int) else v[bass.ds(q, 1)].rearrange("a p t d -> (a p) t d")

            def load_pair(q, ring):
                wait(act, tT_done, q - 3)
                act.dma_start(xl[:, ring, :, :], pair_of(xsv, q)).then_inc(tile_loaded[ring], 16)

            def store_pair(q, ring):
                act.wait_ge(tY_done, q + 1)
                act.dma_start(pair_of(ysv, q), yo[:, ring, :, :]).then_inc(tile_stored[ring], 16)

            def tile_high(q, b):
                act.wait_ge(tT_done, q + 1)
                wait(act, tU_done, q - 1)
                act.activation(hH[:, b, :], ps[:, b, :], ACT.Copy).then_inc(tT_high, 1)

            def tile_silu(q, b):
                act.wait_ge(tU_done, q + 1)
                wait(act, tM_done, q - 1)
                act.activation(rs_[:, b, :, :], ps[:, 2 + b, :].rearrange("p (t c) -> p t c", t=2)[:, :, 0:P], ACT.Silu).then_inc(tS_done, 1)

            def hidden_high(q, b):
                act.wait_ge(tHT_done, q + 1)
                wait(act, tile_done, pairs_done(q - 1))
                act.activation(rhH[:, b, :, :], ps[:, 4 + b, 0:D].rearrange("p (t c) -> p t c", t=2), ACT.Copy).then_inc(tH_high, 1)

            act.wait_ge(scattered, 64 * 16)
            act.wait_ge(evac_done, 4 * M_FA)
            wait_low(act, 8)
            act.wait_ge(table_done, 1)
            for q in range(4):
                load_pair(q, q)
            tile_high(0, 0)
            tile_high(1, 1)
            tile_silu(0, 0)

            def body(it, first=False, last=False):
                for j in range(4):
                    q = it * 4 + j
                    if not (last and j >= 2):
                        tile_high(q + 2, j % 2)
                    if not (last and j == 3):
                        tile_silu(q + 1, (j + 1) % 2)
                    hidden_high(q, j % 2)
                    if not last:
                        load_pair(q + 4, j)
                    if not (first and j < 2):
                        store_pair(q - 2, (j + 2) % 4)

            body(0, first=True)
            with act.Fori(1, PAIRS // 4 - 1) as it:
                body(it)
            body(PAIRS // 4 - 1, last=True)
            store_pair(PAIRS - 2, 2)
            store_pair(PAIRS - 1, 3)
            split_high(1, 1, 16, plain=True)

            def dense(u0, bias):
                for i in range(16):
                    n, b, u = 8 * u0 + i, i % 2, u0 + i // 8
                    c = 2 * (i // 8) + i % 2
                    act.wait_ge(up_done, n + 1)
                    wait_low(act, n - 1)
                    act.activation(hF[:, b, :], ps[:, b, :], ACT.Silu, bias=cols[:, bias + c:bias + c + 1]).then_inc(silu_done, 1)
                    if i % 8 == 1:
                        split_high(u + 1, (u + 1) % 2, 16 * ((u + 1) // 2 + 1), plain=u + 1 < U_L1)

            for g in range(4):
                deviation_group(g)
                deviation_group(g)
                transposed(1, 0, 2, [g])
            dense(U_FA, 8)
            deviation()
            transposed(2, 4, 6)
            dense(U_FB, 12)
            deviation()
            transposed(3)
            copy_logits(1, 16)
            act.wait_ge(shifted_done, 2)
            s1 = sc0[:, :, 0:16]
            act.activation(s1, s1, ACT.Exp).then_inc(exp_done, 1)

            def experts(it, last):
                for local in range(16):
                    silu(it * 16 + (8 * U_L1 + local), local % 2, PLAIN)
                    if local == 1:
                        split_high(it * 2 + (U_L1 + 1), 0, it * 16 + 16 * (U_L1 // 2 + 2))
                    if local == 9 and not last:
                        split_high(it * 2 + (U_L1 + 2), 1, it * 16 + 16 * (U_L1 // 2 + 2))

            with act.Fori(0, N_L1 // 2 - 1) as it:
                experts(it, False)
            experts(N_L1 // 2 - 1, True)

        @block.gpsimd
        def _(pool):
            steps = [0]

            def link(ins):
                steps[0] += 1
                ins.then_inc(pool_step, 1)
                pool.wait_ge(pool_step, steps[0])

            pool.memset(qM[:, :, :], 0.0).then_inc(zero_done, 1)
            link(pool.memset(zcol[:, :], 0.0))
            link(pool.memset(gateW[:, :, :, :], 0.0))
            pool.wait_ge(const_loaded, 13 * 16)
            link(pool.tensor_tensor(gwt[:, 2:4, :], gwt[:, 2:4, :], gwt[:, 4:6, :], ALU.add))
            for b in range(B):
                for a in range(2):
                    last = pool.tensor_copy(gateW[:, :, b, 64 * a + 8 * b:64 * a + 8 * b + 8], gwt[:, 0:4, 8 * a:8 * a + 8])
            last.then_inc(gatew_done, 1)
            pool.tensor_copy(idb[:, :], ident[:, :])
            pool.tensor_tensor(id2[:, :], ident[:, 0:64], ident[:, 64:128], ALU.add).then_inc(id2_done, 1)
            pool.wait_ge(id2_done, 1)
            def mask_queries(heads):
                for i in heads:
                    if i < B * NH:
                        r, c, t0 = DH * (i % 4), i % NH // 4, i // NH * SEQ
                        wait(pool, qk_done, i - 11)
                        pool.tensor_copy(qM[r:r + DH, i % 12, :], qT[r:r + DH, c, t0:t0 + SEQ]).then_inc(q_masked, 1)
                        pool.wait_ge(q_masked, i + 1)

            pool.wait_ge(mixT_copied, 16)
            pool.wait_ge(zero_done, 1)
            pool.wait_ge(zeros_stored, 16 * (TILES * D // UW))
            def rows_of(ap):
                return ap.rearrange("p s h -> p (s h)").unsqueeze(2).to_broadcast([P, 2 * NH, DH])

            mask_queries(range(10))
            for b in range(B):
                mask_queries(range(8 * b + 10, 8 * b + 18))
                hc = hC[:, b, :].rearrange("p (g d) -> p g d", d=DH)
                pool.wait_ge(head_scaled, b + 1)
                pool.tensor_tensor(hc, hN[:, b % 2, :].rearrange("p (g d) -> p g d", d=DH), rows_of(mean[:, b % 2, :, :]),
                                   ALU.subtract).then_inc(head_centred, 1)
                pool.wait_ge(head_centred, b + 1)
            pool.wait_ge(head_rstd, 2)
            for b in range(B):
                hc = hC[:, b, :].rearrange("p (g d) -> p g d", d=DH)
                link(pool.tensor_tensor(hc, hc, rows_of(rstd[:, b, :, :]), ALU.mult))
                h2 = hC[:, b, :].rearrange("p (s d) -> p s d", s=2)
                link(pool.tensor_tensor(h2, h2, bcv[:, 2:3, :].to_broadcast([P, 2, D]), ALU.mult))
                pool.tensor_tensor(x[:, 2 * b:2 * b + 2, :], x[:, 2 * b:2 * b + 2, :], h2, ALU.add).then_inc(head_added, 1)

            pool.wait_ge(filtF_copied, 1)
            for q in range(4):
                for fh in range(2):
                    n = 2 * q + fh
                    pool.wait_ge(zF_copied, n + 1)
                    wait(pool, inv_done, n - 1)
                    z = Zs[0:FT, n % 2, :, :].rearrange("p a (b d) -> p a b d", b=2)[:, :, :, 0:IM_POOL]
                    o = PI[0:FT, n % 2, :].rearrange("p (b d) -> p b d", b=2)[:, :, 0:IM_POOL]
                    for s, (zi, wi) in enumerate(((0, 1), (1, 0), (0, 1), (1, 0))):
                        w = WF[0:FT, s // 2, 2 * wi + fh:2 * wi + fh + 1, 0:IM_POOL].to_broadcast([FT, 2, IM_POOL])
                        dst = o if s == 0 else tp[0:FT, s % 2, :].rearrange("p (b d) -> p b d", b=2)[:, :, 0:IM_POOL]
                        link(pool.tensor_tensor(dst, z[:, 2 * (s // 2) + zi], w, ALU.mult))
                        if s:
                            last = pool.tensor_tensor(o, o, dst, ALU.add)
                            if s < 3:
                                link(last)
                    last.then_inc(prod_pool, 1)

            def low_parts(r, groups=range(4)):
                for j in range(2 * groups[0], 2 * groups[-1] + 2):
                    g, c = j // 2, j % 2
                    pool.wait_ge(xT_high, 8 * r + j + 1)
                    pool.tensor_tensor(xTL[:, c, g * 512:(g + 1) * 512], tF[:, j % 2, :],
                                       f32(xTH[:, c, g * 512:(g + 1) * 512]), ALU.subtract).then_inc(xT_low, 1)

            def add_bias(r, which, g):
                pool.wait_ge(norm_done, NT * (r + 1) + 4 * g + 4)
                t = ya[:, 4 * g:4 * g + 4, :]
                pool.tensor_tensor(t, t, bcv[:, which:which + 1, :].to_broadcast([P, 4, D]), ALU.add).then_inc(bias_added, 1)

            def split_low(u, slot, plain=False):
                pool.wait_ge(w_high, u + 1)
                pool.tensor_tensor(blocks(wL, slot, plain), blocks(wS, slot, plain), f32(blocks(wH, slot, plain)),
                                   ALU.subtract).then_inc(w_low, 1)

            def low(n, b):
                pool.wait_ge(h_high, n + 1)
                pool.tensor_tensor(hL[:, b, :], hF[:, b, :], f32(hH[:, b, :]), ALU.subtract).then_inc(h_low, 1)

            def split_expert(ring, e, loaded, ahead):
                cols_ = slice(ring * EW, (ring + 1) * EW)
                if ahead is not None:
                    pool.wait_ge(tile_done, pool.value_load(ptab[0:1, ahead], min_val=1, max_val=TILES + 1))
                pool.wait_ge(estage_loaded[ring], loaded)
                pool.tensor_tensor(eH[:, cols_], eS[:, cols_], zcol[:, :].to_broadcast([P, EW]), ALU.add).then_inc(ew_high, 1)
                pool.wait_ge(ew_high, e + 1)
                pool.tensor_tensor(eL[:, cols_], eS[:, cols_], f32(eH[:, cols_]), ALU.subtract).then_inc(ew_ready, 1)

            low_parts(0)
            split_low(0, 0)
            for e in range(2):
                split_expert(e + 2, e, 16, None)
            pool.wait_ge(zeros_stored, 16 * (TILES * D // UW))

            def scatter(count):
                for _ in range(count):
                    k, n = sent[0] // NT, sent[0] % NT
                    if n == 0:
                        pool.wait_ge(slots_done, k + 1)
                    pool.indirect_dma_start(xs_d, bass.IndirectOffsetOnAxis(ap=idS[:, n, k:k + 1], axis=0), xn[:, n, :], None,
                                            bounds_check=TILES * P - 1, oob_is_err=False).then_inc(scattered, 16)
                    sent[0] += 1

            sent = [0]
            scatter(NT * TOPK)
            pool.wait_ge(table_done, 1)
            pool.wait_ge(evac_done, 4 * M_FA)
            for e in range(2, 4):
                split_expert(e - 2, e, 16, None)
            with pool.Fori(1, E0 // 4) as it:
                for e in range(4):
                    split_expert((e + 2) % 4, it * 4 + e, it * 16 + 16, bass.ds(it * 4 + (e - 4), 1))
            pool.wait_ge(slots_done, TOPK + 1)
            for i in range(4):
                pool.wait_ge(tile_stored[i], PAIRS // 4 * 16)
            for n in range(NT):
                wait(pool, combined, n - 3)
                for k in range(TOPK):
                    pool.indirect_dma_start(yg[:, n % 4, k, :], None, ys_d, bass.IndirectOffsetOnAxis(ap=idG[:, n, k:k + 1], axis=0),
                                            bounds_check=TILES * P - 1, oob_is_err=False).then_inc(gathered[n % 4], 16)
                if n % 4 == 3 and n > 3:
                    low_parts(1, [n // 4 - 1])
            low_parts(1, [3])
            split_low(1, 1, True)

            def dense(u0, r):
                for i in range(16):
                    low(8 * u0 + i, i % 2)
                    if i < 8 and i % 2 == 0:
                        add_bias(r, r - 1, i // 2)
                    if i % 8 == 1:
                        u = u0 + i // 8 + 1
                        split_low(u, u % 2, u < U_L1)

            dense(U_FA, 1)
            low_parts(2)
            dense(U_FB, 2)
            low_parts(3)

            def experts(it, last):
                for local in range(16):
                    low(it * 16 + (8 * U_L1 + local), local % 2)
                    if local == 1:
                        split_low(it * 2 + (U_L1 + 1), 0)
                    if local == 9 and not last:
                        split_low(it * 2 + (U_L1 + 2), 1)

            with pool.Fori(0, N_L1 // 2 - 1) as it:
                experts(it, False)
            experts(N_L1 // 2 - 1, True)

        @block.tensor
        def _(pe):
            pe.wait_ge(const_loaded, 13 * 16)
            pe.wait_ge(ctx_loaded, 16)
            for j in range(16):
                src, g, c = (cx, xn)[j // 8], j % 8 // 2, j % 2
                wait(pe, mixT_copied, j - 3)
                if src is xn:
                    pe.wait_ge(norm_done, 4 * g + 4)
                for t in range(4):
                    last = pe.transpose(ps[:, j % 4, t * P:(t + 1) * P], src[:, 4 * g + t, c * P:(c + 1) * P], ident[:, :])
                last.then_inc(mixT_done, 1)
            pe.wait_ge(gatew_done, 1)
            pe.wait_ge(mixT_copied, 16)
            for b in range(B):
                for k in range(4):
                    rhs = (qT, kT)[k // 2][:, k % 2, b * SEQ:(b + 1) * SEQ]
                    last = pe.matmul(ps[:, 4, 0:SEQ], gateW[:, k, b, :], rhs, start=(b == 0 and k == 0), stop=(b == B - 1 and k == 3))
            last.then_inc(gates_done, 1)
            pe.wait_ge(rows_done, 1)
            for h in range(2):
                last = pe.transpose(ps[:, 5, h * P:(h + 1) * P], AE[:, h * P:(h + 1) * P], ident[:, :])
            last.then_inc(rowsT_done, 1)
            pe.wait_ge(sel_done, 1)
            pe.wait_ge(vext_done, 1)
            pe.wait_ge(rowsT_copied, 1)

            def scores(i):
                b, h = i // NH, i % NH
                c = h // 4
                t0 = b * SEQ
                wait(pe, mixed_done, i - 1)
                pe.wait_ge(q_masked, i + 1)
                pe.matmul(ps[:, i % 2, 0:256], kT[:, c, t0:t0 + P], qM[:, i % 12, :], start=True, stop=True)
                pe.matmul(ps[:, i % 2, 256:384], kT[:, c, t0 + P:t0 + SEQ], qM[:, i % 12, P:],
                          start=True, stop=True).then_inc(qk_done, 1)
                wait(pe, decay_done, i - 1)
                pe.matmul(ps[:, 2 + i % 2, 0:384], idb[:, :], maskT[:, :], start=True, stop=False, skip_group_check=True)
                pe.matmul(ps[:, 2 + i % 2, 0:256], sel[:, i, :], MHL[:, :], start=False, stop=False, skip_group_check=True)
                pe.matmul(ps[:, 2 + i % 2, 256:384], sel[:, i, :], MHL[:, P:SEQ], start=False, stop=True,
                          skip_group_check=True).then_inc(arg_done, 1)

            def values(i):
                b, h = i // NH, i % NH
                o0, o1 = (ps[:, 4 + 2 * (b % 2) + s, h * (DH + 1):(h + 1) * (DH + 1)] for s in range(2))
                pe.wait_ge(mixed_done, i + 1)
                if h == 0:
                    wait(pe, head_read, b - 1)
                pe.matmul(o0, Cm[:, i % 3, 0:P], vext[:, 2 * b, h, :], start=True, stop=True)
                pe.matmul(o1, Cm[:, i % 3, P:2 * P], vext[:, 2 * b, h, :], start=True, stop=False)
                pe.matmul(o1, Cm[:, i % 3, 2 * P:3 * P], vext[:, 2 * b + 1, h, :], start=False, stop=True).then_inc(pv_done, 1)

            for i in range(B * NH):
                scores(i)
                if i >= 2:
                    values(i - 2)
            values(B * NH - 2)
            values(B * NH - 1)

            pe.wait_ge(conv_loaded, 7 * 16)
            pe.wait_ge(mixed_done, B * NH)
            pe.wait_ge(decay_done, B * NH)
            for k in range(3):
                rows = P if k < 2 else 64
                last = pe.matmul(ps[0:rows, k, :], Wp1[:, k * P:k * P + rows], peT[:, :], start=True, stop=True)
            last.then_inc(pos1_done, 1)
            pe.wait_ge(pos1_silu, 1)
            pe.wait_ge(head_read, B)
            for lt in range(4):
                first = 256 * (lt % 2) + lt // 2
                for k in range(3):
                    rows = P if k < 2 else 64
                    last = pe.matmul(ps[:, 4 + lt // 2, (lt % 2) * D:(lt % 2 + 1) * D], h1T[0:rows, k, first:first + 255:2],
                                     Wp2[0:rows, k, :], start=k == 0, stop=k == 2)
            last.then_inc(pos2_done, 1)
            pe.wait_ge(filt_done, 1)
            for e in range(2):
                for f in range(4):
                    for k in range(2):
                        last = pe.matmul(ps[0:FT, 2 * e + f // 2, (f % 2) * D:(f % 2 + 1) * D], FW[:, 2 * e + k, f, :],
                                         wf[:, 2 * e + k, :], start=k == 0, stop=k == 1)
            last.then_inc(filtF_done, 1)
            pe.wait_ge(filtF_copied, 1)
            for b in range(B):
                for r in range(2):
                    for k in range(2):
                        last = pe.matmul(ps[:, b, r * D:(r + 1) * D], kT[:, k, b * SEQ + r:(b + 1) * SEQ:2], Win[:, k, :],
                                         start=k == 0, stop=k == 1)
                last.then_inc(zlin_done, 1)

            def inverse(n):
                q, fh = n // 2, n % 2
                pe.wait_ge(prod_dve, n + 1)
                pe.wait_ge(prod_pool, n + 1)
                if fh == 0:
                    wait(pe, inv_copied, 2 * (q - 1))
                for h in range(2):
                    for ri, src in enumerate((PR, PI)):
                        last = pe.matmul(ps[:, 4 + 2 * (q % 2) + h, :], GI[0:FT, 2 * ri + fh, h * P:(h + 1) * P], src[0:FT, n % 2, :],
                                         start=(fh == 0 and ri == 0), stop=(fh == 1 and ri == 1))
                last.then_inc(inv_done, 1)

            pe.wait_ge(zlin_copied, B)
            for n in range(8):
                q, fh = n // 2, n % 2
                pe.wait_ge(zaff_dve, q + 1)
                wait(pe, zF_copied, n)
                for e in range(2):
                    for ri in range(2):
                        last = pe.matmul(ps[0:FT, 2 * e + ri, :].rearrange("p (b d) -> p b d", b=2), FZ[:, 2 * ri + fh, :],
                                         zn[:, 2 * q:2 * q + 2, e, :], start=True, stop=True)
                last.then_inc(zF_done, 1)
                if n:
                    inverse(n - 1)
            inverse(7)

            def transposes(r):
                for j in range(8):
                    g, c = j // 2, j % 2
                    if j >= 4:
                        pe.wait_ge(xT_copied, 8 * r + j - 3)
                    pe.wait_ge(norm_done, NT * (r + 1) + 4 * g + 4)
                    for t in range(4):
                        last = pe.transpose(ps[:, j % 4, t * P:(t + 1) * P], xn[:, 4 * g + t, c * P:(c + 1) * P], ident[:, :])
                    last.then_inc(xT_done, 1)

            def logits(r, q, gH, gL, width):
                pe.wait_ge(gate_split, 1)
                for g in range(4):
                    pe.wait_ge(xT_low, 8 * r + 2 * g + 2)
                    i = 0
                    for k in range(2):
                        for a, w in ((xTH, gH), (xTL, gH), (xTH, gL)):
                            last = pe.matmul(ps[0:width, 4 + g, :], w[:, k, :], a[:, k, g * 512:(g + 1) * 512],
                                             start=i == 0, stop=i == 5)
                            i += 1
                    last.then_inc(logitsT_done, 1)
                pe.wait_ge(logitsT_copied, 4 * (q + 1))
                for n in range(NT):
                    last = pe.transpose(ps[:, 4, n * width:(n + 1) * width], lgT[0:width, n * P:(n + 1) * P],
                                        ident[0:width, 0:width])
                last.then_inc(logits_done, 1)

            def up(n, local, u, slot, muls):
                g, c, b = local % 8 // 2, local % 2, local % 2
                if local % 8 == 0:
                    pe.wait_ge(w_low, u + 1)
                wait(pe, silu_done, n - 1)
                if muls is not None:
                    wait(pe, mul_done, n - 1 - muls)
                for half in range(2 if muls is not None else 1):
                    q = 0
                    for k in range(2):
                        col = half * BLK + k * D + c * P
                        for w, v in ((wH, xTH), (wL, xTH), (wH, xTL)):
                            last = pe.matmul(ps[:, 2 * half + b, :], w[:, slot, col:col + P], v[:, k, g * 512:(g + 1) * 512],
                                             start=q == 0, stop=q == 5)
                            q += 1
                last.then_inc(up_done, 1)

            def down(n, local, m, slot, pair, opens, closes):
                c, b = local % 2, local % 2
                wait_low(pe, n + 1)
                if opens:
                    wait(pe, evac_done, (m - 1) * 4)
                for t in range(4):
                    o = ps[:, 4 + 2 * pair + t // 2, (t % 2) * D:(t % 2 + 1) * D]
                    col = 2 * BLK + c * D
                    for q, (h, w) in enumerate(((hH, wH), (hL, wH), (hH, wL))):
                        last = pe.matmul(o, h[:, b, t * P:(t + 1) * P], w[:, slot, col:col + D],
                                         start=(opens and t % 2 == 0 and q == 0), stop=(closes and q == 2), skip_group_check=True)
                last.then_inc(down_done, 1)

            transposes(0)
            logits(0, 0, wg0H, wg0L, E0)
            pe.wait_ge(chosen_done, 1)
            rhs = selm[:, :, :].rearrange("p n e -> p (n e)")
            pe.matmul(ps[:, 6, :], tri[:, 0, :], rhs, start=True, stop=True)
            pe.matmul(ps[:, 5, :], tri[:, 1, :], rhs, start=True, stop=True).then_inc(counts_done, 1)
            pe.wait_ge(xT_copied, 8)

            for i in range(9):
                if i < 8:
                    up(i, i, 0, 0, 0)
                if i == 1:
                    pe.wait_ge(counts_read, 1)
                if i:
                    j = i - 1
                    down(j, j, j // 2, 0, j // 2 % 2, j % 2 == 0, j % 2 == 1)

            def tile_transpose(q, b, ring, loaded):
                pe.wait_ge(tile_loaded[ring], loaded)
                wait(pe, tT_low, q - 1)
                for t in range(2):
                    for k in range(2):
                        last = pe.transpose(ps[:, b, (2 * t + k) * P:(2 * t + k + 1) * P], xl[:, ring, t, k * P:(k + 1) * P], ident[:, :])
                return last.then_inc(tT_done, 1)

            def word(i):
                return pe.value_load(words[0:1, slice(i, i + 1) if isinstance(i, int) else bass.ds(i, 1)], min_val=0, max_val=(1 << 24) - 1)

            def place(v):
                return (v & 0xF00).with_bounds(min_val=0, max_val=3 * EW)

            def tile_up(q, b, v):
                pe.wait_ge(tT_low, q + 1)
                wait(pe, tM_done, q - 1)
                pe.wait_ge(ew_ready, v & 255)
                offs = [place(v), place(v >> 4)]
                for t in range(2):
                    off = offs[t]
                    i = 0
                    for k in range(2):
                        for h, w in ((hH, eH), (hL, eH), (hH, eL)):
                            last = pe.matmul(ps[:, 2 + b, t * D:(t + 1) * D], h[:, b, (2 * t + k) * P:(2 * t + k + 1) * P],
                                             w[:, bass.ds(off + k * D, D)], start=i == 0, stop=i == 5)
                            i += 1
                last.then_inc(tU_done, 1)

            def hidden_transpose(q, b):
                pe.wait_ge(tM_done, q + 1)
                wait(pe, tH_low, q - 1)
                for t in range(2):
                    last = pe.transpose(ps[:, 4 + b, t * P:(t + 1) * P], rh[:, b, t, :], ident[:, :])
                last.then_inc(tHT_done, 1)

            def tile_down(q, b, v):
                offs = [place(v >> 8), place(v >> 12)]
                pe.wait_ge(tH_low, q + 1)
                wait(pe, tY_done, q - 1)
                for t in range(2):
                    off = offs[t]
                    for i, (h, w) in enumerate(((rhH, eH), (rhL, eH), (rhH, eL))):
                        last = pe.matmul(ps[:, 6 + b, t * D:(t + 1) * D], h[:, b, t, :], w[:, bass.ds(off + 2 * D, D)],
                                         start=i == 0, stop=i == 2)
                    last.then_inc(tile_done, 1)

            pe.wait_ge(evac_done, 4 * M_FA)
            tile_transpose(0, 0, 0, 16)
            tile_transpose(1, 1, 1, 16)
            pe.wait_ge(tT_done, 2)
            pe.sem_inc(tile_done, 1)
            tile_up(0, 0, word(0))

            def body(it, first=False, last=False):
                v = word(it * 4 + 1)
                for j in range(4):
                    q = it * 4 + j
                    if not (last and j >= 2):
                        tile_transpose(q + 2, j % 2, (j + 2) % 4, it * 16 + (16 if j < 2 else 32))
                    if not (last and j == 3):
                        tile_up(q + 1, (j + 1) % 2, v)
                    after = word(it * 4 + (j + 2)) if j < 3 else None
                    hidden_transpose(q, j % 2)
                    if not (first and j == 0):
                        tile_down(q - 1, (j + 1) % 2, v)
                    v = after

            body(0, first=True)
            with pe.Fori(1, PAIRS // 4 - 1) as it:
                body(it)
            body(PAIRS // 4 - 1, last=True)
            tile_down(PAIRS - 1, 1, word(PAIRS + 1))

            def dense(u0, m0, r):
                pe.wait_ge(xT_copied, 8 * (r + 1))
                for i in range(17):
                    if i < 8 and i % 2 == 0:
                        pe.wait_ge(xT_low, 8 * r + i + 2)
                    if i < 16:
                        up(8 * u0 + i, i, u0 + i // 8, (u0 + i // 8) % 2, None)
                    if i:
                        j = i - 1
                        down(8 * u0 + j, j, m0 + j // 2, (u0 + j // 8) % 2, j // 2 % 2, j % 2 == 0, j % 2 == 1)

            transposes(1)
            dense(U_FA, M_FA, 1)
            transposes(2)
            dense(U_FB, M_FB, 2)
            transposes(3)
            logits(3, 1, wg1H, wg1L, 16)

            def expert_up(it, local):
                up(it * 16 + (8 * U_L1 + local), local, it * 2 + (U_L1 + local // 8), 1 - local // 8, PLAIN)

            def expert_down(it, local):
                down(it * 16 + (8 * U_L1 + local), local, it * 8 + (M_L1 + local // 2), 1 - local // 8, local // 2 % 2,
                     local % 2 == 0, local % 2 == 1)

            def experts(it, last):
                for local in range(16):
                    if local < 15:
                        expert_up(it, local + 1)
                    elif not last:
                        expert_up(it + 1, 0)
                    expert_down(it, local)

            expert_up(0, 0)
            pe.wait_ge(cw_done, 1)
            with pe.Fori(0, N_L1 // 2 - 1) as it:
                experts(it, False)
            experts(N_L1 // 2 - 1, True)


def constants(np):
    n = 4 * FT
    w = 2 * np.pi * (np.arange(2 * FT) + 0.5) / n
    p = np.arange(P)

    def forward(pos):
        a = np.outer(pos, w)
        return np.concatenate([np.cos(a), -np.sin(a)], 1).reshape(len(pos), 4, FT)

    pos = np.arange(2 * P)
    odd = forward(pos + 1)
    fw = np.concatenate([forward(pos).reshape(2, P, 4, FT), odd.reshape(2, P, 4, FT)]).transpose(1, 0, 2, 3)
    a = np.outer(w, np.arange(D))
    gi = np.concatenate([np.cos(a), -np.sin(a)]).reshape(4, FT, D) * (2.0 / n)
    gfull = np.zeros((P, 4, D))
    gfull[:FT] = gi.transpose(1, 0, 2)
    t, s = np.arange(P)[:, None], np.arange(P)[None, :]
    mask = np.zeros((P, 3 * P))
    mask[:, 0:P] = mask[:, 2 * P:] = np.where(t <= s, 0.0, -1e30)
    tri = np.stack([(t < s) * 1.0, np.ones((P, P))], 1)
    nl = -np.stack([2 * p, 2 * (p + P), 2 * p + 1, 2 * (p + P) + 1], 1)
    f = np.float32
    return {"ident": np.eye(P).astype(f), "fz": forward(p).astype(f), "fw": fw.astype(f), "gi": gfull.astype(f),
            "maskT": mask, "tri": tri, "nl": nl.astype(f), "iot": np.tile(np.arange(E0), (P, 1)).astype(f),
            "tilen": np.tile(np.arange(TILES), (P, 1)).astype(f)}


def kernel(**inputs):
    import ml_dtypes
    import numpy as np
    import concourse.bacc as bacc
    from concourse.bass_utils import run_bass_kernel_spmd as run

    nc = bacc.Bacc("TRN2", target_bir_lowering=False, num_devices=1)
    I = {k: np.asarray(v) for k, v in inputs.items()}

    def chunked(w):
        return w.reshape(2, P, -1).transpose(1, 0, 2)

    def column(v, k):
        return np.concatenate([v, np.zeros(P * k - len(v), v.dtype)]).reshape(k, P).T

    A = constants(np)
    A["maskT"] = A["maskT"].astype(ml_dtypes.bfloat16)
    A["tri"] = A["tri"].astype(ml_dtypes.bfloat16)
    A["x"], A["ctx"] = I["x"], I["ctx_1024"]
    gates = np.concatenate([I["L0_xattn_igate_w"], I["L0_xattn_fgate_w"]], 0).T
    A["gw"] = gates.reshape(6, P, 16).transpose(1, 0, 2)
    A["gbias"] = np.concatenate([np.tile(I["L0_xattn_igate_b"], B), np.tile(I["L0_xattn_fgate_b"], B)]).reshape(P, 1)
    rows = np.stack([I[n] for n in ("L1_xattn_b1b", "L1_xattn_b2b", "L0_xattn_norm_w", "L1_xattn_b_in", "L1_xattn_g_ln",
                                    "L1_xattn_beta_ln", "L1_xattn_bp2")])
    A["bcv"] = np.broadcast_to(rows[None], (P, 7, D))
    A["cols"] = np.concatenate([column(I["L1_xattn_" + n], k) for n, k in
                                (("g1", 2), ("be1", 2), ("g2", 2), ("be2", 2), ("b1a", 4), ("b2a", 4), ("bp1", 3))], 1)
    A["alog"] = np.broadcast_to(I["L1_xattn_a"].reshape(1, 1), (P, 1))
    A["win"] = chunked(I["L1_xattn_W_in"])
    A["pet"] = I["L1_xattn_pe"].T
    A["wp1"] = I["L1_xattn_Wp1"]
    wp2 = I["L1_xattn_Wp2"]
    A["wp2"] = np.concatenate([wp2, np.zeros((64, D), wp2.dtype)]).reshape(3, P, D).transpose(1, 0, 2)
    A["wg0"] = chunked(I["L0_ffn_Wg"])
    A["wg1"] = chunked(np.concatenate([I["L1_ffn_w_router"], I["L1_ffn_w_gating"]], 1))
    sh = np.concatenate([chunked(I["L0_ffn_" + n]).reshape(P, BLK) for n in ("Ws1", "Ws3", "Ws2")], 1)[None]
    A["w0"] = sh
    w13 = np.stack([I["L0_ffn_W1"], I["L0_ffn_W3"]], 2).reshape(E0, 2, P, D).transpose(0, 2, 1, 3).reshape(E0, P, BLK)
    A["wr"] = np.concatenate([w13, I["L0_ffn_W2"]], 2)
    ab = []
    for n in ("1", "2"):
        a = I[f"L1_xattn_W{n}a"].reshape(2, P, 2, D).transpose(2, 1, 0, 3).reshape(2, P, BLK)
        b = I[f"L1_xattn_W{n}b"].reshape(2, 2, P, D).transpose(0, 2, 1, 3).reshape(2, P, BLK)
        ab.append(np.concatenate([a, b], 2))
    A["wab"] = np.concatenate(ab)
    gu = [I["L1_ffn_" + n].reshape(E1, 2, P, 4, D).transpose(0, 3, 2, 1, 4).reshape(N_L1, P, BLK) for n in ("w_gate", "w_up")]
    gu.append(I["L1_ffn_w_down"].reshape(E1, 4, 2, P, D).transpose(0, 1, 3, 2, 4).reshape(N_L1, P, BLK))
    A["w1"] = np.concatenate(gu, 2)
    A = {k: np.ascontiguousarray(v) for k, v in A.items()}
    dram = {k: nc.dram_tensor("in_" + k, v.shape, mybir.dt.from_np(v.dtype), kind="ExternalInput").ap() for k, v in A.items()}
    out = nc.dram_tensor("out_0", (B, SEQ, D), F32, kind="ExternalOutput").ap()
    build(nc, dram, out)
    r = run(nc, [{"in_" + k: v for k, v in A.items()}], core_ids=[0])
    return r.results[0]["out_0"]
```
